# Optimizing a Trainium2 kernel written in Bass

```python
import numpy as np
import jax
import jax.numpy as jnp

def _softmax(x, axis=-1):
    return jax.nn.softmax(x, axis=axis)

def _gelu(x):
    return jax.nn.gelu(x, approximate=True)

def _silu(x):
    return jax.nn.silu(x)

def _sigmoid(x):
    return jax.nn.sigmoid(x)

def _layernorm(x, axis=-1, eps=1e-05):
    m = jnp.mean(x, axis=axis, keepdims=True)
    v = jnp.var(x, axis=axis, keepdims=True)
    return (x - m) / jnp.sqrt(v + eps)

def _scatter_add(tgt, idx, src, axis=0):
    return tgt.at[idx].add(src)

def _segment_sum(src, seg, n):
    return jax.ops.segment_sum(src, seg, n)
kernel_name = 'mk_xattn_seq_d4_seqx_r4_14c2b4'

def setup_inputs(seed: int=0):
    np.random.seed(seed)
    _w = jnp.asarray

    def _rec_inputs():
        import jax
        import jax.numpy as jnp
        _rk = jax.random.key(seed)
        x = 7.22e-05 + 1 * jax.random.normal(jax.random.fold_in(_rk, 1), (8, 256, 512), jnp.float32)
        _lenS = 256 - jax.random.randint(jax.random.fold_in(_rk, 7), (8,), 0, max(1, 256 // 4) + 1, jnp.int32)
        _lenS2 = 256 - jax.random.randint(jax.random.fold_in(_rk, 8), (8,), 0, max(1, 256 // 4) + 1, jnp.int32)
        _ctx_2048P = jax.random.normal(jax.random.fold_in(_rk, 11), (8, 16, 512), jnp.float32)
        _ctx_2048c = jax.random.dirichlet(jax.random.fold_in(_rk, 511), 0.3 * jnp.ones((16,), jnp.float32), (8, 256))
        _ctx_2048t = jnp.einsum('bsk,bkd->bsd', _ctx_2048c, _ctx_2048P)
        _ctx_2048t = _ctx_2048t * jax.lax.rsqrt(jnp.mean(jnp.square(_ctx_2048t)) + 1e-12) * 0.953939
        ctx_2048 = 0.000189249 + 0.0999589 * (_ctx_2048t + 0.3 * jax.random.normal(jax.random.fold_in(_rk, 611), (8, 256, 512), jnp.float32))
        _validS = jnp.arange(256)[None, :] < _lenS[:, None]
        _validS2 = jnp.arange(256)[None, :] < _lenS2[:, None]
        _causal = jnp.tril(jnp.ones((256, 256), dtype=bool))
        mask_BxS2_ik0 = jnp.where(jnp.broadcast_to(_validS2[:, :], (8, 256)), 0, 1).astype(jnp.int32)
        return (x, ctx_2048, mask_BxS2_ik0)
    x, ctx_2048, mask_BxS2_ik0 = _rec_inputs()

    def _L0_xattn_setup():
        import jax, jax.numpy as jnp
        import numpy as np
        E, H, L, B = (512, 32, 256, 4)
        S = E // H
        DM, DD = (32, 64)

        def _ln(x, w, b, eps=1e-05):
            m = x.mean(-1, keepdims=True)
            v = ((x - m) ** 2).mean(-1, keepdims=True)
            return (x - m) / jnp.sqrt(v + eps) * w + b

        def _block(x, state, ln1_w, ln1_b, ln2_w, ln2_b, maa_x, maa_w1, maa_w2, maa_stack, time_decay, td_w1, td_w2, u, Wr, Wk, Wv, Wg, Wo, gn_w, gn_b, ffn_maa_k, ffn_maa_r, Wfk, Wfr, Wfv):
            b, l, e = x.shape
            h = u.shape[0]
            s_ = e // h
            xa = _ln(x, ln1_w, ln1_b)
            sx = jnp.concatenate([state[:, 1:2] - xa[:, :1], xa[:, :-1] - xa[:, 1:]], axis=1)
            xxx = jnp.tanh((xa + sx * maa_x) @ maa_w1).reshape(b, l, 5, DM)
            xxx = jnp.einsum('blfd,fde->blfe', xxx, maa_w2)
            xm = xa[:, :, None] + sx[:, :, None] * (maa_stack + xxx)
            xk, xw, xv, xr, xg = (xm[:, :, j] for j in range(5))
            w = jnp.exp(-jnp.exp(time_decay + jnp.tanh(xw @ td_w1) @ td_w2)).reshape(b, l, h, s_)
            r = (xr @ Wr.T).reshape(b, l, h, s_)
            k = (xk @ Wk.T).reshape(b, l, h, s_)
            v = (xv @ Wv.T).reshape(b, l, h, s_)
            g = jax.nn.silu(xg @ Wg.T)
            s0 = state[:, 2:2 + s_].reshape(b, h, s_, s_)

            def step(s, rkvw):
                r_t, k_t, v_t, w_t = rkvw
                a = k_t[..., :, None] * v_t[..., None, :]
                out = jnp.einsum('bhi,bhij->bhj', r_t, u * a + s)
                s = a + w_t[..., :, None] * s
                return (s, out)
            rkvw = tuple((jnp.moveaxis(t, 1, 0) for t in (r, k, v, w)))
            _, out = jax.lax.scan(step, s0, rkvw)
            out = jnp.moveaxis(out, 0, 1).reshape(b, l, e)
            og = out.reshape(b, l, h, s_)
            m = og.mean(-1, keepdims=True)
            va = ((og - m) ** 2).mean(-1, keepdims=True)
            og = ((og - m) / jnp.sqrt(va + 1e-05)).reshape(b, l, e) * gn_w + gn_b
            x1 = x + og * g @ Wo.T
            xc = _ln(x1, ln2_w, ln2_b)
            sx2 = jnp.concatenate([state[:, 0:1] - xc[:, :1], xc[:, :-1] - xc[:, 1:]], axis=1)
            xk2 = xc + sx2 * ffn_maa_k
            xr2 = xc + sx2 * ffn_maa_r
            rr = jax.nn.sigmoid(xr2 @ Wfr.T)
            kk = jnp.square(jax.nn.relu(xk2 @ Wfk.T))
            return x1 + rr * (kk @ Wfv.T)
        key = jax.random.key(seed)
        ks = jax.random.split(key, 24)
        sc = 0.02
        d = {'x': jax.random.normal(ks[0], (B, L, E), jnp.float32), 'state': jax.random.normal(ks[1], (B, 2 + S, E), jnp.float32) * 0.1, 'ln1_w': jnp.ones((E,), jnp.float32), 'ln1_b': jnp.zeros((E,), jnp.float32), 'ln2_w': jnp.ones((E,), jnp.float32), 'ln2_b': jnp.zeros((E,), jnp.float32), 'maa_x': jax.random.normal(ks[2], (E,), jnp.float32) * 0.1, 'maa_w1': jax.random.normal(ks[3], (E, 5 * DM), jnp.float32) * sc, 'maa_w2': jax.random.normal(ks[4], (5, DM, E), jnp.float32) * sc, 'maa_stack': jax.random.normal(ks[5], (1, 5, E), jnp.float32) * 0.1, 'time_decay': jax.random.normal(ks[6], (E,), jnp.float32) * 0.5, 'td_w1': jax.random.normal(ks[7], (E, DD), jnp.float32) * sc, 'td_w2': jax.random.normal(ks[8], (DD, E), jnp.float32) * sc, 'u': jax.random.normal(ks[9], (H, S, 1), jnp.float32) * 0.1, 'Wr': jax.random.normal(ks[10], (E, E), jnp.float32) * sc, 'Wk': jax.random.normal(ks[11], (E, E), jnp.float32) * sc, 'Wv': jax.random.normal(ks[12], (E, E), jnp.float32) * sc, 'Wg': jax.random.normal(ks[13], (E, E), jnp.float32) * sc, 'Wo': jax.random.normal(ks[14], (E, E), jnp.float32) * sc, 'gn_w': jnp.ones((E,), jnp.float32), 'gn_b': jnp.zeros((E,), jnp.float32), 'ffn_maa_k': jax.random.normal(ks[15], (E,), jnp.float32) * 0.1, 'ffn_maa_r': jax.random.normal(ks[16], (E,), jnp.float32) * 0.1, 'Wfk': jax.random.normal(ks[17], (E, E), jnp.float32) * sc, 'Wfr': jax.random.normal(ks[18], (E, E), jnp.float32) * sc, 'Wfv': jax.random.normal(ks[19], (E, E), jnp.float32) * sc}
        return d
    _L0_xattn_all = _L0_xattn_setup()
    _L0_xattn_in = {k: v for k, v in _L0_xattn_all.items() if k in ('ln1_w', 'ln1_b', 'ln2_w', 'ln2_b', 'maa_x', 'maa_w1', 'maa_w2', 'maa_stack', 'time_decay', 'td_w1', 'td_w2', 'u', 'Wr', 'Wk', 'Wv', 'Wg', 'Wo', 'gn_w', 'gn_b', 'ffn_maa_k', 'ffn_maa_r', 'Wfk', 'Wfr', 'Wfv')}
    del _L0_xattn_all

    def _L1_xattn_setup():
        import jax, jax.numpy as jnp
        import numpy as np
        B, P, K, H, NH = (4, 512, 64, 512, 16)
        DH = H // NH
        EPS = 1e-06

        def rmsnorm(x, w):
            var = jnp.mean(jnp.square(x), axis=-1, keepdims=True)
            return x * jax.lax.rsqrt(var + EPS) * w
        key = jax.random.key(seed)
        ks = jax.random.split(key, 12)
        s = 0.02
        return {'x': jax.random.normal(ks[0], (B, P, H), jnp.float32), 'latents': jax.random.normal(ks[1], (B, K, H), jnp.float32), 'attention_mask': jax.random.randint(ks[2], (B, P), 0, 2, jnp.int32), 'q_w': s * jax.random.normal(ks[3], (H, H), jnp.float32), 'q_b': jnp.zeros((H,), jnp.float32), 'kv_w': s * jax.random.normal(ks[4], (H, 2 * H), jnp.float32), 'kv_b': jnp.zeros((2 * H,), jnp.float32), 'out_w': s * jax.random.normal(ks[5], (H, H), jnp.float32), 'out_b': jnp.zeros((H,), jnp.float32), 'postnorm_w': jnp.ones((H,), jnp.float32), 'mlp_w1': s * jax.random.normal(ks[6], (H, 4 * H), jnp.float32), 'mlp_b1': jnp.zeros((4 * H,), jnp.float32), 'mlp_w2': s * jax.random.normal(ks[7], (4 * H, H), jnp.float32), 'mlp_b2': jnp.zeros((H,), jnp.float32)}
    _L1_xattn_all = _L1_xattn_setup()
    _L1_xattn_in = {k: v for k, v in _L1_xattn_all.items() if k in ('q_w', 'q_b', 'kv_w', 'kv_b', 'out_w', 'out_b', 'postnorm_w', 'mlp_w1', 'mlp_b1', 'mlp_w2', 'mlp_b2')}
    del _L1_xattn_all

    def _L2_xattn_setup():
        import jax, jax.numpy as jnp
        import numpy as np
        B, L, E, H = (4, 128, 512, 32)
        S = E // H
        EXTRA_MAA, EXTRA_DECAY = (32, 64)
        EPS = 1e-05

        def _ln(x, w, b):
            m = jnp.mean(x, axis=-1, keepdims=True)
            v = jnp.mean((x - m) ** 2, axis=-1, keepdims=True)
            return (x - m) * jax.lax.rsqrt(v + EPS) * w + b

        def _token_shift(xn, prev_row):
            first = (prev_row - xn[:, 0])[:, None]
            rest = xn[:, :-1] - xn[:, 1:]
            return jnp.concatenate([first, rest], axis=1)
        key = jax.random.key(seed)
        ks = jax.random.split(key, 24)
        rn = lambda k, shp, s=1.0: jax.random.normal(k, shp, dtype=jnp.float32) * s
        return dict(x=rn(ks[0], (B, L, E)), state=rn(ks[1], (B, 2 + S, E), 0.1), ln1_w=jnp.ones((E,), jnp.float32), ln1_b=jnp.zeros((E,), jnp.float32), ln2_w=jnp.ones((E,), jnp.float32), ln2_b=jnp.zeros((E,), jnp.float32), maa_x=rn(ks[2], (E,), 0.02), maa_w1=rn(ks[3], (E, 5 * EXTRA_MAA), 0.02), maa_w2=rn(ks[4], (5, EXTRA_MAA, E), 0.02), maa_stack=rn(ks[5], (5, E), 0.02), time_decay=rn(ks[6], (E,), 0.5), decay_w1=rn(ks[7], (E, EXTRA_DECAY), 0.02), decay_w2=rn(ks[8], (EXTRA_DECAY, E), 0.02), faaaa=rn(ks[9], (H, S), 0.1), Wr=rn(ks[10], (E, E), 0.02), Wk=rn(ks[11], (E, E), 0.02), Wv=rn(ks[12], (E, E), 0.02), Wg=rn(ks[13], (E, E), 0.02), Wo=rn(ks[14], (E, E), 0.02), gn_w=jnp.ones((E,), jnp.float32), gn_b=jnp.zeros((E,), jnp.float32), ffn_maa_k=rn(ks[15], (E,), 0.02), ffn_maa_r=rn(ks[16], (E,), 0.02), ffn_Wk=rn(ks[17], (E, E), 0.02), ffn_Wr=rn(ks[18], (E, E), 0.02), ffn_Wv=rn(ks[19], (E, E), 0.02), i=0)
    _L2_xattn_all = _L2_xattn_setup()
    _L2_xattn_in = {k: v for k, v in _L2_xattn_all.items() if k in ('ln1_w', 'ln1_b', 'ln2_w', 'ln2_b', 'maa_x', 'maa_w1', 'maa_w2', 'maa_stack', 'time_decay', 'decay_w1', 'decay_w2', 'faaaa', 'Wr', 'Wk', 'Wv', 'Wg', 'Wo', 'gn_w', 'gn_b', 'ffn_maa_k', 'ffn_maa_r', 'ffn_Wk', 'ffn_Wr', 'ffn_Wv')}
    del _L2_xattn_all

    def _L3_xattn_setup():
        import jax, jax.numpy as jnp
        import numpy as np
        H = 512
        B, L, S = (4, 1024, 10)
        key = jax.random.key(seed)
        k1, k2, k3, k4, k5, k6 = jax.random.split(key, 6)
        scale = 1.0 / np.sqrt(H)
        return {'h_english': jax.random.normal(k1, (B, L, H), dtype=jnp.float32), 'h_lojban': jax.random.normal(k2, (B, S, H), dtype=jnp.float32), 'w_q': jax.random.normal(k3, (H, H), dtype=jnp.float32) * scale, 'w_k': jax.random.normal(k4, (H, H), dtype=jnp.float32) * scale, 'w_v': jax.random.normal(k5, (H, H), dtype=jnp.float32) * scale, 'w_o': jax.random.normal(k6, (H, H), dtype=jnp.float32) * scale, 'alpha': jnp.float32(0.1)}
    _L3_xattn_all = _L3_xattn_setup()
    _L3_xattn_in = {k: v for k, v in _L3_xattn_all.items() if k in ('w_q', 'w_k', 'w_v', 'w_o', 'alpha')}
    del _L3_xattn_all
    return {'x': x, 'ctx_2048': ctx_2048, 'mask_BxS2_ik0': mask_BxS2_ik0, 'L0_xattn_ln1_w': _L0_xattn_in['ln1_w'], 'L0_xattn_ln1_b': _L0_xattn_in['ln1_b'], 'L0_xattn_ln2_w': _L0_xattn_in['ln2_w'], 'L0_xattn_ln2_b': _L0_xattn_in['ln2_b'], 'L0_xattn_maa_x': _L0_xattn_in['maa_x'], 'L0_xattn_maa_w1': _L0_xattn_in['maa_w1'], 'L0_xattn_maa_w2': _L0_xattn_in['maa_w2'], 'L0_xattn_maa_stack': _L0_xattn_in['maa_stack'], 'L0_xattn_time_decay': _L0_xattn_in['time_decay'], 'L0_xattn_td_w1': _L0_xattn_in['td_w1'], 'L0_xattn_td_w2': _L0_xattn_in['td_w2'], 'L0_xattn_u': _L0_xattn_in['u'], 'L0_xattn_Wr': _L0_xattn_in['Wr'], 'L0_xattn_Wk': _L0_xattn_in['Wk'], 'L0_xattn_Wv': _L0_xattn_in['Wv'], 'L0_xattn_Wg': _L0_xattn_in['Wg'], 'L0_xattn_Wo': _L0_xattn_in['Wo'], 'L0_xattn_gn_w': _L0_xattn_in['gn_w'], 'L0_xattn_gn_b': _L0_xattn_in['gn_b'], 'L0_xattn_ffn_maa_k': _L0_xattn_in['ffn_maa_k'], 'L0_xattn_ffn_maa_r': _L0_xattn_in['ffn_maa_r'], 'L0_xattn_Wfk': _L0_xattn_in['Wfk'], 'L0_xattn_Wfr': _L0_xattn_in['Wfr'], 'L0_xattn_Wfv': _L0_xattn_in['Wfv'], 'L1_xattn_q_w': _L1_xattn_in['q_w'], 'L1_xattn_q_b': _L1_xattn_in['q_b'], 'L1_xattn_kv_w': _L1_xattn_in['kv_w'], 'L1_xattn_kv_b': _L1_xattn_in['kv_b'], 'L1_xattn_out_w': _L1_xattn_in['out_w'], 'L1_xattn_out_b': _L1_xattn_in['out_b'], 'L1_xattn_postnorm_w': _L1_xattn_in['postnorm_w'], 'L1_xattn_mlp_w1': _L1_xattn_in['mlp_w1'], 'L1_xattn_mlp_b1': _L1_xattn_in['mlp_b1'], 'L1_xattn_mlp_w2': _L1_xattn_in['mlp_w2'], 'L1_xattn_mlp_b2': _L1_xattn_in['mlp_b2'], 'L2_xattn_ln1_w': _L2_xattn_in['ln1_w'], 'L2_xattn_ln1_b': _L2_xattn_in['ln1_b'], 'L2_xattn_ln2_w': _L2_xattn_in['ln2_w'], 'L2_xattn_ln2_b': _L2_xattn_in['ln2_b'], 'L2_xattn_maa_x': _L2_xattn_in['maa_x'], 'L2_xattn_maa_w1': _L2_xattn_in['maa_w1'], 'L2_xattn_maa_w2': _L2_xattn_in['maa_w2'], 'L2_xattn_maa_stack': _L2_xattn_in['maa_stack'], 'L2_xattn_time_decay': _L2_xattn_in['time_decay'], 'L2_xattn_decay_w1': _L2_xattn_in['decay_w1'], 'L2_xattn_decay_w2': _L2_xattn_in['decay_w2'], 'L2_xattn_faaaa': _L2_xattn_in['faaaa'], 'L2_xattn_Wr': _L2_xattn_in['Wr'], 'L2_xattn_Wk': _L2_xattn_in['Wk'], 'L2_xattn_Wv': _L2_xattn_in['Wv'], 'L2_xattn_Wg': _L2_xattn_in['Wg'], 'L2_xattn_Wo': _L2_xattn_in['Wo'], 'L2_xattn_gn_w': _L2_xattn_in['gn_w'], 'L2_xattn_gn_b': _L2_xattn_in['gn_b'], 'L2_xattn_ffn_maa_k': _L2_xattn_in['ffn_maa_k'], 'L2_xattn_ffn_maa_r': _L2_xattn_in['ffn_maa_r'], 'L2_xattn_ffn_Wk': _L2_xattn_in['ffn_Wk'], 'L2_xattn_ffn_Wr': _L2_xattn_in['ffn_Wr'], 'L2_xattn_ffn_Wv': _L2_xattn_in['ffn_Wv'], 'L3_xattn_w_q': _L3_xattn_in['w_q'], 'L3_xattn_w_k': _L3_xattn_in['w_k'], 'L3_xattn_w_v': _L3_xattn_in['w_v'], 'L3_xattn_w_o': _L3_xattn_in['w_o'], 'L3_xattn_alpha': _L3_xattn_in['alpha']}

def reference(x, ctx_2048, mask_BxS2_ik0, L0_xattn_ln1_w, L0_xattn_ln1_b, L0_xattn_ln2_w, L0_xattn_ln2_b, L0_xattn_maa_x, L0_xattn_maa_w1, L0_xattn_maa_w2, L0_xattn_maa_stack, L0_xattn_time_decay, L0_xattn_td_w1, L0_xattn_td_w2, L0_xattn_u, L0_xattn_Wr, L0_xattn_Wk, L0_xattn_Wv, L0_xattn_Wg, L0_xattn_Wo, L0_xattn_gn_w, L0_xattn_gn_b, L0_xattn_ffn_maa_k, L0_xattn_ffn_maa_r, L0_xattn_Wfk, L0_xattn_Wfr, L0_xattn_Wfv, L1_xattn_q_w, L1_xattn_q_b, L1_xattn_kv_w, L1_xattn_kv_b, L1_xattn_out_w, L1_xattn_out_b, L1_xattn_postnorm_w, L1_xattn_mlp_w1, L1_xattn_mlp_b1, L1_xattn_mlp_w2, L1_xattn_mlp_b2, L2_xattn_ln1_w, L2_xattn_ln1_b, L2_xattn_ln2_w, L2_xattn_ln2_b, L2_xattn_maa_x, L2_xattn_maa_w1, L2_xattn_maa_w2, L2_xattn_maa_stack, L2_xattn_time_decay, L2_xattn_decay_w1, L2_xattn_decay_w2, L2_xattn_faaaa, L2_xattn_Wr, L2_xattn_Wk, L2_xattn_Wv, L2_xattn_Wg, L2_xattn_Wo, L2_xattn_gn_w, L2_xattn_gn_b, L2_xattn_ffn_maa_k, L2_xattn_ffn_maa_r, L2_xattn_ffn_Wk, L2_xattn_ffn_Wr, L2_xattn_ffn_Wv, L3_xattn_w_q, L3_xattn_w_k, L3_xattn_w_v, L3_xattn_w_o, L3_xattn_alpha):
    import jax
    import jax.numpy as jnp

    def _L0_xattn_ref(x, state, ln1_w, ln1_b, ln2_w, ln2_b, maa_x, maa_w1, maa_w2, maa_stack, time_decay, td_w1, td_w2, u, Wr, Wk, Wv, Wg, Wo, gn_w, gn_b, ffn_maa_k, ffn_maa_r, Wfk, Wfr, Wfv):
        import jax, jax.numpy as jnp
        import numpy as np
        E, H, L, B = (512, 32, 256, 4)
        S = E // H
        DM, DD = (32, 64)

        def _ln(x, w, b, eps=1e-05):
            m = x.mean(-1, keepdims=True)
            v = ((x - m) ** 2).mean(-1, keepdims=True)
            return (x - m) / jnp.sqrt(v + eps) * w + b

        def _block(x, state, ln1_w, ln1_b, ln2_w, ln2_b, maa_x, maa_w1, maa_w2, maa_stack, time_decay, td_w1, td_w2, u, Wr, Wk, Wv, Wg, Wo, gn_w, gn_b, ffn_maa_k, ffn_maa_r, Wfk, Wfr, Wfv):
            b, l, e = x.shape
            h = u.shape[0]
            s_ = e // h
            xa = _ln(x, ln1_w, ln1_b)
            sx = jnp.concatenate([state[:, 1:2] - xa[:, :1], xa[:, :-1] - xa[:, 1:]], axis=1)
            xxx = jnp.tanh((xa + sx * maa_x) @ maa_w1).reshape(b, l, 5, DM)
            xxx = jnp.einsum('blfd,fde->blfe', xxx, maa_w2)
            xm = xa[:, :, None] + sx[:, :, None] * (maa_stack + xxx)
            xk, xw, xv, xr, xg = (xm[:, :, j] for j in range(5))
            w = jnp.exp(-jnp.exp(time_decay + jnp.tanh(xw @ td_w1) @ td_w2)).reshape(b, l, h, s_)
            r = (xr @ Wr.T).reshape(b, l, h, s_)
            k = (xk @ Wk.T).reshape(b, l, h, s_)
            v = (xv @ Wv.T).reshape(b, l, h, s_)
            g = jax.nn.silu(xg @ Wg.T)
            s0 = state[:, 2:2 + s_].reshape(b, h, s_, s_)

            def step(s, rkvw):
                r_t, k_t, v_t, w_t = rkvw
                a = k_t[..., :, None] * v_t[..., None, :]
                out = jnp.einsum('bhi,bhij->bhj', r_t, u * a + s)
                s = a + w_t[..., :, None] * s
                return (s, out)
            rkvw = tuple((jnp.moveaxis(t, 1, 0) for t in (r, k, v, w)))
            _, out = jax.lax.scan(step, s0, rkvw)
            out = jnp.moveaxis(out, 0, 1).reshape(b, l, e)
            og = out.reshape(b, l, h, s_)
            m = og.mean(-1, keepdims=True)
            va = ((og - m) ** 2).mean(-1, keepdims=True)
            og = ((og - m) / jnp.sqrt(va + 1e-05)).reshape(b, l, e) * gn_w + gn_b
            x1 = x + og * g @ Wo.T
            xc = _ln(x1, ln2_w, ln2_b)
            sx2 = jnp.concatenate([state[:, 0:1] - xc[:, :1], xc[:, :-1] - xc[:, 1:]], axis=1)
            xk2 = xc + sx2 * ffn_maa_k
            xr2 = xc + sx2 * ffn_maa_r
            rr = jax.nn.sigmoid(xr2 @ Wfr.T)
            kk = jnp.square(jax.nn.relu(xk2 @ Wfk.T))
            return x1 + rr * (kk @ Wfv.T)
        return _block(x, state, ln1_w, ln1_b, ln2_w, ln2_b, maa_x, maa_w1, maa_w2, maa_stack, time_decay, td_w1, td_w2, u, Wr, Wk, Wv, Wg, Wo, gn_w, gn_b, ffn_maa_k, ffn_maa_r, Wfk, Wfr, Wfv)

    def _L1_xattn_ref(x, latents, attention_mask, q_w, q_b, kv_w, kv_b, out_w, out_b, postnorm_w, mlp_w1, mlp_b1, mlp_w2, mlp_b2):
        import jax, jax.numpy as jnp
        import numpy as np
        B, P, K, H, NH = (4, 512, 64, 512, 16)
        DH = H // NH
        EPS = 1e-06

        def rmsnorm(x, w):
            var = jnp.mean(jnp.square(x), axis=-1, keepdims=True)
            return x * jax.lax.rsqrt(var + EPS) * w
        b, p, _ = x.shape
        k_len = latents.shape[1]
        residual = latents
        h = jnp.concatenate([x, latents], axis=1)
        q = (latents @ q_w + q_b).reshape(b, k_len, NH, DH)
        kv = (h @ kv_w + kv_b).reshape(b, p + k_len, NH, DH, 2)
        kmat, v = (kv[..., 0], kv[..., 1])
        attn = jnp.einsum('bkhd,bnhd->bhkn', q, kmat) / DH
        full_mask = jnp.concatenate([attention_mask.astype(bool), jnp.ones((b, k_len), bool)], axis=-1)
        attn = jnp.where(full_mask[:, None, None, :], attn, -jnp.inf)
        attn = jax.nn.softmax(attn.astype(jnp.float32), axis=-1).astype(q.dtype)
        attn_out = jnp.einsum('bhkn,bnhd->bkhd', attn, v).reshape(b, k_len, H)
        attn_out = attn_out @ out_w + out_b + residual
        out = rmsnorm(attn_out, postnorm_w)
        out = jax.nn.gelu(out @ mlp_w1 + mlp_b1) @ mlp_w2 + mlp_b2
        return out + residual

    def _L2_xattn_ref(x, state, ln1_w, ln1_b, ln2_w, ln2_b, maa_x, maa_w1, maa_w2, maa_stack, time_decay, decay_w1, decay_w2, faaaa, Wr, Wk, Wv, Wg, Wo, gn_w, gn_b, ffn_maa_k, ffn_maa_r, ffn_Wk, ffn_Wr, ffn_Wv, i):
        import jax, jax.numpy as jnp
        import numpy as np
        B, L, E, H = (4, 128, 512, 32)
        S = E // H
        EXTRA_MAA, EXTRA_DECAY = (32, 64)
        EPS = 1e-05

        def _ln(x, w, b):
            m = jnp.mean(x, axis=-1, keepdims=True)
            v = jnp.mean((x - m) ** 2, axis=-1, keepdims=True)
            return (x - m) * jax.lax.rsqrt(v + EPS) * w + b

        def _token_shift(xn, prev_row):
            first = (prev_row - xn[:, 0])[:, None]
            rest = xn[:, :-1] - xn[:, 1:]
            return jnp.concatenate([first, rest], axis=1)
        b, l = (x.shape[0], x.shape[1])
        i0 = (2 + S) * i + 0
        i1 = (2 + S) * i + 1
        xn = _ln(x, ln1_w, ln1_b)
        sx = _token_shift(xn, state[:, i1])
        xxx = jnp.tanh((xn + sx * maa_x) @ maa_w1).reshape(b, l, 5, 1, EXTRA_MAA)
        xxx = jnp.matmul(xxx, maa_w2).reshape(b, l, 5, E)
        x5 = xn[:, :, None] + sx[:, :, None] * (maa_stack + xxx)
        w = jnp.exp(-jnp.exp(time_decay + jnp.tanh(x5[:, :, 1] @ decay_w1) @ decay_w2))
        w = w.reshape(b, l, H, S)
        r = (x5[:, :, 3] @ Wr.T).reshape(b, l, H, S)
        k = (x5[:, :, 0] @ Wk.T).reshape(b, l, H, S)
        v = (x5[:, :, 2] @ Wv.T).reshape(b, l, H, S)
        g = jax.nn.silu(x5[:, :, 4] @ Wg.T)
        s0 = state[:, (2 + S) * i + 2:(2 + S) * (i + 1)].reshape(b, H, S, S)
        u = faaaa[None, :, :, None]

        def step(s, rkvw):
            r_t, k_t, v_t, w_t = rkvw
            a = k_t[:, :, :, None] * v_t[:, :, None, :]
            out = jnp.einsum('bhk,bhkd->bhd', r_t, u * a + s)
            return (a + w_t[:, :, :, None] * s, out)
        xs = tuple((jnp.moveaxis(t, 1, 0) for t in (r, k, v, w)))
        _, outs = jax.lax.scan(step, s0, xs)
        att = jnp.moveaxis(outs, 0, 1).reshape(b, l, E)
        a4 = att.reshape(b, l, H, S)
        m = jnp.mean(a4, axis=-1, keepdims=True)
        var = jnp.mean((a4 - m) ** 2, axis=-1, keepdims=True)
        att = ((a4 - m) * jax.lax.rsqrt(var + EPS)).reshape(b, l, E) * gn_w + gn_b
        x = x + att * g @ Wo.T
        xn2 = _ln(x, ln2_w, ln2_b)
        sx2 = _token_shift(xn2, state[:, i0])
        xk = xn2 + sx2 * ffn_maa_k
        xr = xn2 + sx2 * ffn_maa_r
        rr = jax.nn.sigmoid(xr @ ffn_Wr.T)
        kk = jnp.square(jax.nn.relu(xk @ ffn_Wk.T))
        x = x + rr * (kk @ ffn_Wv.T)
        return x

    def _L3_xattn_ref(h_english, h_lojban, w_q, w_k, w_v, w_o, alpha):
        import jax, jax.numpy as jnp
        import numpy as np
        H = 512
        B, L, S = (4, 1024, 10)
        h = h_english.shape[-1]
        q = jnp.einsum('blh,oh->blo', h_english, w_q)
        k = jnp.einsum('bsh,oh->bso', h_lojban, w_k)
        v = jnp.einsum('bsh,oh->bso', h_lojban, w_v)
        scores = jnp.einsum('blh,bsh->bls', q, k) / jnp.sqrt(jnp.float32(h))
        probs = jax.nn.softmax(scores, axis=-1)
        context = jnp.einsum('bls,bsh->blh', probs, v)
        delta = jnp.einsum('blh,oh->blo', context, w_o)
        return h_english + alpha * delta
    x = _L0_xattn_ref(x, ctx_2048, L0_xattn_ln1_w, L0_xattn_ln1_b, L0_xattn_ln2_w, L0_xattn_ln2_b, L0_xattn_maa_x, L0_xattn_maa_w1, L0_xattn_maa_w2, L0_xattn_maa_stack, L0_xattn_time_decay, L0_xattn_td_w1, L0_xattn_td_w2, L0_xattn_u, L0_xattn_Wr, L0_xattn_Wk, L0_xattn_Wv, L0_xattn_Wg, L0_xattn_Wo, L0_xattn_gn_w, L0_xattn_gn_b, L0_xattn_ffn_maa_k, L0_xattn_ffn_maa_r, L0_xattn_Wfk, L0_xattn_Wfr, L0_xattn_Wfv)
    x = _L1_xattn_ref(ctx_2048, x, mask_BxS2_ik0, L1_xattn_q_w, L1_xattn_q_b, L1_xattn_kv_w, L1_xattn_kv_b, L1_xattn_out_w, L1_xattn_out_b, L1_xattn_postnorm_w, L1_xattn_mlp_w1, L1_xattn_mlp_b1, L1_xattn_mlp_w2, L1_xattn_mlp_b2)
    x = _L2_xattn_ref(x, ctx_2048, L2_xattn_ln1_w, L2_xattn_ln1_b, L2_xattn_ln2_w, L2_xattn_ln2_b, L2_xattn_maa_x, L2_xattn_maa_w1, L2_xattn_maa_w2, L2_xattn_maa_stack, L2_xattn_time_decay, L2_xattn_decay_w1, L2_xattn_decay_w2, L2_xattn_faaaa, L2_xattn_Wr, L2_xattn_Wk, L2_xattn_Wv, L2_xattn_Wg, L2_xattn_Wo, L2_xattn_gn_w, L2_xattn_gn_b, L2_xattn_ffn_maa_k, L2_xattn_ffn_maa_r, L2_xattn_ffn_Wk, L2_xattn_ffn_Wr, L2_xattn_ffn_Wv, 0)
    x = _L3_xattn_ref(x, ctx_2048, L3_xattn_w_q, L3_xattn_w_k, L3_xattn_w_v, L3_xattn_w_o, L3_xattn_alpha)
    return x

_drawn_inputs = setup_inputs


def setup_inputs(seed=0):
    import zlib

    import numpy as np

    out = dict(_drawn_inputs(seed))
    spreads = {'L0_xattn_ln1_w': (1.0, 0.2),
     'L0_xattn_ln1_b': (0.0, 0.1),
     'L0_xattn_ln2_w': (1.0, 0.6),
     'L0_xattn_ln2_b': (0.0, 0.8),
     'L0_xattn_gn_w': (1.0, 0.6),
     'L0_xattn_gn_b': (0.0, 0.653),
     'L1_xattn_q_b': (0.0, 0.8),
     'L1_xattn_kv_b': (0.0, 0.757),
     'L1_xattn_out_b': (0.0, 0.346),
     'L1_xattn_postnorm_w': (1.0, 0.2),
     'L1_xattn_mlp_b1': (0.0, 0.1),
     'L1_xattn_mlp_b2': (0.0, 0.1),
     'L2_xattn_ln1_w': (1.0, 0.2),
     'L2_xattn_ln1_b': (0.0, 0.294),
     'L2_xattn_ln2_w': (1.0, 0.6),
     'L2_xattn_ln2_b': (0.0, 0.8),
     'L2_xattn_gn_w': (1.0, 0.6),
     'L2_xattn_gn_b': (0.0, 0.714)}
    factors = {'ctx_2048': 3.874,
     'L0_xattn_maa_x': 8.0,
     'L0_xattn_maa_w1': 2.77,
     'L0_xattn_maa_w2': 2.805,
     'L0_xattn_td_w1': 8.0,
     'L0_xattn_td_w2': 8.0,
     'L0_xattn_u': 2.881,
     'L0_xattn_ffn_maa_k': 5.554,
     'L0_xattn_ffn_maa_r': 8.0,
     'L0_xattn_Wfr': 3.893,
     'L1_xattn_q_w': 8.0,
     'L1_xattn_kv_w': 8.0,
     'L1_xattn_out_w': 5.243,
     'L2_xattn_maa_x': 8.0,
     'L2_xattn_maa_w1': 3.052,
     'L2_xattn_maa_w2': 3.078,
     'L2_xattn_maa_stack': 6.696,
     'L2_xattn_decay_w1': 8.0,
     'L2_xattn_decay_w2': 8.0,
     'L2_xattn_faaaa': 3.115,
     'L2_xattn_ffn_maa_k': 8.0,
     'L2_xattn_ffn_maa_r': 8.0,
     'L2_xattn_ffn_Wr': 4.23,
     'L3_xattn_w_q': 8.0,
     'L3_xattn_w_k': 8.0,
     'L3_xattn_w_v': 8.0,
     'L3_xattn_w_o': 8.0}
    for name, (base, spread) in spreads.items():
        noise = np.random.default_rng([zlib.crc32(name.encode()), seed]).standard_normal(out[name].shape)
        drawn = base * np.exp(spread * noise) if base else spread * noise
        out[name] = jnp.asarray(drawn.astype(out[name].dtype))
    for name, factor in factors.items():
        out[name] = (out[name] * factor).astype(out[name].dtype)
    return out
```

```python
import numpy as np
from contextlib import ExitStack

import concourse.bass as bass
from concourse import mybir

F32 = mybir.dt.float32
F32R = mybir.dt.float32r
I32 = mybir.dt.int32
ALU = mybir.AluOpType
ACT = mybir.ActivationFunctionType
AX = mybir.AxisListType.X

P = 128
E = 512
NC = E // P
B = 8
T = 256
TT = T // P
S = 16
HT = P // S
DM = 32
DD = 64
NG = 16
EPS = 1e-5

(LN1W, LN1B, MAAX, MAAK, MAAW, MAAV, MAAR, MAAG, DECAY, BONUS,
 GNW, GNB, LN2W, LN2B, FMK, FMR) = range(16)
NPAR = 16

(C_OT, C_GNT, C_WO, C_XT, C_FR, C_FK, C_FV,
 A_XT, A_W1, A_XK, A_XW, A_PK, A_XV, A_PD1, A_XR, A_PD2, A_PV, A_XG, A_PR, A_PG, A_CF, A_VT) = range(22)
NJ_C, NJ_A = 7, 15


def up_to(n, per, k):
    return n * per + k


def wait(eng, sem, value):
    if not (isinstance(value, int) and value <= 0):
        eng.wait_ge(sem, value)


def wait_apart(eng, s, sem, value):
    eng.wait_ge(sem, value)
    eng.nop().then_inc(s["parted"], 1)


class Step:

    def __init__(self, layer, t, u=None):
        tt = t if u is None else u * 2 + t
        self.t = tt
        self.parity = t % 2
        self.wkv = 0 <= t < B
        self.ahead = t + 1 < B
        self.behind = 1 <= t
        self.nb = tt + B * layer
        self.na = tt + (1 + B * layer)
        self.nc = tt + (B * layer - 1)
        behind = (tt - 1) if t >= 1 else 0
        self.steps = tt + (1 + (B + 2) * layer)
        ahead = tt + 1 if t < B else B
        self.jobs = ahead * NJ_A + behind * NJ_C + B * layer * (NJ_A + NJ_C)
        self.fills = [ahead * 7 + behind * 4 + B * layer * 11, ahead * 8 + behind * 3 + B * layer * 11]

    def job(self, j):
        return self.jobs + (j + 1 if self.behind else j + 1 - NJ_C)

    def fills_before(self, j):
        first = 0 if self.behind else NJ_C
        return self.fills[j % 2] + sum(1 for i in range(first, j) if i % 2 == j % 2)


def pipeline(eng, layer, body):
    body(Step(layer, -1))
    body(Step(layer, 0))
    with eng.Fori(0, (B - 2) // 2) as u:
        body(Step(layer, 1, u))
        body(Step(layer, 2, u))
    body(Step(layer, B - 1))
    body(Step(layer, B))


def rwkv_layer(nc, layer, k, sems, w, x_src, x_dst):
    ident, stT, s0, selr, red, head8 = k["ident"], k["stT"], k["s0"], k["selr"], k["red"], k["head8"]
    tag = f"r{layer}_"
    with ExitStack() as ctx:
        def sb(name, shape, dt=F32):
            return ctx.enter_context(nc.sbuf_tensor(tag + name, shape, dt))

        wr, wk, wv, wg, wo = (sb(n, [P, NC, E]) for n in ("wr", "wk", "wv", "wg", "wo"))
        wfk, wfr, wfv = (sb(n, [P, NC, E]) for n in ("wfk", "wfr", "wfv"))
        w1 = sb("w1", [P, NC, 5 * DM])
        w2 = sb("w2", [P, E])
        w2g = sb("w2g", [P, E])
        td1 = sb("td1", [P, NC, DD])
        td2 = sb("td2", [P, E])
        par = sb("par", [P, NPAR, NC])

        decay = [sb(f"decay{i}", [P, NC, T + 1]) for i in range(2)]
        kT = [sb(f"kT{i}", [P, NC, T]) for i in range(2)]
        rT = [sb(f"rT{i}", [P, NC, T]) for i in range(2)]
        vhi = [sb(f"vhi{i}", [P, NC, T], F32R) for i in range(2)]
        vlo = [sb(f"vlo{i}", [P, NC, T], F32R) for i in range(2)]
        gT = [sb(f"gT{i}", [P, NC, T]) for i in range(2)]
        uv = [sb(f"uv{i}", [P, TT, E]) for i in range(2)]
        oP = [sb(f"oP{i}", [P, NC, T]) for i in range(2)]
        wrep = sb("wrep", [P, 4, T])
        drive = [sb(f"drive{i}", [P, 4, T]) for i in range(2)]
        state = [sb(f"state{i}", [P, 4, T]) for i in range(2)]
        t0, t1, t2, t3, t4 = (sb(f"t{i}", [P, 1024]) for i in range(5))
        ext = sb("ext", [P, NC, T + 1])
        th = sb("th", [P, 4, T])
        thg = sb("thg", [P, T])
        td = sb("td", [P, T])
        small = sb("small", [P, 512])
        stats = small[:, 0:12].rearrange("p (a b) -> p a b", a=2)
        mv = small[:, 16:20].rearrange("p (a b) -> p a b", a=2)
        vare = small[:, 24:26]
        rstd = small[:, 28:30]
        hsum = small[:, 64:128]
        hvar = small[:, 128:192]
        hve = small[:, 192:256]
        hrs = small[:, 256:320]
        coef = small[:, 320:384]
        nhalf = k["nhalf"]

        def cm(x):
            return x[:, :].rearrange("p (c t) -> p c t", c=NC)

        def tm(x):
            return x[:, :].rearrange("p (s e) -> p s e", s=TT)

        D, V, O = k["D"], k["V"], k["O"]
        dcm = [d[:, :, :].rearrange("p b (c t) -> p (b c) t", t=T) for d in D]

        s = sems
        xs = x_src.rearrange("b (s p) e -> b p s e", p=P)
        xd = x_dst.rearrange("b (s p) e -> b p s e", p=P)

        def step_end(eng, st):
            eng.nop().then_inc(s["step_done"], 1)
            wait_apart(eng, s, s["step_done"], up_to(st.steps, 5, 5))

        def job_of(st, j):
            return D[j % 2], dcm[j % 2]

        with nc.Block() as block:

            @block.sync
            def _(sp):
                for dst, name in ((w1, "w1"), (td1, "td1"), (wk, "Wk"), (wv, "Wv"), (wr, "Wr"), (wg, "Wg"),
                                  (wo, "Wo"), (wfr, "Wfr"), (wfk, "Wfk"), (wfv, "Wfv")):
                    sp.dma_start(dst[:, :, :], w[name].rearrange("(c p) n -> p c n", p=P)).then_inc(s["weights"], 16)
                sp.dma_start(w2[:, :], w["w2"][0:P, :]).then_inc(s["weights"], 16)
                sp.wait_ge(s["zeros"], up_to(layer, 7, 2))
                sp.dma_start(w2g[0:DM, :], w["w2"][P:P + DM, :]).then_inc(s["weights"], 16)
                sp.dma_start(td2[0:DD, :], w["td2"]).then_inc(s["weights"], 16)
                sp.dma_start(par[:, :, :], w["par"]).then_inc(s["weights"], 16)
                sp.wait_ge(s["weights"], up_to(layer, 16 * 14, 16 * 14))

                def body(st):
                    if st.behind:
                        sp.dma_start(tm(t1), xs[st.t - 1]).then_inc(s["x_residual"], 16)
                        wait_apart(sp, s, s["x_new"], up_to(st.nc, 1, 1))
                        sp.dma_start(xd[st.t - 1], tm(t1)).then_inc(s["x_stored"], 16)
                    if st.ahead:
                        if st.behind:
                            wait_apart(sp, s, s["dense"], st.job(C_FV))
                        sp.dma_start(tm(t0), xs[st.t + 1]).then_inc(s["x_loaded"], 16)
                        sp.wait_ge(s["x_loaded"], up_to(st.na, 16, 16))
                    if st.behind:
                        sp.wait_ge(s["x_stored"], up_to(st.nc, 16, 16))
                    step_end(sp, st)

                pipeline(sp, layer, body)

            @block.tensor
            def _(pe):
                pe.wait_ge(s["weights"], up_to(layer, 16 * 14, 16 * 14))
                pe.wait_ge(s["zeros"], up_to(layer, 7, 7))

                def free(st, j):
                    wait(pe, s[f"free{j % 2}"], st.fills_before(j))
                    return job_of(st, j)

                def transposes_cm(dst, src):
                    for c in range(NC):
                        for tt in range(TT):
                            m = pe.transpose(dst[:, c, tt * P:(tt + 1) * P], src[:, tt, c * P:(c + 1) * P], ident[:, :])
                    return m

                def transposes_tm(dst, src):
                    for tt in range(TT):
                        for c in range(NC):
                            m = pe.transpose(dst[:, tt, c * P:(c + 1) * P], src[:, c, tt * P:(tt + 1) * P], ident[:, :])
                    return m

                def product_cm(dst, wt, x):
                    for o in range(NC):
                        for c in range(NC):
                            m = pe.matmul(dst[:, o, :], wt[:, c, o * P:(o + 1) * P], x[:, c, :],
                                          start=(c == 0), stop=(c == NC - 1))
                    return m

                def product_tm(dst, wt, x):
                    for tt in range(TT):
                        for c in range(NC):
                            m = pe.matmul(dst[:, tt, :], x[:, c, tt * P:(tt + 1) * P], wt[:, c, :],
                                          start=(c == 0), stop=(c == NC - 1))
                    return m

                def dense(st, j):
                    dt_, dc = free(st, j)
                    q = st.parity
                    if j == C_OT:
                        m = transposes_tm(dt_, oP[1 - q])
                    elif j == C_GNT:
                        pe.wait_ge(s["gn_scaled"], up_to(st.nc, 1, 1))
                        m = transposes_cm(dc, tm(t3))
                    elif j == C_WO:
                        pe.wait_ge(s["gated"], up_to(st.nc, 1, 1))
                        m = product_tm(dt_, wo, cm(t4))
                    elif j == C_XT:
                        pe.wait_ge(s["normed2"], up_to(st.nc, 2, 2))
                        m = transposes_cm(dc, tm(t3))
                    elif j == C_FR:
                        pe.wait_ge(s["mix2"], up_to(st.nc, 8, 4))
                        m = product_tm(dt_, wfr, cm(t0))
                    elif j == C_FK:
                        pe.wait_ge(s["mix2"], up_to(st.nc, 8, 8))
                        m = product_cm(dc, wfk, cm(t4))
                    elif j == C_FV:
                        pe.wait_ge(s["kk"], up_to(st.nc, 1, 1))
                        m = product_tm(dt_, wfv, cm(t0))
                    elif j == A_XT:
                        pe.wait_ge(s["normed1"], up_to(st.na, 2, 2))
                        m = transposes_cm(dc, tm(t3))
                    elif j == A_W1:
                        pe.wait_ge(s["mix0"], up_to(st.na, 4, 4))
                        for c in range(NC):
                            pe.matmul(dt_[:, 0, 0:T], w1[:, c, 0:P], cm(t4)[:, c, :], start=(c == 0), stop=(c == NC - 1))
                        for c in range(NC):
                            m = pe.matmul(dt_[0:DM, 0, T:2 * T], w1[:, c, P:P + DM], cm(t4)[:, c, :],
                                          start=(c == 0), stop=(c == NC - 1))
                    elif j in (A_XK, A_XW, A_XV, A_XR, A_XG):
                        f = (A_XK, A_XW, A_XV, A_XR, A_XG).index(j)
                        pe.wait_ge(s["tanh1"], up_to(st.na, 5, 5))
                        for o in range(NC):
                            lhs = w2 if f < 4 else w2g
                            m = pe.matmul(dc[:, o, :], lhs[:, o * P:(o + 1) * P], th[:, f, :] if f < 4 else thg[:, :],
                                          start=True, stop=True)
                    elif j in (A_PK, A_PV, A_PR, A_PG):
                        f = {A_PK: 0, A_PV: 2, A_PR: 3, A_PG: 4}[j]
                        pe.wait_ge(s["mixed"], up_to(st.na, 5, f + 1))
                        m = product_cm(dc, (wk, None, wv, wr, wg)[f], cm((t3, t4)[f % 2]))
                    elif j == A_PD1:
                        pe.wait_ge(s["mixed"], up_to(st.na, 5, 2))
                        for c in range(NC):
                            m = pe.matmul(dt_[0:DD, 0, 0:T], td1[:, c, :], cm(t4)[:, c, :], start=(c == 0), stop=(c == NC - 1))
                    elif j == A_PD2:
                        pe.wait_ge(s["tanh_d"], up_to(st.na, 1, 1))
                        for o in range(NC):
                            m = pe.matmul(dc[:, o, :], td2[:, o * P:(o + 1) * P], td[:, :], start=True, stop=True)
                    elif j == A_CF:
                        pe.wait_ge(s["ruk"], up_to(st.na, 4, 4))
                        for tt in range(TT):
                            for c in range(NC):
                                m = pe.matmul(dt_[:, 0, (tt * NC + c) * HT:(tt * NC + c + 1) * HT],
                                              cm(t2)[:, c, tt * P:(tt + 1) * P], head8[:, :], start=True, stop=True)
                    elif j == A_VT:
                        pe.wait_ge(s["v"], up_to(st.na, 1, 1))
                        m = transposes_tm(dt_, cm(t1))
                    m.then_inc(s["dense"], 1)

                def spread_v(st, g):
                    c, jg = g // 4, g % 4
                    for half in range(2):
                        n = 2 * g + half
                        if n >= 2:
                            pe.wait_ge(s["kv"], up_to(st.nb, 2 * NG, n - 1))
                        for i in range(2):
                            j = 4 * (2 * half + i) + jg
                            for part in (vhi, vlo):
                                m = pe.matmul(V[half][:, i * T:(i + 1) * T], selr[:, j, :], part[st.parity][:, c, :],
                                              start=(part is vhi), stop=(part is vlo))
                        m.then_inc(s["spread"], 1)

                def reduce_heads(st, g):
                    c, jg = g // 4, g % 4
                    if jg == 0 and c >= 2:
                        pe.wait_ge(s["o_read"], up_to(st.nb, NC, c - 1))
                    pe.wait_ge(s["rs"] if g not in ON_POOL else s["rs_pool"],
                               rs_value(st, g))
                    for q in range(4):
                        m = pe.matmul(O[c % 2][32 * q:32 * q + 32, 0:T], red[:, jg, :], state[g % 2][:, q, :],
                                      start=(jg == 0), stop=(jg == 3))
                    m.then_inc(s["reduced"], 1)

                def body(st):
                    if st.wkv:
                        spread_v(st, 0)
                    for g in range(NG):
                        if st.wkv and g >= 1:
                            spread_v(st, g)
                            reduce_heads(st, g - 1)
                        for j in SLOTS[g]:
                            if st.behind if j < NJ_C else st.ahead:
                                dense(st, j)
                    if st.wkv:
                        reduce_heads(st, NG - 1)
                        pe.wait_ge(s["reduced"], up_to(st.nb, NG, NG))
                    pe.wait_ge(s["dense"], st.job(A_VT if st.ahead else C_FV))
                    step_end(pe, st)

                pipeline(pe, layer, body)

            @block.scalar
            def _(act):
                act.wait_ge(s["weights"], up_to(layer, 16 * 14, 16 * 14))
                act.wait_ge(s["zeros"], up_to(layer, 7, 7))

                def dense(st, j):
                    dt_, dc = job_of(st, j)
                    q = st.parity

                    def made():
                        act.wait_ge(s["dense"], st.job(j))

                    fr = s[f"free{j % 2}"]
                    if j == C_OT:
                        act.wait_ge(s["centred"], up_to(st.nc, 1, 1))
                        act.activation(t2[:, :], t3[:, :], ACT.Square).then_inc(s["squared"], 1)
                    elif j == C_GNT:
                        made()
                        for c in range(NC):
                            m = act.activation(cm(t4)[:, c, :], dc[:, c, :], ACT.Identity,
                                               bias=par[:, GNB, c:c + 1], scale=par[:, GNW, c:c + 1])
                        m.then_inc(fr, 1)
                    elif j in (C_XT, A_XT):
                        lw, lb, row, n = (LN2W, LN2B, 0, st.nc) if j == C_XT else (LN1W, LN1B, 1, st.na)
                        batch = st.t - 1 if j == C_XT else st.t + 1
                        made()
                        act.activation(ext[:, :, 0:1], stT[:, bass.ds(batch, 1), row, :].rearrange("p a c -> p c a"),
                                       ACT.Copy)
                        for c in range(NC):
                            m = act.activation(ext[:, c, 1:T + 1], dc[:, c, :], ACT.Identity,
                                               bias=par[:, lb, c:c + 1], scale=par[:, lw, c:c + 1])
                        m.then_inc(fr, 1)
                    elif j == C_FR:
                        made()
                        act.activation(tm(t3), dt_[:, :, :], ACT.Tanh, scale=0.5).then_inc(fr, 1)
                    elif j == C_FK:
                        made()
                        act.activation(cm(t2), dc, ACT.Relu).then_inc(fr, 1)
                        act.wait_ge(fr, st.fills_before(j) + 1)
                        act.activation(t0[:, :], t2[:, :], ACT.Square).then_inc(s["kk"], 1)
                    elif j == A_W1:
                        made()
                        for f in range(4):
                            act.activation(th[f * DM:(f + 1) * DM, f, :], dt_[f * DM:(f + 1) * DM, 0, 0:T],
                                           ACT.Tanh).then_inc(s["tanh1"], 1)
                        act.activation(thg[0:DM, :], dt_[0:DM, 0, T:2 * T], ACT.Tanh).then_inc(s["tanh1"], 1)
                        act.wait_ge(s["tanh1"], up_to(st.na, 5, 5))
                        act.nop().then_inc(fr, 1)
                    elif j == A_PK:
                        made()
                        act.activation(kT[1 - q][:, :, :], dc, ACT.Copy).then_inc(fr, 1)
                    elif j == A_PR:
                        made()
                        act.activation(rT[1 - q][:, :, :], dc, ACT.Copy).then_inc(fr, 1)
                    elif j == A_PD1:
                        made()
                        act.activation(td[0:DD, :], dt_[0:DD, 0, 0:T], ACT.Tanh).then_inc(s["tanh_d"], 1)
                        act.wait_ge(s["tanh_d"], up_to(st.na, 1, 1))
                        act.nop().then_inc(fr, 1)
                    elif j == A_PD2:
                        made()
                        for c in range(NC):
                            m = act.activation(cm(t0)[:, c, :], dc[:, c, :], ACT.Exp, bias=par[:, DECAY, c:c + 1])
                        m.then_inc(fr, 1)
                        act.wait_ge(fr, st.fills_before(j) + 1)
                        act.activation(decay[1 - q][:, :, 1:T + 1], cm(t0), ACT.Exp, scale=-1.0).then_inc(s["decay"], 1)
                    elif j == A_PV:
                        made()
                        if st.behind:
                            act.wait_ge(s["x_stored"], up_to(st.nc, 16, 16))
                        act.activation(t1[:, :], D[j % 2][:, :, :].rearrange("p b n -> p (b n)"), ACT.Copy).then_inc(s["v"], 1)
                        act.wait_ge(s["v"], up_to(st.na, 1, 1))
                        act.nop().then_inc(fr, 1)
                        act.activation(vhi[1 - q][:, :, :], cm(t1), ACT.Copy).then_inc(s["v_high"], 1)
                    elif j == A_PG:
                        made()
                        act.wait_ge(s["decay"], up_to(st.na, 1, 1))
                        act.activation(cm(t0), dc, ACT.Tanh, scale=0.5).then_inc(s["g_tanh"], 1)

                def wkv(st, g):
                    c, jg = g // 4, g % 4
                    if jg == 0:
                        if c >= 1:
                            act.wait_ge(s["scanned"], up_to(st.nb, NG, 4 * c))
                        act.activation(wrep[:, :, :], decay[st.parity][:, c:c + 1, 0:T].broadcast_to([P, 4, T]),
                                       ACT.Copy).then_inc(s["wrep"], 1)
                    if g >= 2:
                        act.wait_ge(s["scanned"], up_to(st.nb, NG, g - 1))
                    act.activation(drive[g % 2][:, :, 0:1],
                                   s0[:, bass.ds(st.t, 1), c, jg:S:4].rearrange("p a j -> p j a"),
                                   ACT.Copy).then_inc(s["s0_in"], 1)

                def read_o(st, c):
                    act.wait_ge(s["reduced"], up_to(st.nb, NG, 4 * c + 4))
                    act.activation(oP[st.parity][:, c, :], O[c % 2][:, 0:T], ACT.Copy).then_inc(s["o_read"], 1)

                def body(st):
                    for g in range(NG):
                        if st.wkv:
                            wkv(st, g)
                            if g % 4 == 1 and g >= 4:
                                read_o(st, g // 4 - 1)
                        for j in SLOTS[g]:
                            if st.behind if j < NJ_C else st.ahead:
                                dense(st, j)
                    if st.wkv:
                        read_o(st, NC - 1)
                        act.wait_ge(s["o_read"], up_to(st.nb, NC, NC))
                    elif st.ahead:
                        act.wait_ge(s["g_tanh"], up_to(st.na, 1, 1))
                    else:
                        act.wait_ge(s["kk"], up_to(st.nc, 1, 1))
                    step_end(act, st)

                pipeline(act, layer, body)

            @block.gpsimd
            def _(pool):
                pool.memset(w2g[:, :], 0.0).then_inc(s["zeros"], 1)
                pool.memset(td2[:, :], 0.0).then_inc(s["zeros"], 1)
                pool.memset(th[:, :, :], 0.0).then_inc(s["zeros"], 1)
                pool.memset(thg[:, :], 0.0).then_inc(s["zeros"], 1)
                pool.memset(td[:, :], 0.0).then_inc(s["zeros"], 1)
                pool.memset(decay[0][:, :, 0:1], 0.0).then_inc(s["zeros"], 1)
                pool.memset(decay[1][:, :, 0:1], 0.0).then_inc(s["zeros"], 1)

                def inverse_root(ssem, var, tmp, out, n, scale):
                    pool.tensor_scalar(tmp, var, scale, EPS, ALU.mult, ALU.add).then_inc(ssem, 1)
                    pool.wait_ge(ssem, up_to(n, 2, 1))
                    pool.tensor_tensor(out, tmp, nhalf[:, 0:tmp.shape[1]], ALU.pow).then_inc(ssem, 1)

                def dense(st, j):
                    q = st.parity
                    if j == C_OT:
                        wait_apart(pool, s, s["hvar"], up_to(st.nc, 1, 1))
                        inverse_root(s["hrs"], hvar, hve, hrs, st.nc, 1.0 / S)
                        pool.wait_ge(s["hrs"], up_to(st.nc, 2, 2))
                        v = t3[:, :].rearrange("p (h j) -> p h j", j=S)
                        pool.tensor_tensor(v, v, hrs.unsqueeze(2).broadcast_to([P, TT * NC * HT, S]),
                                           ALU.mult).then_inc(s["gn_scaled"], 1)
                    elif j == C_WO:
                        wait_apart(pool, s, s["moments2"], up_to(st.nc, 2, 2))
                        inverse_root(s["rstd2"], mv[:, :, 1], vare, rstd, st.nc, 1.0)
                    elif j == A_XT:
                        wait_apart(pool, s, s["moments1"], up_to(st.na, 2, 2))
                        inverse_root(s["rstd1"], mv[:, :, 1], vare, rstd, st.na, 1.0)
                    elif j in (A_XK, A_XW, A_XV, A_XR, A_XG):
                        f = (A_XK, A_XW, A_XV, A_XR, A_XG).index(j)
                        pool.wait_ge(s["shift_mixed"], up_to(st.na, 20, 4 * f + 4))
                        m = cm((t3, t4)[f % 2])
                        pool.tensor_tensor(m, m, ext[:, :, 1:T + 1], ALU.add).then_inc(s["mixed"], 1)
                    elif j == A_PV:
                        pool.wait_ge(s["v_high"], up_to(st.na, 1, 1))
                        pool.tensor_tensor(vlo[1 - q][:, :, :], cm(t1), vhi[1 - q][:, :, :].bitcast(F32),
                                           ALU.subtract).then_inc(s["v_low"], 1)

                def wkv(st, g):
                    if g in ON_POOL:
                        c = g // 4
                        pool.wait_ge(s["scanned"], up_to(st.nb, NG, g + 1))
                        pool.tensor_tensor(state[g % 2][:, :, :], state[g % 2][:, :, :],
                                           rT[st.parity][:, c:c + 1, :].broadcast_to([P, 4, T]),
                                           ALU.mult).then_inc(s["rs_pool"], 1)

                def body(st):
                    for g in range(NG):
                        if st.wkv:
                            wkv(st, g)
                        for j in SLOTS[g]:
                            if st.behind if j < NJ_C else st.ahead:
                                dense(st, j)
                    if st.wkv:
                        pool.wait_ge(s["rs_pool"], up_to(st.nb, len(ON_POOL), len(ON_POOL)))
                    if st.ahead:
                        pool.wait_ge(s["v_low"], up_to(st.na, 1, 1))
                        pool.wait_ge(s["mixed"], up_to(st.na, 5, 5))
                    if st.behind:
                        pool.wait_ge(s["rstd2"], up_to(st.nc, 2, 2))
                    step_end(pool, st)

                pipeline(pool, layer, body)

            @block.vector
            def _(dve):
                dve.wait_ge(s["weights"], up_to(layer, 16 * 14, 16 * 14))

                def layernorm(x, n, which):
                    for tt in range(TT):
                        dve.bn_stats(stats[:, tt, :], x[:, tt, :]).then_inc(s["stats" + which], 1)
                    for tt in range(TT):
                        wait_apart(dve, s, s["stats" + which], up_to(n, 2, tt + 1))
                        dve.bn_aggr(mv[:, tt, :], stats[:, tt, :]).then_inc(s["moments" + which], 1)
                    dve.wait_ge(s["moments" + which], up_to(n, 2, 2))
                    dve.wait_ge(s["rstd" + which], up_to(n, 2, 2))
                    for tt in range(TT):
                        dve.tensor_scalar(tm(t3)[:, tt, :], x[:, tt, :], mv[:, tt, 0:1], rstd[:, tt:tt + 1],
                                          ALU.subtract, ALU.mult).then_inc(s["normed" + which], 1)

                def shift(st, j):
                    dve.wait_ge(s[f"free{j % 2}"], st.fills_before(j) + 1)
                    dve.tensor_tensor(cm(t2), ext[:, :, 0:T], ext[:, :, 1:T + 1], ALU.subtract)\
                       .then_inc(s["shifted2" if j == C_XT else "shifted1"], 1)

                def mix(out, coef_row, sem):
                    for c in range(NC):
                        dve.scalar_tensor_tensor(out=cm(out)[:, c, :], in0=cm(t2)[:, c, :],
                                                 scalar=par[:, coef_row, c:c + 1], in1=ext[:, c, 1:T + 1],
                                                 op0=ALU.mult, op1=ALU.add).then_inc(sem, 1)

                def dense(st, j):
                    dt_, dc = job_of(st, j)
                    q = st.parity

                    def made():
                        dve.wait_ge(s["dense"], st.job(j))

                    fr = s[f"free{j % 2}"]
                    if j == C_OT:
                        made()
                        for tt in range(TT):
                            m = dve.tensor_tensor(
                                tm(t0)[:, tt, :].rearrange("p (c h j) -> p c h j", c=NC, h=HT),
                                dt_[:, tt, :].rearrange("p (c j h) -> p c h j", c=NC, h=HT),
                                uv[1 - q][:, tt, :].rearrange("p (c h j) -> p c h j", c=NC, h=HT), ALU.add)
                        m.then_inc(fr, 1)
                        dve.wait_ge(fr, st.fills_before(j) + 1)
                        o = t0[:, :].rearrange("p (h j) -> p h j", j=S)
                        dve.tensor_reduce(hsum, o, AX, ALU.add).then_inc(s["hsum"], 1)
                        dve.wait_ge(s["hsum"], up_to(st.nc, 1, 1))
                        dve.scalar_tensor_tensor(out=t3[:, :].rearrange("p (h j) -> p h j", j=S),
                                                 in0=hsum.unsqueeze(2).broadcast_to([P, TT * NC * HT, S]),
                                                 scalar=-1.0 / S, in1=o, op0=ALU.mult, op1=ALU.add)\
                           .then_inc(s["centred"], 1)
                        dve.wait_ge(s["squared"], up_to(st.nc, 1, 1))
                        dve.tensor_reduce(hvar, t2[:, :].rearrange("p (h j) -> p h j", j=S), AX, ALU.add)\
                           .then_inc(s["hvar"], 1)
                    elif j == C_GNT:
                        dve.wait_ge(fr, st.fills_before(j) + 1)
                        dve.scalar_tensor_tensor(out=cm(t4), in0=cm(t4), scalar=0.5, in1=gT[1 - q][:, :, :],
                                                 op0=ALU.mult, op1=ALU.mult).then_inc(s["gated"], 1)
                    elif j == C_WO:
                        made()
                        dve.wait_ge(s["x_residual"], up_to(st.nc, 16, 16))
                        dve.tensor_tensor(tm(t1), tm(t1), dt_[:, :, :], ALU.add).then_inc(fr, 1)
                        dve.wait_ge(fr, st.fills_before(j) + 1)
                        layernorm(tm(t1), st.nc, "2")
                    elif j == C_XT:
                        shift(st, j)
                        dve.wait_ge(s["shifted2"], up_to(st.nc, 1, 1))
                        mix(t0, FMR, s["mix2"])
                        mix(t4, FMK, s["mix2"])
                    elif j == C_FV:
                        made()
                        dve.wait_ge(s["free0"], st.fills_before(C_FR) + 1)
                        dve.scalar_tensor_tensor(out=tm(t3), in0=tm(t3), scalar=1.0, in1=dt_[:, :, :],
                                                 op0=ALU.add, op1=ALU.mult).then_inc(fr, 1)
                        dve.wait_ge(fr, st.fills_before(j) + 1)
                        dve.scalar_tensor_tensor(out=t1[:, :], in0=t3[:, :], scalar=0.5, in1=t1[:, :],
                                                 op0=ALU.mult, op1=ALU.add).then_inc(s["x_new"], 1)
                    elif j == A_XT:
                        shift(st, j)
                        dve.wait_ge(s["shifted1"], up_to(st.na, 1, 1))
                        mix(t4, MAAX, s["mix0"])
                    elif j in (A_XK, A_XW, A_XV, A_XR, A_XG):
                        f = (A_XK, A_XW, A_XV, A_XR, A_XG).index(j)
                        made()
                        dve.wait_ge(s["dense"], st.job((A_W1, A_W1, A_PK, A_PD1, A_PV)[f]))
                        for c in range(NC):
                            m = dve.scalar_tensor_tensor(out=cm((t3, t4)[f % 2])[:, c, :], in0=dc[:, c, :],
                                                         scalar=par[:, MAAK + f, c:c + 1], in1=cm(t2)[:, c, :],
                                                         op0=ALU.add, op1=ALU.mult).then_inc(s["shift_mixed"], 1)
                        dve.wait_ge(s["shift_mixed"], up_to(st.na, 20, 4 * f + 4))
                        dve.nop().then_inc(fr, 1)
                    elif j == A_PG:
                        dve.wait_ge(s["g_tanh"], up_to(st.na, 1, 1))
                        dve.scalar_tensor_tensor(out=gT[1 - q][:, :, :], in0=cm(t0), scalar=1.0, in1=dc,
                                                 op0=ALU.add, op1=ALU.mult).then_inc(fr, 1)
                    elif j == A_PR:
                        dve.wait_ge(fr, st.fills_before(j) + 1)
                        dve.wait_ge(s[f"free{A_PK % 2}"], st.fills_before(A_PK) + 1)
                        for c in range(NC):
                            dve.scalar_tensor_tensor(out=cm(t2)[:, c, :], in0=rT[1 - q][:, c, :],
                                                     scalar=par[:, BONUS, c:c + 1], in1=kT[1 - q][:, c, :],
                                                     op0=ALU.mult, op1=ALU.mult).then_inc(s["ruk"], 1)
                    elif j == A_CF:
                        made()
                        dve.tensor_copy(coef, dt_[:, 0, 0:TT * NC * HT]).then_inc(fr, 1)
                    elif j == A_VT:
                        made()
                        dve.wait_ge(s[f"free{A_CF % 2}"], st.fills_before(A_CF) + 1)
                        dve.tensor_tensor(uv[1 - q][:, :, :].rearrange("p s (h j) -> p (s h) j", j=S),
                                          dt_[:, :, :].rearrange("p s (h j) -> p (s h) j", j=S),
                                          coef.unsqueeze(2).broadcast_to([P, TT * NC * HT, S]), ALU.mult).then_inc(fr, 1)

                def wkv(st, g):
                    c = g // 4
                    k_ = kT[st.parity][:, c:c + 1, 0:T - 1].broadcast_to([P, 2, T - 1])
                    for half in range(2):
                        dve.wait_ge(s["spread"], up_to(st.nb, 2 * NG, 2 * g + half + 1))
                        dve.tensor_tensor(drive[g % 2][:, 2 * half:2 * half + 2, 1:T],
                                          V[half][:, :].rearrange("p (i t) -> p i t", i=2)[:, :, 0:T - 1], k_,
                                          ALU.mult).then_inc(s["kv"], 1)
                    dve.wait_ge(s["kv"], up_to(st.nb, 2 * NG, 2 * g + 2))
                    dve.wait_ge(s["s0_in"], up_to(st.nb, NG, g + 1))
                    dve.wait_ge(s["wrep"], up_to(st.nb, NC, c + 1))
                    if g >= 2:
                        dve.wait_ge(s["reduced"], up_to(st.nb, NG, g - 1))
                    dve.tensor_tensor_scan(state[g % 2][:, :, :].rearrange("p j t -> p (j t)"),
                                           wrep[:, :, :].rearrange("p j t -> p (j t)"),
                                           drive[g % 2][:, :, :].rearrange("p j t -> p (j t)"),
                                           0.0, ALU.mult, ALU.add).then_inc(s["scanned"], 1)
                    if g not in ON_POOL:
                        dve.wait_ge(s["scanned"], up_to(st.nb, NG, g + 1))
                        dve.tensor_tensor(state[g % 2][:, :, :], state[g % 2][:, :, :],
                                          rT[st.parity][:, c:c + 1, :].broadcast_to([P, 4, T]),
                                          ALU.mult).then_inc(s["rs"], 1)

                def body(st):
                    for g in range(NG):
                        if st.wkv:
                            wkv(st, g)
                        if st.ahead and A_XT in SLOTS[g]:
                            dve.wait_ge(s["x_loaded"], up_to(st.na, 16, 16))
                            if st.behind:
                                dve.wait_ge(s["x_new"], up_to(st.nc, 1, 1))
                            layernorm(tm(t0), st.na, "1")
                        for j in SLOTS[g]:
                            if st.behind if j < NJ_C else st.ahead:
                                dense(st, j)
                    if st.wkv:
                        dve.wait_ge(s["rs"], rs_value(st, NG - 1))
                    if st.ahead:
                        dve.wait_ge(s[f"free{A_VT % 2}"], st.fills_before(A_VT) + 1)
                    if st.behind:
                        dve.wait_ge(s["x_new"], up_to(st.nc, 1, 1))
                    step_end(dve, st)

                pipeline(dve, layer, body)


SLOTS = [[C_OT], [], [C_GNT], [C_WO], [], [C_XT], [C_FR, C_FK], [C_FV], [A_XT, A_W1],
         [A_XK, A_XW], [A_PK, A_XV], [A_PD1, A_XR], [A_PD2, A_PV], [A_XG, A_PR], [A_PG, A_CF], [A_VT]]
ON_POOL = (1, 3, 5, 7, 9, 11, 13)


def rs_value(st, g):
    if g in ON_POOL:
        return up_to(st.nb, len(ON_POOL), ON_POOL.index(g) + 1)
    mine = [i for i in range(NG) if i not in ON_POOL]
    return up_to(st.nb, len(mine), mine.index(g) + 1)


NH = 16
DH = 32
KEYS = 2 * T
KT = KEYS // P
F = 2048
NF = F // P
RMS_EPS = 1e-6
MASKED = -3e38
QB, KB, VB, PW, B1 = 0, NC, 2 * NC, 3 * NC, 4 * NC
L_CT, L_XT, L_Q, L_K, L_V, L_P, L_RT, L_RB, L_OUT, L_NT, L_H, L_M2 = 0, 1, 2, 3, 5, 7, 23, 24, 25, 26, 27, 31
NJ_L = 32


def latent_layer(nc, k, s, w, ctx_dram, mask, x_src, x_dst):
    ident, nhalf = k["ident"], k["nhalf"]
    with ExitStack() as ctx:
        def sb(name, shape, dt=F32):
            return ctx.enter_context(nc.sbuf_tensor("l_" + name, shape, dt))

        wq, wk, wv, wo = (sb(n, [P, NC, E]) for n in ("wq", "wk", "wv", "wo"))
        w1 = sb("w1", [P, NC, F])
        w2 = sb("w2", [P, NF, E])
        par = sb("par", [P, 4 * NC + NF])
        out_b = sb("out_b", [P, E])
        b2 = sb("b2", [P, E])
        expand = sb("expand", [NH, E])
        ctok = sb("ctok", [P, TT, E])
        xtok = sb("xtok", [P, TT, E])
        maski = sb("maski", [P, T], I32)
        maskb = sb("maskb", [P, KEYS])
        hT = sb("hT", [P, NC, KEYS])
        qz = sb("qz", [P, NC, 4, T])
        kT = sb("kT", [P, NC, KEYS])
        v = sb("v", [P, KT, E])
        probs = [[sb(f"probs{i}{j}", [P, KEYS]) for j in range(TT)] for i in range(2)]
        ring = sb("ring", [P, 8, KT, T])
        small = sb("small", [P, 256])
        top = small[:, 0:TT * NH]
        neg = small[:, 32:32 + TT * NH]
        total = small[:, 64:64 + TT * NH]
        inv = small[:, 96:96 + TT * NH]
        squares = small[:, 128:130]
        meane = small[:, 132:134]
        rstd = small[:, 136:138]
        invT = sb("invT", [NH, T])
        D, V, O = k["D"], k["V"], k["O"]
        dcm = [d[:, :, :].rearrange("p b (c t) -> p (b c) t", t=T) for d in D]
        hidden = ring[:, 0:4, :, :].rearrange("p a c t -> p (a c) t")
        xb = ctok
        aT = hT[:, :, 0:T]
        attended = ring[:, 4, :, :].rearrange("p c t -> p (c t)").rearrange("p (s e) -> p s e", s=TT)
        scratch = ring[:, 5, :, :].rearrange("p c t -> p (c t)").rearrange("p (s e) -> p s e", s=TT)
        xn = ring[:, 6, :, :].rearrange("p c t -> p (c t)").rearrange("p (s e) -> p s e", s=TT)
        xnT = ring[:, 7, :, :]
        cs = ctx_dram.rearrange("b (s p) e -> b p s e", p=P)
        xs = x_src.rearrange("b (s p) e -> b p s e", p=P)
        xd = x_dst.rearrange("b (s p) e -> b p s e", p=P)

        def made_value(n, j):
            return up_to(n, NJ_L, j + 1)

        def fills_before(n, j):
            return up_to(n, NJ_L // 2, j // 2)

        def batch_end(eng, n):
            eng.nop().then_inc(s["l_batch_done"], 1)
            wait_apart(eng, s, s["l_batch_done"], up_to(n, 5, 5))

        with nc.Block() as block:

            @block.sync
            def _(sp):
                for dst, name in ((wq, "wq"), (wk, "wk"), (wv, "wv"), (wo, "wo"), (w1, "w1"), (w2, "w2")):
                    sp.dma_start(dst[:, :, :], w[name].rearrange("(c p) n -> p c n", p=P)).then_inc(s["l_weights"], 16)
                sp.dma_start(par[:, :], w["par"]).then_inc(s["l_weights"], 16)
                sp.dma_start(expand[:, :], w["expand"]).then_inc(s["l_weights"], 16)
                sp.dma_start(out_b[:, :], w["out_b"].partition_broadcast(P)).then_inc(s["l_weights"], 16)
                sp.dma_start(b2[:, :], w["b2"].partition_broadcast(P)).then_inc(s["l_weights"], 16)
                with sp.Fori(0, B) as n:
                    sp.dma_start(ctok[:, :, :], cs[n]).then_inc(s["l_ctx"], 16)
                    sp.dma_start(xtok[:, :, :], xs[n]).then_inc(s["l_x"], 16)
                    sp.dma_start(maski[:, :], mask[n].partition_broadcast(P)).then_inc(s["l_mask"], 16)
                    wait_apart(sp, s, s["l_new"], up_to(n, 1, 1))
                    sp.dma_start(xd[n], xtok[:, :, :]).then_inc(s["l_stored"], 16)
                    sp.wait_ge(s["l_stored"], up_to(n, 16, 16))
                    batch_end(sp, n)

            @block.tensor
            def _(pe):
                pe.wait_ge(s["l_weights"], 16 * 10)
                pe.wait_ge(s["l_zeros"], 2)

                def batch(n):
                    def free(j):
                        if j >= 2:
                            pe.wait_ge(s[f"l_free{j % 2}"], fills_before(n, j))
                        return D[j % 2], dcm[j % 2]

                    def evacuated(j):
                        pe.wait_ge(s[f"l_free{j % 2}"], fills_before(n, j) + 1)

                    def done(m):
                        m.then_inc(s["l_dense"], 1)

                    def transposes_cm(dst, src):
                        for c in range(NC):
                            for tt in range(TT):
                                m = pe.transpose(dst[:, c, tt * P:(tt + 1) * P], src[:, tt, c * P:(c + 1) * P],
                                                 ident[:, :])
                        return m

                    def product_tm(dst, wt, x, n_in):
                        for tt in range(TT):
                            for c in range(n_in):
                                m = pe.matmul(dst[:, tt, :], x[:, c, tt * P:(tt + 1) * P], wt[:, c, :],
                                              start=(c == 0), stop=(c == n_in - 1))
                        return m

                    pe.wait_ge(s["l_ctx"], up_to(n, 16, 16))
                    _, dc = free(L_CT)
                    done(transposes_cm(dc, ctok))
                    pe.wait_ge(s["l_x"], up_to(n, 16, 16))
                    _, dc = free(L_XT)
                    done(transposes_cm(dc, xtok))
                    evacuated(L_XT)
                    _, dc = free(L_Q)
                    for o in range(NC):
                        for c in range(NC):
                            m = pe.matmul(dc[:, o, :], wq[:, c, o * P:(o + 1) * P], hT[:, c, T:KEYS],
                                          start=(c == 0), stop=(c == NC - 1))
                    done(m)
                    for half in range(2):
                        dt_, _ = free(L_K + half)
                        for i in range(2):
                            o = 2 * half + i
                            for c in range(NC):
                                m = pe.matmul(dt_[:, i, :], wk[:, c, o * P:(o + 1) * P], hT[:, c, :],
                                              start=(c == 0), stop=(c == NC - 1))
                        done(m)
                    for half in range(2):
                        dt_, _ = free(L_V + half)
                        for i in range(2):
                            kt = 2 * half + i
                            for c in range(NC):
                                m = pe.matmul(dt_[:, i, :], hT[:, c, kt * P:(kt + 1) * P], wv[:, c, :],
                                              start=(c == 0), stop=(c == NC - 1))
                        done(m)

                    def scores(h):
                        c, hh = h // 4, h % 4
                        if h == 0:
                            evacuated(L_Q)
                            evacuated(L_K)
                            evacuated(L_K + 1)
                        for tt in range(TT):
                            if h >= 1:
                                pe.wait_ge(s["l_masked"], up_to(n, TT * NH, TT * (h - 1) + tt + 1))
                            pe.matmul(V[tt][:, :], qz[:, c, hh, tt * P:(tt + 1) * P], kT[:, c, :],
                                      start=True, stop=True).then_inc(s["l_scores"], 1)

                    def turn(h):
                        pe.wait_ge(s["l_exp"], up_to(n, TT * NH, TT * (h + 1)))
                        _, dc = free(L_P + h)
                        for kt in range(KT):
                            for tt in range(TT):
                                m = pe.transpose(dc[:, kt, tt * P:(tt + 1) * P],
                                                 probs[h % 2][tt][:, kt * P:(kt + 1) * P], ident[:, :])
                        done(m)

                    def values(c):
                        if c == 0:
                            evacuated(L_V)
                            evacuated(L_V + 1)
                        evacuated(L_P + 4 * c + 2)
                        evacuated(L_P + 4 * c + 3)
                        if c >= 2:
                            pe.wait_ge(s["l_o_read"], up_to(n, NC, c - 1))
                        for kt in range(KT):
                            for hh in range(4):
                                h = 4 * c + hh
                                m = pe.matmul(O[c % 2][DH * hh:DH * hh + DH, 0:T], v[:, kt, h * DH:(h + 1) * DH],
                                              ring[:, h % 8, kt, :], start=(kt == 0), stop=(kt == KT - 1))
                        m.then_inc(s["l_values"], 1)

                    for h in range(NH + 2):
                        if h < NH:
                            scores(h)
                        if 1 <= h <= NH:
                            turn(h - 1)
                        if h >= 5 and (h - 5) % 4 == 0:
                            values((h - 5) // 4)

                    dt_, _ = free(L_RT)
                    pe.wait_ge(s["l_inv"], up_to(n, 1, 1))
                    for tt in range(TT):
                        m = pe.transpose(dt_[0:NH, 0, tt * P:(tt + 1) * P], inv[:, tt * NH:(tt + 1) * NH], ident[:, :])
                    done(m)
                    evacuated(L_RT)
                    _, dc = free(L_RB)
                    for c in range(NC):
                        m = pe.matmul(dc[:, c, :], expand[:, c * P:(c + 1) * P], invT[:, :], start=True, stop=True)
                    done(m)
                    dt_, _ = free(L_OUT)
                    pe.wait_ge(s["l_attended"], up_to(n, NC, NC))
                    done(product_tm(dt_, wo, aT, NC))
                    _, dc = free(L_NT)
                    pe.wait_ge(s["l_normed"], up_to(n, 2, 2))
                    done(transposes_cm(dc, xn))
                    evacuated(L_NT)
                    for part in range(4):
                        _, dc = free(L_H + part)
                        for i in range(4):
                            o = 4 * part + i
                            for c in range(NC):
                                m = pe.matmul(dc[:, i, :], w1[:, c, o * P:(o + 1) * P], xnT[:, c, :],
                                              start=(c == 0), stop=(c == NC - 1))
                        done(m)
                    dt_, _ = free(L_M2)
                    evacuated(L_H + 2)
                    evacuated(L_H + 3)
                    done(product_tm(dt_, w2, hidden, NF))

                with pe.Fori(0, B) as n:
                    batch(n)
                    pe.wait_ge(s["l_dense"], made_value(n, L_M2))
                    batch_end(pe, n)

            @block.scalar
            def _(act):
                act.wait_ge(s["l_weights"], 16 * 10)

                def batch(n):
                    def made(j):
                        act.wait_ge(s["l_dense"], made_value(n, j))
                        return D[j % 2], dcm[j % 2]

                    def done(m, j):
                        m.then_inc(s[f"l_free{j % 2}"], 1)

                    _, dc = made(L_CT)
                    done(act.activation(hT[:, :, 0:T], dc, ACT.Copy), L_CT)
                    _, dc = made(L_XT)
                    done(act.activation(hT[:, :, T:KEYS], dc, ACT.Copy), L_XT)
                    for half in range(2):
                        dt_, _ = made(L_K + half)
                        for i in range(2):
                            o = 2 * half + i
                            m = act.activation(kT[:, o, :], dt_[:, i, :], ACT.Identity, bias=par[:, KB + o:KB + o + 1])
                        done(m, L_K + half)
                    for half in range(2):
                        dt_, _ = made(L_V + half)
                        done(act.activation(v[:, 2 * half:2 * half + 2, :], dt_[:, :, :], ACT.Copy), L_V + half)

                    def exps(h):
                        act.wait_ge(s["l_neg"], up_to(n, NH, h + 1))
                        for tt in range(TT):
                            p_ = probs[h % 2][tt]
                            act.activation(p_[:, :], p_[:, :], ACT.Exp, bias=neg[:, TT * h + tt:TT * h + tt + 1],
                                           scale=1.0 / DH, accum_out=total[:, tt * NH + h:tt * NH + h + 1])\
                               .then_inc(s["l_exp"], 1)

                    def evacuate(h):
                        _, dc = made(L_P + h)
                        if h >= 8:
                            act.wait_ge(s["l_values"], up_to(n, NC, h // 4 - 1))
                        done(act.activation(ring[:, h % 8, :, :], dc, ACT.Copy), L_P + h)

                    def read_o(c):
                        act.wait_ge(s["l_values"], up_to(n, NC, c + 1))
                        act.activation(aT[:, c, :], O[c % 2][:, 0:T], ACT.Copy).then_inc(s["l_o_read"], 1)

                    for h in range(NH + 2):
                        if h < NH:
                            exps(h)
                        if 1 <= h <= NH and (h - 1) % 2 == 0:
                            evacuate(h - 1)
                        if h >= 6 and (h - 6) % 4 == 0:
                            read_o((h - 6) // 4)
                    read_o(NC - 1)
                    dt_, _ = made(L_RT)
                    done(act.activation(invT[:, :], dt_[0:NH, 0, 0:T], ACT.Copy), L_RT)
                    act.wait_ge(s["l_scaled"], up_to(n, 1, 1))
                    for c in range(NC):
                        act.activation(aT[:, c, :], aT[:, c, :], ACT.Identity, bias=par[:, VB + c:VB + c + 1])\
                           .then_inc(s["l_attended"], 1)
                    act.wait_ge(s["l_residual"], up_to(n, 1, 1))
                    for tt in range(TT):
                        act.activation(scratch[:, tt, :], attended[:, tt, :], ACT.Square,
                                       accum_out=squares[:, tt:tt + 1]).then_inc(s["l_squares"], 1)
                    _, dc = made(L_NT)
                    for c in range(NC):
                        m = act.activation(xnT[:, c, :], dc[:, c, :], ACT.Copy, scale=par[:, PW + c:PW + c + 1])
                    done(m, L_NT)
                    for part in range(4):
                        _, dc = made(L_H + part)
                        for i in range(4):
                            o = 4 * part + i
                            m = act.activation(hidden[:, o, :], dc[:, i, :], ACT.Gelu_apprx_tanh,
                                               bias=par[:, B1 + o:B1 + o + 1])
                        done(m, L_H + part)

                with act.Fori(0, B) as n:
                    batch(n)
                    act.wait_ge(s[f"l_free{(L_H + 3) % 2}"], fills_before(n, L_H + 3) + 1)
                    batch_end(act, n)

            @block.gpsimd
            def _(pool):
                pool.memset(qz[:, :, :, :], 0.0).then_inc(s["l_zeros"], 1)
                pool.memset(maskb[:, T:KEYS], 0.0).then_inc(s["l_zeros"], 1)
                pool.wait_ge(s["l_weights"], 16 * 10)
                with pool.Fori(0, B) as n:
                    pool.wait_ge(s["l_x"], up_to(n, 16, 16))
                    pool.wait_ge(s["l_dense"], made_value(n, L_XT))
                    for tt in range(TT):
                        pool.tensor_tensor(xb[:, tt, :], xtok[:, tt, :], out_b[:, :], ALU.add)
                        m = pool.tensor_tensor(xtok[:, tt, :], xtok[:, tt, :], b2[:, :], ALU.add)
                    m.then_inc(s["l_biased"], 1)
                    wait_apart(pool, s, s["l_squares"], up_to(n, 2, 2))
                    pool.tensor_scalar(meane, squares, 1.0 / E, RMS_EPS, ALU.mult, ALU.add).then_inc(s["l_rstd"], 1)
                    pool.wait_ge(s["l_rstd"], up_to(n, 2, 1))
                    pool.tensor_tensor(rstd, meane, nhalf[:, 0:2], ALU.pow).then_inc(s["l_rstd"], 1)
                    pool.wait_ge(s["l_rstd"], up_to(n, 2, 2))
                    batch_end(pool, n)

            @block.vector
            def _(dve):
                dve.wait_ge(s["l_weights"], 16 * 10)
                dve.wait_ge(s["l_zeros"], 2)

                def batch(n):
                    def made(j):
                        dve.wait_ge(s["l_dense"], made_value(n, j))
                        return D[j % 2], dcm[j % 2]

                    def done(m, j):
                        m.then_inc(s[f"l_free{j % 2}"], 1)

                    dve.wait_ge(s["l_mask"], up_to(n, 16, 16))
                    dve.tensor_scalar(maskb[:, 0:T], maski[:, :], 0.0, MASKED, ALU.is_equal, ALU.mult)\
                       .then_inc(s["l_bias"], 1)
                    _, dc = made(L_Q)
                    for hh in range(4):
                        r = slice(DH * hh, DH * hh + DH)
                        m = dve.tensor_tensor(qz[r, :, hh, :], dc[r, :, :],
                                              par[r, QB:QB + NC].unsqueeze(2).broadcast_to([DH, NC, T]), ALU.add)
                    done(m, L_Q)
                    dve.wait_ge(s["l_bias"], up_to(n, 1, 1))

                    def mask_and_max(h):
                        if h >= 2:
                            dve.wait_ge(s["l_dense"], made_value(n, L_P + h - 2))
                        for tt in range(TT):
                            wait_apart(dve, s, s["l_scores"], up_to(n, TT * NH, TT * h + tt + 1))
                            dve.tensor_tensor_reduce(probs[h % 2][tt][:, :], V[tt][:, :], maskb[:, :], 1.0, MASKED,
                                                     ALU.add, ALU.max, top[:, TT * h + tt:TT * h + tt + 1])\
                               .then_inc(s["l_masked"], 1)
                        dve.wait_ge(s["l_masked"], up_to(n, TT * NH, TT * h + TT))
                        dve.tensor_scalar(neg[:, TT * h:TT * h + TT], top[:, TT * h:TT * h + TT], -1.0 / DH, None,
                                          ALU.mult).then_inc(s["l_neg"], 1)

                    def evacuate(h):
                        _, dc = made(L_P + h)
                        if h >= 8:
                            dve.wait_ge(s["l_values"], up_to(n, NC, h // 4 - 1))
                        done(dve.tensor_copy(ring[:, h % 8, :, :], dc), L_P + h)

                    for h in range(NH + 2):
                        if h < NH:
                            mask_and_max(h)
                        if 1 <= h <= NH and (h - 1) % 2 == 1:
                            evacuate(h - 1)
                    dve.wait_ge(s["l_exp"], up_to(n, TT * NH, TT * NH))
                    dve.reciprocal(inv, total).then_inc(s["l_inv"], 1)
                    _, dc = made(L_RB)
                    dve.wait_ge(s["l_o_read"], up_to(n, NC, NC))
                    m = dve.tensor_tensor(aT[:, :, :], aT[:, :, :], dc, ALU.mult)
                    done(m, L_RB)
                    dve.wait_ge(s[f"l_free{L_RB % 2}"], fills_before(n, L_RB) + 1)
                    dve.nop().then_inc(s["l_scaled"], 1)
                    dt_, _ = made(L_OUT)
                    dve.wait_ge(s["l_biased"], up_to(n, 1, 1))
                    done(dve.tensor_tensor(attended, xb[:, :, :], dt_[:, :, :], ALU.add), L_OUT)
                    dve.wait_ge(s[f"l_free{L_OUT % 2}"], fills_before(n, L_OUT) + 1)
                    dve.nop().then_inc(s["l_residual"], 1)
                    dve.wait_ge(s["l_rstd"], up_to(n, 2, 2))
                    for tt in range(TT):
                        dve.tensor_scalar(xn[:, tt, :], attended[:, tt, :], rstd[:, tt:tt + 1], None, ALU.mult)\
                           .then_inc(s["l_normed"], 1)
                    dt_, _ = made(L_M2)
                    done(dve.tensor_tensor(xtok[:, :, :], xtok[:, :, :], dt_[:, :, :], ALU.add), L_M2)
                    dve.wait_ge(s[f"l_free{L_M2 % 2}"], fills_before(n, L_M2) + 1)
                    dve.nop().then_inc(s["l_new"], 1)

                with dve.Fori(0, B) as n:
                    batch(n)
                    batch_end(dve, n)


X_CT, X_XT, X_K, X_V, X_S, X_PT, X_O = range(7)


def cross_layer(nc, k, s, w, ctx_dram, x_src, out):
    ident = k["ident"]
    scale = float(E) ** -0.5
    with ExitStack() as ctx:
        def sb(name, shape, dt=F32):
            return ctx.enter_context(nc.sbuf_tensor("x_" + name, shape, dt))

        wq, wk, wv, wo = (sb(n, [P, NC, E]) for n in ("wq", "wk", "wv", "wo"))
        wkq = sb("wkq", [P, NC, E])
        wvo = sb("wvo", [P, NC, E])
        alpha = sb("alpha", [P, 1])
        ctok = sb("ctok", [P, TT, E])
        xtok = sb("xtok", [P, TT, E])
        cT = sb("cT", [P, NC, T])
        xT = sb("xT", [P, NC, T])
        kT = sb("kT", [P, NC, T])
        v = sb("v", [P, TT, E])
        probs = sb("probs", [P, TT, T])
        pT = sb("pT", [P, TT, T])
        y = sb("y", [P, TT, E])
        small = sb("small", [P, 32])
        top, neg, total, inv, gain = (small[:, 4 * i:4 * i + TT] for i in range(5))
        D = k["D"]
        dcm = [d[:, :, :].rearrange("p b (c t) -> p (b c) t", t=T) for d in D]
        cs = ctx_dram.rearrange("b (s p) e -> b p s e", p=P)
        xs = x_src.rearrange("b (s p) e -> b p s e", p=P)
        yd = out.rearrange("b (s p) e -> b p s e", p=P)

        def made_value(n, j):
            return up_to(n, 7, j + 1 + 4)

        def fills_before(n, j):
            return up_to(n, 4 - j % 2, j // 2 + 2)

        def batch_end(eng, n):
            eng.nop().then_inc(s["x_batch_done"], 1)
            wait_apart(eng, s, s["x_batch_done"], up_to(n, 4, 4))

        with nc.Block() as block:

            @block.sync
            def _(sp):
                for dst, name in ((wq, "wq"), (wk, "wk"), (wv, "wv"), (wo, "wo")):
                    sp.dma_start(dst[:, :, :], w[name].rearrange("(c p) n -> p c n", p=P)).then_inc(s["x_weights"], 16)
                sp.dma_start(alpha[:, :], w["alpha"].partition_broadcast(P)).then_inc(s["x_weights"], 16)
                with sp.Fori(0, B) as n:
                    sp.dma_start(ctok[:, :, :], cs[n]).then_inc(s["x_ctx"], 16)
                    sp.dma_start(xtok[:, :, :], xs[n]).then_inc(s["x_x"], 16)
                    wait_apart(sp, s, s["x_y"], up_to(n, 2, 2))
                    sp.dma_start(yd[n], y[:, :, :]).then_inc(s["x_out"], 16)
                    sp.wait_ge(s["x_out"], up_to(n, 16, 16))
                    batch_end(sp, n)

            @block.tensor
            def _(pe):
                pe.wait_ge(s["x_weights"], 16 * 5)
                for i, (a, b_) in enumerate(((wk, wq), (wv, wo))):
                    for half in range(2):
                        if i:
                            pe.wait_ge(s[f"x_free{half}"], i)
                        for r in range(2):
                            o = 2 * half + r
                            for c in range(NC):
                                m = pe.matmul(D[half][:, r, :], a[:, c, o * P:(o + 1) * P], b_[:, c, :],
                                              start=(c == 0), stop=(c == NC - 1))
                        m.then_inc(s["x_dense"], 1)
                pe.wait_ge(s["x_free0"], 2)
                pe.wait_ge(s["x_free1"], 2)

                def batch(n):
                    def free(j):
                        pe.wait_ge(s[f"x_free{j % 2}"], fills_before(n, j))
                        return D[j % 2], dcm[j % 2]

                    def evacuated(j):
                        pe.wait_ge(s[f"x_free{j % 2}"], fills_before(n, j) + 1)

                    def done(m):
                        m.then_inc(s["x_dense"], 1)

                    for j, src, loaded in ((X_CT, ctok, "x_ctx"), (X_XT, xtok, "x_x")):
                        pe.wait_ge(s[loaded], up_to(n, 16, 16))
                        _, dc = free(j)
                        for c in range(NC):
                            for tt in range(TT):
                                m = pe.transpose(dc[:, c, tt * P:(tt + 1) * P], src[:, tt, c * P:(c + 1) * P],
                                                 ident[:, :])
                        done(m)
                    _, dc = free(X_K)
                    for o in range(NC):
                        for c in range(NC):
                            m = pe.matmul(dc[:, o, :], wkq[:, c, o * P:(o + 1) * P], cT[:, c, :],
                                          start=(c == 0), stop=(c == NC - 1))
                    done(m)
                    dt_, _ = free(X_V)
                    for tt in range(TT):
                        for c in range(NC):
                            m = pe.matmul(dt_[:, tt, :], cT[:, c, tt * P:(tt + 1) * P], wvo[:, c, :],
                                          start=(c == 0), stop=(c == NC - 1))
                    done(m)
                    evacuated(X_K)
                    dt_, _ = free(X_S)
                    for tt in range(TT):
                        for c in range(NC):
                            m = pe.matmul(dt_[:, tt, 0:T], xT[:, c, tt * P:(tt + 1) * P], kT[:, c, :],
                                          start=(c == 0), stop=(c == NC - 1))
                    done(m)
                    evacuated(X_S)
                    _, dc = free(X_PT)
                    for kt in range(TT):
                        for tt in range(TT):
                            m = pe.transpose(dc[:, kt, tt * P:(tt + 1) * P], probs[:, tt, kt * P:(kt + 1) * P],
                                             ident[:, :])
                    done(m)
                    evacuated(X_PT)
                    dt_, _ = free(X_O)
                    for tt in range(TT):
                        for kt in range(TT):
                            m = pe.matmul(dt_[:, tt, :], pT[:, kt, tt * P:(tt + 1) * P], v[:, kt, :],
                                          start=(kt == 0), stop=(kt == TT - 1))
                    done(m)

                with pe.Fori(0, B) as n:
                    batch(n)
                    pe.wait_ge(s["x_dense"], made_value(n, X_O))
                    batch_end(pe, n)

            @block.scalar
            def _(act):
                for i, dst in enumerate((wkq, wvo)):
                    for half in range(2):
                        act.wait_ge(s["x_dense"], 2 * i + half + 1)
                        act.activation(dst[:, 2 * half:2 * half + 2, :], D[half][:, :, :], ACT.Copy)\
                           .then_inc(s[f"x_free{half}"], 1)

                def batch(n):
                    def made(j):
                        act.wait_ge(s["x_dense"], made_value(n, j))
                        return D[j % 2], dcm[j % 2]

                    def done(m, j):
                        m.then_inc(s[f"x_free{j % 2}"], 1)

                    _, dc = made(X_CT)
                    done(act.activation(cT[:, :, :], dc, ACT.Copy), X_CT)
                    _, dc = made(X_XT)
                    done(act.activation(xT[:, :, :], dc, ACT.Copy), X_XT)
                    _, dc = made(X_K)
                    done(act.activation(kT[:, :, :], dc, ACT.Copy), X_K)
                    act.wait_ge(s["x_neg"], up_to(n, 1, 1))
                    dt_, _ = D[X_S % 2], None
                    for tt in range(TT):
                        m = act.activation(probs[:, tt, :], dt_[:, tt, 0:T], ACT.Exp, bias=neg[:, tt:tt + 1],
                                           scale=scale, accum_out=total[:, tt:tt + 1])
                    done(m, X_S)
                    _, dc = made(X_PT)
                    done(act.activation(pT[:, :, :], dc[:, 0:TT, :], ACT.Copy), X_PT)

                with act.Fori(0, B) as n:
                    batch(n)
                    act.wait_ge(s["x_free1"], fills_before(n, X_PT) + 1)
                    batch_end(act, n)

            @block.vector
            def _(dve):
                dve.wait_ge(s["x_weights"], 16 * 5)

                def batch(n):
                    def made(j):
                        dve.wait_ge(s["x_dense"], made_value(n, j))
                        return D[j % 2], dcm[j % 2]

                    dt_, _ = made(X_V)
                    dve.tensor_copy(v[:, :, :], dt_[:, :, :]).then_inc(s["x_free1"], 1)
                    dt_, _ = made(X_S)
                    dve.tensor_reduce(top, dt_[:, :, 0:T], AX, ALU.max).then_inc(s["x_top"], 1)
                    dve.wait_ge(s["x_top"], up_to(n, 1, 1))
                    dve.tensor_scalar(neg, top, -scale, None, ALU.mult).then_inc(s["x_neg"], 1)
                    dve.wait_ge(s["x_free0"], fills_before(n, X_S) + 1)
                    dve.reciprocal(inv, total).then_inc(s["x_inv"], 1)
                    dve.wait_ge(s["x_inv"], up_to(n, 1, 1))
                    dve.tensor_scalar(gain, inv, alpha[:, 0:1], None, ALU.mult).then_inc(s["x_gain"], 1)
                    dve.wait_ge(s["x_gain"], up_to(n, 1, 1))
                    dve.wait_ge(s["x_x"], up_to(n, 16, 16))
                    dt_, _ = made(X_O)
                    for tt in range(TT):
                        m = dve.scalar_tensor_tensor(out=y[:, tt, :], in0=dt_[:, tt, :], scalar=gain[:, tt:tt + 1],
                                                     in1=xtok[:, tt, :], op0=ALU.mult, op1=ALU.add)
                        m.then_inc(s["x_y"], 1)
                    dve.wait_ge(s["x_y"], up_to(n, 2, 2))
                    dve.nop().then_inc(s["x_free0"], 1)

                with dve.Fori(0, B) as n:
                    batch(n)
                    batch_end(dve, n)


RWKV_SEMS = """weights zeros step_done dense free0 free1 spread kv s0_in wrep scanned rs rs_pool reduced o_read
x_residual x_new x_stored x_loaded centred squared hsum hvar hrs gn_scaled gated stats1 moments1 rstd1 normed1
stats2 moments2 rstd2 normed2 shifted1 shifted2 mix0 mix2 kk tanh1 shift_mixed mixed tanh_d decay v v_high
v_low g_tanh ruk""".split()
LATENT_SEMS = """l_batch_done l_weights l_zeros l_ctx l_x l_mask l_bias l_dense l_free0 l_free1 l_scores l_masked
l_neg l_exp l_values l_o_read l_inv l_scaled l_attended l_residual l_squares l_biased l_rstd l_normed l_new
l_stored""".split()
CROSS_SEMS = """x_batch_done x_weights x_ctx x_x x_dense x_free0 x_free1 x_top x_neg x_inv x_gain x_y x_out""".split()


def four_layers(nc, t, out):
    scratch = [nc.dram_tensor(f"x_after_{i}", [B, T, E], F32, kind="Internal").ap() for i in range(3)]
    with ExitStack() as ctx:
        def sb(name, shape, dt=F32):
            return ctx.enter_context(nc.sbuf_tensor(name, shape, dt))

        s = {n: ctx.enter_context(nc.semaphore("s_" + n)) for n in ["constants", "rounded", "parted"] + RWKV_SEMS + LATENT_SEMS + CROSS_SEMS}
        k = dict(
            ident=sb("ident", [P, P]), stT=sb("stT", [P, B, 2, NC]), s0=sb("s0", [P, B, NC, S]),
            selr=sb("selr", [P, S, P], F32R), red=sb("red", [P, 4, 32]), head8=sb("head8", [P, HT]),
            nhalf=sb("nhalf", [P, 64]),
            D=[ctx.enter_context(nc.psum_tensor(f"D{i}", [P, 2, 512], F32)) for i in range(2)],
            V=[ctx.enter_context(nc.psum_tensor(f"V{i}", [P, 512], F32)) for i in range(2)],
            O=[ctx.enter_context(nc.psum_tensor(f"O{i}", [P, 512], F32)) for i in range(2)],
        )
        with nc.sbuf_tensor("sel", [P, S, P], F32) as sel, nc.Block() as block:
            @block.sync
            def _(sp):
                for dst, name in ((k["ident"], "c_ident"), (sel, "c_sel"), (k["red"], "c_red"), (k["head8"], "c_head8"),
                                  (k["stT"], "state_rows"), (k["s0"], "state_heads")):
                    sp.dma_start(dst[tuple([slice(None)] * len(dst.shape))], t[name]).then_inc(s["constants"], 16)
                sp.wait_ge(s["constants"], 16 * 6)

            @block.vector
            def _(dve):
                dve.memset(k["nhalf"][:, :], -0.5).then_inc(s["rounded"], 1)
                dve.wait_ge(s["constants"], 16 * 6)
                dve.tensor_copy(k["selr"][:, :, :], sel[:, :, :]).then_inc(s["rounded"], 1)
                dve.wait_ge(s["rounded"], 2)

        def rw(i):
            return {n: t[f"r{i}_{n}"] for n in ("w1", "w2", "td1", "td2", "Wk", "Wv", "Wr", "Wg", "Wo", "Wfr", "Wfk", "Wfv", "par")}

        rwkv_layer(nc, 0, k, s, rw(0), t["x"], scratch[0])
        latent_layer(nc, k, s, {n: t["l_" + n] for n in ("wq", "wk", "wv", "wo", "w1", "w2", "par", "expand", "out_b", "b2")},
                     t["ctx"], t["mask"], scratch[0], scratch[1])
        rwkv_layer(nc, 1, k, s, rw(1), scratch[1], scratch[2])
        cross_layer(nc, k, s, {n: t["x_" + n] for n in ("wq", "wk", "wv", "wo", "alpha")}, t["ctx"], scratch[2], out)


def laid_out(inputs):
    a = {n: np.asarray(x) for n, x in inputs.items()}
    cols = lambda v: v.reshape(-1, P).T
    head = np.arange(P) // S
    row = np.arange(P) % S
    sel = np.zeros((P, S, P), np.float32)
    for j in range(S):
        sel[:, j, :] = (head[:, None] == head[None, :]) & (row[:, None] == j)
    red = np.zeros((P, 4, 32), np.float32)
    for jg in range(4):
        red[np.arange(P), jg, HT * jg + head] = 1.0
    ctx = a["ctx_2048"]
    t = {
        "x": a["x"], "ctx": ctx, "mask": a["mask_BxS2_ik0"].reshape(B, 1, T),
        "c_ident": np.eye(P, dtype=np.float32), "c_sel": sel, "c_red": red,
        "c_head8": (head[:, None] == np.arange(HT)[None, :]).astype(np.float32),
        "state_rows": ctx[:, 0:2].reshape(B, 2, NC, P).transpose(3, 0, 1, 2),
        "state_heads": ctx[:, 2:2 + S].reshape(B, NC, P, S).transpose(2, 0, 1, 3),
    }
    for i, pre, names in ((0, "L0_xattn_", ("td_w1", "td_w2", "u", "Wfk", "Wfr", "Wfv")),
                          (1, "L2_xattn_", ("decay_w1", "decay_w2", "faaaa", "ffn_Wk", "ffn_Wr", "ffn_Wv"))):
        td1, td2, u, fk, fr, fv = (a[pre + n] for n in names)
        g = lambda n: a[pre + n]
        stack = g("maa_stack").reshape(5, E)
        vectors = [g("ln1_w"), g("ln1_b"), g("maa_x"), *stack, g("time_decay"), u.reshape(E), g("gn_w"), g("gn_b"),
                   g("ln2_w"), g("ln2_b"), g("ffn_maa_k"), g("ffn_maa_r")]
        t |= {f"r{i}_w1": g("maa_w1"), f"r{i}_w2": g("maa_w2").reshape(5 * DM, E), f"r{i}_td1": td1, f"r{i}_td2": td2,
              f"r{i}_Wk": g("Wk").T, f"r{i}_Wv": g("Wv").T, f"r{i}_Wr": g("Wr").T, f"r{i}_Wg": g("Wg").T,
              f"r{i}_Wo": g("Wo").T, f"r{i}_Wfr": fr.T, f"r{i}_Wfk": fk.T, f"r{i}_Wfv": fv.T,
              f"r{i}_par": np.stack([cols(v) for v in vectors], axis=1)}
    g = lambda n: a["L1_xattn_" + n]
    kvw, kvb = g("kv_w").reshape(E, E, 2), g("kv_b").reshape(E, 2)
    t |= {"l_wq": g("q_w"), "l_wk": kvw[:, :, 0], "l_wv": kvw[:, :, 1], "l_wo": g("out_w"), "l_w1": g("mlp_w1"),
          "l_w2": g("mlp_w2"),
          "l_par": np.concatenate([cols(v) for v in (g("q_b"), kvb[:, 0], kvb[:, 1], g("postnorm_w"), g("mlp_b1"))], axis=1),
          "l_expand": (np.arange(NH)[:, None] == np.arange(E)[None, :] // DH).astype(np.float32),
          "l_out_b": g("out_b").reshape(1, E), "l_b2": g("mlp_b2").reshape(1, E)}
    g = lambda n: a["L3_xattn_" + n]
    t |= {"x_wq": g("w_q"), "x_wk": g("w_k"), "x_wv": g("w_v"), "x_wo": g("w_o").T, "x_alpha": g("alpha").reshape(1, 1)}
    return {n: np.ascontiguousarray(x) for n, x in t.items()}


def kernel(**inputs):
    import concourse.bacc as bacc
    from concourse.bass_utils import run_bass_kernel_spmd

    nc = bacc.Bacc("TRN2", target_bir_lowering=False, num_devices=1)
    arrays = {f"in_{n}": x for n, x in laid_out(inputs).items()}
    t = {n[3:]: nc.dram_tensor(n, x.shape, mybir.dt.from_np(x.dtype), kind="ExternalInput").ap()
         for n, x in arrays.items()}
    out = nc.dram_tensor("out", [B, T, E], F32, kind="ExternalOutput").ap()
    four_layers(nc, t, out)
    r = run_bass_kernel_spmd(nc, [arrays], core_ids=[0])
    return r.results[0]["out"]
```

```python
import numpy as np
from contextlib import ExitStack

import concourse.bass as bass
from concourse import mybir

F32 = mybir.dt.float32
F32R = mybir.dt.float32r
I32 = mybir.dt.int32
ALU = mybir.AluOpType
ACT = mybir.ActivationFunctionType
AX = mybir.AxisListType.X

P = 128
E = 512
NC = E // P
B = 8
T = 256
TT = T // P
S = 16
HT = P // S
DM = 32
DD = 64
NG = 16
EPS = 1e-5

(LN1W, LN1B, MAAX, MAAK, MAAW, MAAV, MAAR, MAAG, DECAY, BONUS,
 GNW, GNB, LN2W, LN2B, FMK, FMR) = range(16)
NPAR = 16

(A_XK, C_OT, A_XW, A_PK, A_XR, A_PD1, C_GNT, A_XG, A_PD2, A_PR, C_WO, A_XV, C_XT, A_PG, C_FR, A_CF,
 C_FK, A_PV, C_FV, F_XT, A_VT, F_W1) = range(22)
NJ = 22
IN_C = (C_OT, C_GNT, C_WO, C_XT, C_FR, C_FK, C_FV)
IN_F = (F_XT, F_W1)
MIXES = {A_XK: (0, 0, F_XT), A_XW: (1, 1, F_W1), A_XR: (3, 2, A_PK), A_XG: (4, 3, A_PD1), A_XV: (2, 4, A_PR)}
SLOTS = [[A_XK, C_OT], [A_XW, A_PK], [A_XR, A_PD1], [C_GNT, A_XG], [A_PD2, A_PR], [C_WO], [A_XV], [C_XT, A_PG],
         [C_FR], [A_CF], [C_FK], [A_PV], [C_FV, F_XT], [A_VT], [F_W1], []]
ON_POOL = (1, 3, 5, 7, 9, 11, 13)


NEWTON = 3
ROOT_STEPS = 2 + 3 * NEWTON


def up_to(n, per, k):
    return n * per + k


def wait(eng, sem, value):
    if not (isinstance(value, int) and value <= 0):
        eng.wait_ge(sem, value)


def wait_apart(eng, s, sem, value):
    eng.wait_ge(sem, value)
    eng.nop().then_inc(s["parted"], 1)


def in_step(t, j):
    return 0 <= (t - 1 if j in IN_C else t + 2 if j in IN_F else t + 1) < B


class Step:

    def __init__(self, layer, t, u=None):
        tt = t if u is None else u * 2 + t
        self.first_t, self.t, self.parity = t, tt, t % 2
        self.wkv, self.behind = 0 <= t < B, in_step(t, C_OT)
        self.ahead, self.first = in_step(t, A_XK), in_step(t, F_XT)
        self.nb, self.nc = tt + B * layer, tt + (B * layer - 1)
        self.na, self.nf = tt + (B * layer + 1), tt + (B * layer + 2)
        self.steps = tt + (2 + (B + 3) * layer)
        made = [sum(in_step(i, j) for i in range(-2, t) for j in range(p, NJ, 2)) + B * layer * NJ // 2
                for p in range(2)]
        self.fills = [m if u is None else u * NJ + m for m in made]
        self.jobs = sum(made) if u is None else u * (2 * NJ) + sum(made)

    def job(self, j):
        return self.jobs + sum(in_step(self.first_t, i) for i in range(j + 1))

    def fills_before(self, j):
        return self.fills[j % 2] + sum(in_step(self.first_t, i) for i in range(j % 2, j, 2))

    def read(self, j):
        return self.fills_before(j) + 1


def pipeline(eng, layer, body):
    for t in (-2, -1, 0):
        body(Step(layer, t))
    with eng.Fori(0, 2) as u:
        body(Step(layer, 1, u))
        body(Step(layer, 2, u))
    for t in (5, 6, 7, 8):
        body(Step(layer, t))


def rwkv_layer(nc, layer, k, sems, w, x_src, x_dst):
    ident, stT, s0, selr, red, head8 = k["ident"], k["stT"], k["s0"], k["selr"], k["red"], k["head8"]
    tag = f"r{layer}_"
    with ExitStack() as ctx:
        def sb(name, shape, dt=F32):
            return ctx.enter_context(nc.sbuf_tensor(tag + name, shape, dt))

        wr, wk, wv, wg, wo = (sb(n, [P, NC, E]) for n in ("wr", "wk", "wv", "wg", "wo"))
        wfk, wfr, wfv = (sb(n, [P, NC, E]) for n in ("wfk", "wfr", "wfv"))
        w1 = sb("w1", [P, NC, 5 * DM])
        w2 = sb("w2", [P, E])
        w2g = sb("w2g", [P, E])
        td1 = sb("td1", [P, NC, DD])
        td2 = sb("td2", [P, E])
        par = sb("par", [P, NPAR, NC])

        decay = [sb(f"decay{i}", [P, NC, T + 1]) for i in range(2)]
        kT = [sb(f"kT{i}", [P, NC, T]) for i in range(2)]
        rT = [sb(f"rT{i}", [P, NC, T]) for i in range(2)]
        vhi = [sb(f"vhi{i}", [P, NC, T], F32R) for i in range(2)]
        vlo = [sb(f"vlo{i}", [P, NC, T], F32R) for i in range(2)]
        gT = [sb(f"gT{i}", [P, NC, T]) for i in range(2)]
        uv = [sb(f"uv{i}", [P, TT, E]) for i in range(2)]
        oP = sb("oP", [P, NC, T])
        wrep = sb("wrep", [P, 4, T])
        drive = sb("drive", [P, 4, T])
        state = [sb(f"state{i}", [P, 4, T]) for i in range(2)]
        a0, sx, m0, m1 = (sb(n, [P, 1024]) for n in ("a0", "sx", "m0", "m1"))
        ext = sb("ext", [P, NC, T + 1])
        c0, c1, xr = (sb(n, [P, 1024]) for n in ("c0", "c1", "xr"))
        ext2 = sb("ext2", [P, NC, T + 1])
        th = sb("th", [P, 4, T])
        thg = sb("thg", [P, T])
        td = sb("td", [P, T])
        small = sb("small", [P, 384])
        norms = {w: (small[:, o:o + 12].rearrange("p (a b) -> p a b", a=2),
                     small[:, o + 16:o + 20].rearrange("p (a b) -> p a b", a=2),
                     small[:, o + 24:o + 26], small[:, o + 28:o + 30]) for w, o in (("1", 0), ("2", 32))}
        hsum = small[:, 64:128]
        hvar = small[:, 128:192]
        hve = small[:, 192:256]
        hrs = small[:, 256:320]
        coef = small[:, 320:384]
        nhalf = k["nhalf"]

        def cm(x):
            return x[:, :].rearrange("p (c t) -> p c t", c=NC)

        def tm(x):
            return x[:, :].rearrange("p (s e) -> p s e", s=TT)

        D, V, O = k["D"], k["V"], k["O"]
        dcm = [d[:, :, :].rearrange("p b (c t) -> p (b c) t", t=T) for d in D]

        s = sems
        xs = x_src.rearrange("b (s p) e -> b p s e", p=P)
        xd = x_dst.rearrange("b (s p) e -> b p s e", p=P)

        def step_end(eng, st):
            eng.nop().then_inc(s["step_done"], 1)
            wait_apart(eng, s, s["step_done"], up_to(st.steps, 5, 5))

        def job_of(st, j):
            return D[j % 2], dcm[j % 2]

        with nc.Block() as block:

            @block.sync
            def _(sp):
                for dst, name in ((w1, "w1"), (td1, "td1"), (wk, "Wk"), (wv, "Wv"), (wr, "Wr"), (wg, "Wg"),
                                  (wo, "Wo"), (wfr, "Wfr"), (wfk, "Wfk"), (wfv, "Wfv")):
                    sp.dma_start(dst[:, :, :], w[name].rearrange("(c p) n -> p c n", p=P)).then_inc(s["weights"], 16)
                sp.dma_start(w2[:, :], w["w2"][0:P, :]).then_inc(s["weights"], 16)
                sp.wait_ge(s["zeros"], up_to(layer, 7, 2))
                sp.dma_start(w2g[0:DM, :], w["w2"][P:P + DM, :]).then_inc(s["weights"], 16)
                sp.dma_start(td2[0:DD, :], w["td2"]).then_inc(s["weights"], 16)
                sp.dma_start(par[:, :, :], w["par"]).then_inc(s["weights"], 16)
                sp.wait_ge(s["weights"], up_to(layer, 16 * 14, 16 * 14))

                def body(st):
                    if st.behind:
                        sp.dma_start(tm(xr), xs[st.t - 1]).then_inc(s["x_residual"], 16)
                    if st.first:
                        if st.ahead:
                            wait_apart(sp, s, s["dense"], st.job(A_CF))
                        sp.dma_start(tm(a0), xs[st.t + 2]).then_inc(s["x_loaded"], 16)
                        wait_apart(sp, s, s["x_loaded"], up_to(st.nf, 16, 16))
                    if st.behind:
                        wait_apart(sp, s, s["x_new"], up_to(st.nc, 1, 1))
                        sp.dma_start(xd[st.t - 1], tm(xr)).then_inc(s["x_stored"], 16)
                        sp.wait_ge(s["x_stored"], up_to(st.nc, 16, 16))
                    step_end(sp, st)

                pipeline(sp, layer, body)

            @block.tensor
            def _(pe):
                pe.wait_ge(s["weights"], up_to(layer, 16 * 14, 16 * 14))
                pe.wait_ge(s["zeros"], up_to(layer, 7, 7))

                def free(st, j):
                    wait(pe, s[f"free{j % 2}"], st.fills_before(j))
                    return job_of(st, j)

                def transposes_cm(dst, src):
                    for c in range(NC):
                        for tt in range(TT):
                            m = pe.transpose(dst[:, c, tt * P:(tt + 1) * P], src[:, tt, c * P:(c + 1) * P], ident[:, :])
                    return m

                def transposes_tm(dst, src):
                    for tt in range(TT):
                        for c in range(NC):
                            m = pe.transpose(dst[:, tt, c * P:(c + 1) * P], src[:, c, tt * P:(tt + 1) * P], ident[:, :])
                    return m

                def product_cm(dst, wt, x):
                    for o in range(NC):
                        for c in range(NC):
                            m = pe.matmul(dst[:, o, :], wt[:, c, o * P:(o + 1) * P], x[:, c, :],
                                          start=(c == 0), stop=(c == NC - 1))
                    return m

                def product_tm(dst, wt, x):
                    for tt in range(TT):
                        for c in range(NC):
                            m = pe.matmul(dst[:, tt, :], x[:, c, tt * P:(tt + 1) * P], wt[:, c, :],
                                          start=(c == 0), stop=(c == NC - 1))
                    return m

                def dense(st, j):
                    dt_, dc = free(st, j)
                    q = st.parity
                    if j == C_OT:
                        m = transposes_tm(dt_, oP)
                    elif j == C_GNT:
                        pe.wait_ge(s["gn_scaled"], up_to(st.nc, 1, 1))
                        m = transposes_cm(dc, tm(c1))
                    elif j == C_WO:
                        pe.wait_ge(s["gated"], up_to(st.nc, 1, 1))
                        m = product_tm(dt_, wo, cm(c0))
                    elif j == C_XT:
                        pe.wait_ge(s["normed2"], up_to(st.nc, 2, 2))
                        m = transposes_cm(dc, tm(c1))
                    elif j == C_FR:
                        pe.wait_ge(s["mix2"], up_to(st.nc, 8, 4))
                        m = product_tm(dt_, wfr, cm(c1))
                    elif j == C_FK:
                        pe.wait_ge(s["mix2"], up_to(st.nc, 8, 8))
                        m = product_cm(dc, wfk, cm(c1))
                    elif j == C_FV:
                        pe.wait_ge(s["kk"], up_to(st.nc, 1, 1))
                        m = product_tm(dt_, wfv, cm(c1))
                    elif j == F_XT:
                        pe.wait_ge(s["normed1"], up_to(st.nf, 2, 2))
                        m = transposes_cm(dc, tm(m0))
                    elif j == F_W1:
                        pe.wait_ge(s["mix0"], up_to(st.nf, 4, 4))
                        for c in range(NC):
                            pe.matmul(dt_[:, 0, 0:T], w1[:, c, 0:P], cm(m0)[:, c, :], start=(c == 0), stop=(c == NC - 1))
                        for c in range(NC):
                            m = pe.matmul(dt_[0:DM, 0, T:2 * T], w1[:, c, P:P + DM], cm(m0)[:, c, :],
                                          start=(c == 0), stop=(c == NC - 1))
                    elif j in MIXES:
                        f = MIXES[j][0]
                        pe.wait_ge(s["tanh1"], up_to(st.na, 5, 5))
                        for o in range(NC):
                            lhs = w2 if f < 4 else w2g
                            m = pe.matmul(dc[:, o, :], lhs[:, o * P:(o + 1) * P], th[:, f, :] if f < 4 else thg[:, :],
                                          start=True, stop=True)
                    elif j in (A_PK, A_PV, A_PR, A_PG):
                        turn, wt = {A_PK: (0, wk), A_PR: (2, wr), A_PG: (3, wg), A_PV: (4, wv)}[j]
                        pe.wait_ge(s["mixed"], up_to(st.na, 5, turn + 1))
                        m = product_cm(dc, wt, cm((m0, m1)[turn % 2]))
                    elif j == A_PD1:
                        pe.wait_ge(s["mixed"], up_to(st.na, 5, 2))
                        for c in range(NC):
                            m = pe.matmul(dt_[0:DD, 0, 0:T], td1[:, c, :], cm(m1)[:, c, :], start=(c == 0), stop=(c == NC - 1))
                    elif j == A_PD2:
                        pe.wait_ge(s["tanh_d"], up_to(st.na, 1, 1))
                        for o in range(NC):
                            m = pe.matmul(dc[:, o, :], td2[:, o * P:(o + 1) * P], td[:, :], start=True, stop=True)
                    elif j == A_CF:
                        pe.wait_ge(s["ruk"], up_to(st.na, 4, 4))
                        for tt in range(TT):
                            for c in range(NC):
                                m = pe.matmul(dt_[:, 0, (tt * NC + c) * HT:(tt * NC + c + 1) * HT],
                                              cm(a0)[:, c, tt * P:(tt + 1) * P], head8[:, :], start=True, stop=True)
                    elif j == A_VT:
                        pe.wait_ge(s["v"], up_to(st.na, 1, 1))
                        m = transposes_tm(dt_, cm(m1))
                    m.then_inc(s["dense"], 1)

                def spread_v(st, g):
                    c, jg = g // 4, g % 4
                    for half in range(2):
                        n = 2 * g + half
                        if n >= 2:
                            pe.wait_ge(s["kv"], up_to(st.nb, 2 * NG, n - 1))
                        for i in range(2):
                            j = 4 * (2 * half + i) + jg
                            for part in (vhi, vlo):
                                m = pe.matmul(V[half][:, i * T:(i + 1) * T], selr[:, j, :], part[st.parity][:, c, :],
                                              start=(part is vhi), stop=(part is vlo))
                        m.then_inc(s["spread"], 1)

                def reduce_heads(st, g):
                    c, jg = g // 4, g % 4
                    if jg == 0 and c >= 2:
                        pe.wait_ge(s["o_read"], up_to(st.nb, NC, c - 1))
                    pe.wait_ge(s["rs"] if g not in ON_POOL else s["rs_pool"],
                               rs_value(st, g))
                    for q in range(4):
                        m = pe.matmul(O[c % 2][32 * q:32 * q + 32, 0:T], red[:, jg, :], state[g % 2][:, q, :],
                                      start=(jg == 0), stop=(jg == 3))
                    m.then_inc(s["reduced"], 1)

                def body(st):
                    if st.wkv:
                        spread_v(st, 0)
                    for g in range(NG):
                        if st.wkv and g >= 1:
                            spread_v(st, g)
                        for j in SLOTS[g]:
                            if in_step(st.first_t, j):
                                dense(st, j)
                        if st.wkv and g >= 1:
                            reduce_heads(st, g - 1)
                    if st.wkv:
                        reduce_heads(st, NG - 1)
                        pe.wait_ge(s["reduced"], up_to(st.nb, NG, NG))
                    pe.wait_ge(s["dense"], st.job(NJ - 1))
                    step_end(pe, st)

                pipeline(pe, layer, body)

            @block.scalar
            def _(act):
                act.wait_ge(s["weights"], up_to(layer, 16 * 14, 16 * 14))
                act.wait_ge(s["zeros"], up_to(layer, 7, 7))

                def dense(st, j):
                    dt_, dc = job_of(st, j)
                    q = st.parity

                    def made():
                        act.wait_ge(s["dense"], st.job(j))

                    fr = s[f"free{j % 2}"]
                    if j == C_OT:
                        act.wait_ge(s["centred"], up_to(st.nc, 1, 1))
                        act.activation(oP[:, :, :].rearrange("p c t -> p (c t)"), c1[:, :], ACT.Square)\
                           .then_inc(s["squared"], 1)
                    elif j == C_GNT:
                        made()
                        for c in range(NC):
                            m = act.activation(cm(c0)[:, c, :], dc[:, c, :], ACT.Identity,
                                               bias=par[:, GNB, c:c + 1], scale=par[:, GNW, c:c + 1])
                        m.then_inc(fr, 1)
                    elif j in (C_XT, F_XT):
                        dst, lw, lb, row, batch = ((ext2, LN2W, LN2B, 0, st.t - 1) if j == C_XT
                                                   else (ext, LN1W, LN1B, 1, st.t + 2))
                        made()
                        act.activation(dst[:, :, 0:1], stT[:, bass.ds(batch, 1), row, :].rearrange("p a c -> p c a"),
                                       ACT.Copy)
                        for c in range(NC):
                            m = act.activation(dst[:, c, 1:T + 1], dc[:, c, :], ACT.Identity,
                                               bias=par[:, lb, c:c + 1], scale=par[:, lw, c:c + 1])
                        m.then_inc(fr, 1)
                    elif j == C_FR:
                        made()
                        act.wait_ge(s["mix2"], up_to(st.nc, 8, 8))
                        act.activation(tm(c0), dt_[:, :, :], ACT.Tanh, scale=0.5).then_inc(fr, 1)
                    elif j == C_FK:
                        made()
                        act.activation(cm(c1), dc, ACT.Relu).then_inc(fr, 1)
                        act.wait_ge(fr, st.read(j))
                        act.activation(c1[:, :], c1[:, :], ACT.Square).then_inc(s["kk"], 1)
                    elif j == F_W1:
                        made()
                        for f in range(4):
                            act.activation(th[f * DM:(f + 1) * DM, f, :], dt_[f * DM:(f + 1) * DM, 0, 0:T],
                                           ACT.Tanh).then_inc(s["tanh1"], 1)
                        act.activation(thg[0:DM, :], dt_[0:DM, 0, T:2 * T], ACT.Tanh).then_inc(s["tanh1"], 1)
                        act.wait_ge(s["tanh1"], up_to(st.nf, 5, 5))
                        act.nop().then_inc(fr, 1)
                    elif j == A_PK:
                        made()
                        act.activation(kT[1 - q][:, :, :], dc, ACT.Copy).then_inc(fr, 1)
                    elif j == A_PR:
                        made()
                        act.activation(rT[1 - q][:, :, :], dc, ACT.Copy).then_inc(fr, 1)
                    elif j == A_PD1:
                        made()
                        act.activation(td[0:DD, :], dt_[0:DD, 0, 0:T], ACT.Tanh).then_inc(s["tanh_d"], 1)
                        act.wait_ge(s["tanh_d"], up_to(st.na, 1, 1))
                        act.nop().then_inc(fr, 1)
                    elif j == A_PD2:
                        made()
                        for c in range(NC):
                            m = act.activation(cm(a0)[:, c, :], dc[:, c, :], ACT.Exp, bias=par[:, DECAY, c:c + 1])
                        m.then_inc(fr, 1)
                        act.wait_ge(fr, st.read(j))
                        act.activation(decay[1 - q][:, :, 1:T + 1], cm(a0), ACT.Exp, scale=-1.0).then_inc(s["decay"], 1)
                    elif j == A_PV:
                        made()
                        act.activation(cm(m1), dc, ACT.Copy).then_inc(s["v"], 1)
                        act.wait_ge(s["v"], up_to(st.na, 1, 1))
                        act.nop().then_inc(fr, 1)
                        act.activation(vhi[1 - q][:, :, :], cm(m1), ACT.Copy).then_inc(s["v_high"], 1)
                    elif j == A_PG:
                        made()
                        act.wait_ge(s["decay"], up_to(st.na, 1, 1))
                        act.activation(cm(a0), dc, ACT.Tanh, scale=0.5).then_inc(s["g_tanh"], 1)

                def wkv(st, g):
                    c, jg = g // 4, g % 4
                    if jg == 0:
                        if c >= 1:
                            act.wait_ge(s["scanned"], up_to(st.nb, NG, 4 * c))
                        act.activation(wrep[:, :, :], decay[st.parity][:, c:c + 1, 0:T].broadcast_to([P, 4, T]),
                                       ACT.Copy).then_inc(s["wrep"], 1)
                    if g >= 1:
                        act.wait_ge(s["scanned"], up_to(st.nb, NG, g))
                    act.activation(drive[:, :, 0:1],
                                   s0[:, bass.ds(st.t, 1), c, jg:S:4].rearrange("p a j -> p j a"),
                                   ACT.Copy).then_inc(s["s0_in"], 1)

                def read_o(st, c):
                    act.wait_ge(s["reduced"], up_to(st.nb, NG, 4 * c + 4))
                    if st.behind and c == 0:
                        act.wait_ge(s["hvar"], up_to(st.nc, 1, 1))
                    act.activation(oP[:, c, :], O[c % 2][:, 0:T], ACT.Copy).then_inc(s["o_read"], 1)

                def body(st):
                    for g in range(NG):
                        if st.wkv:
                            wkv(st, g)
                            if g % 4 == 1 and g >= 4:
                                read_o(st, g // 4 - 1)
                        for j in SLOTS[g]:
                            if in_step(st.first_t, j):
                                dense(st, j)
                    if st.wkv:
                        read_o(st, NC - 1)
                        act.wait_ge(s["o_read"], up_to(st.nb, NC, NC))
                    if st.first:
                        act.wait_ge(s["tanh1"], up_to(st.nf, 5, 5))
                    if st.ahead:
                        act.wait_ge(s["v_high"], up_to(st.na, 1, 1))
                    if st.behind:
                        act.wait_ge(s["kk"], up_to(st.nc, 1, 1))
                    step_end(act, st)

                pipeline(act, layer, body)

            @block.gpsimd
            def _(pool):
                pool.memset(w2g[:, :], 0.0).then_inc(s["zeros"], 1)
                pool.memset(td2[:, :], 0.0).then_inc(s["zeros"], 1)
                pool.memset(th[:, :, :], 0.0).then_inc(s["zeros"], 1)
                pool.memset(thg[:, :], 0.0).then_inc(s["zeros"], 1)
                pool.memset(td[:, :], 0.0).then_inc(s["zeros"], 1)
                pool.memset(decay[0][:, :, 0:1], 0.0).then_inc(s["zeros"], 1)
                pool.memset(decay[1][:, :, 0:1], 0.0).then_inc(s["zeros"], 1)

                def inverse_root(ssem, var, tmp, out, n, scale):
                    pool.tensor_scalar(tmp, var, scale, EPS, ALU.mult, ALU.add).then_inc(ssem, 1)
                    pool.wait_ge(ssem, up_to(n, 2, 1))
                    pool.tensor_tensor(out, tmp, nhalf[:, :], ALU.pow).then_inc(ssem, 1)

                def dense(st, j):
                    q = st.parity
                    if j == C_WO:
                        _, mv, vare, rstd = norms["2"]
                        wait_apart(pool, s, s["moments2"], up_to(st.nc, 2, 2))
                        inverse_root(s["rstd2"], mv[:, :, 1], vare, rstd, st.nc, 1.0)
                    elif j in MIXES:
                        turn = MIXES[j][1]
                        pool.wait_ge(s["shift_mixed"], up_to(st.na, 20, 4 * turn + 4))
                        m = cm((m0, m1)[turn % 2])
                        pool.tensor_tensor(m, m, ext[:, :, 1:T + 1], ALU.add).then_inc(s["mixed"], 1)
                    elif j == A_PV:
                        pool.wait_ge(s["v_high"], up_to(st.na, 1, 1))
                        pool.tensor_tensor(vlo[1 - q][:, :, :], cm(m1), vhi[1 - q][:, :, :].bitcast(F32),
                                           ALU.subtract).then_inc(s["v_low"], 1)

                def scale_heads(st):
                    pool.wait_ge(s["hrs"], up_to(st.nc, ROOT_STEPS, ROOT_STEPS))
                    v = c1[:, :].rearrange("p (h j) -> p h j", j=S)
                    pool.tensor_tensor(v, v, hrs.unsqueeze(2).broadcast_to([P, TT * NC * HT, S]),
                                       ALU.mult).then_inc(s["gn_scaled"], 1)

                def wkv(st, g):
                    if g in ON_POOL:
                        c = g // 4
                        pool.wait_ge(s["scanned"], up_to(st.nb, NG, g + 1))
                        pool.tensor_tensor(state[g % 2][:, :, :], state[g % 2][:, :, :],
                                           rT[st.parity][:, c:c + 1, :].broadcast_to([P, 4, T]),
                                           ALU.mult).then_inc(s["rs_pool"], 1)

                def body(st):
                    for g in range(NG):
                        if st.wkv:
                            wkv(st, g)
                        if st.first and C_FK in SLOTS[g]:
                            _, mv, vare, rstd = norms["1"]
                            wait_apart(pool, s, s["moments1"], up_to(st.nf, 2, 2))
                            inverse_root(s["rstd1"], mv[:, :, 1], vare, rstd, st.nf, 1.0)
                        for j in SLOTS[g]:
                            if in_step(st.first_t, j):
                                dense(st, j)
                        if st.behind and g == 1:
                            scale_heads(st)
                    if st.wkv:
                        pool.wait_ge(s["rs_pool"], up_to(st.nb, len(ON_POOL), len(ON_POOL)))
                    if st.ahead:
                        pool.wait_ge(s["v_low"], up_to(st.na, 1, 1))
                        pool.wait_ge(s["mixed"], up_to(st.na, 5, 5))
                    if st.behind:
                        pool.wait_ge(s["rstd2"], up_to(st.nc, 2, 2))
                    if st.first:
                        pool.wait_ge(s["rstd1"], up_to(st.nf, 2, 2))
                    step_end(pool, st)

                pipeline(pool, layer, body)

            @block.vector
            def _(dve):
                dve.wait_ge(s["weights"], up_to(layer, 16 * 14, 16 * 14))

                def moments(x, n, which):
                    stats, mv, _, rstd = norms[which]
                    for tt in range(TT):
                        dve.bn_stats(stats[:, tt, :], x[:, tt, :]).then_inc(s["stats" + which], 1)
                    for tt in range(TT):
                        wait_apart(dve, s, s["stats" + which], up_to(n, 2, tt + 1))
                        dve.bn_aggr(mv[:, tt, :], stats[:, tt, :]).then_inc(s["moments" + which], 1)

                def normalise(x, out, n, which):
                    stats, mv, _, rstd = norms[which]
                    dve.wait_ge(s["moments" + which], up_to(n, 2, 2))
                    dve.wait_ge(s["rstd" + which], up_to(n, 2, 2))
                    for tt in range(TT):
                        dve.tensor_scalar(out[:, tt, :], x[:, tt, :], mv[:, tt, 0:1], rstd[:, tt:tt + 1],
                                          ALU.subtract, ALU.mult).then_inc(s["normed" + which], 1)

                def inverse_root(sem, n, x, half, y):
                    done = [0]

                    def then(m):
                        m.then_inc(sem, 1)
                        done[0] += 1
                        dve.wait_ge(sem, up_to(n, ROOT_STEPS, done[0]))

                    then(dve.tensor_scalar(half.bitcast(I32), x.bitcast(I32), 1, None, ALU.logical_shift_right))
                    then(dve.tensor_scalar(y.bitcast(I32), half.bitcast(I32), -1, 0x5F3759DF, ALU.mult, ALU.add))
                    for _ in range(NEWTON):
                        then(dve.scalar_tensor_tensor(out=half, in0=y, scalar=-0.5, in1=y, op0=ALU.mult, op1=ALU.mult))
                        then(dve.tensor_tensor(half, half, x, ALU.mult))
                        then(dve.scalar_tensor_tensor(out=y, in0=half, scalar=1.5, in1=y, op0=ALU.add, op1=ALU.mult))

                def shift(src, out, sem):
                    dve.tensor_tensor(cm(out), src[:, :, 0:T], src[:, :, 1:T + 1], ALU.subtract).then_inc(sem, 1)

                def mix(out, shifted, src, coef_row, sem):
                    for c in range(NC):
                        dve.scalar_tensor_tensor(out=cm(out)[:, c, :], in0=cm(shifted)[:, c, :],
                                                 scalar=par[:, coef_row, c:c + 1], in1=src[:, c, 1:T + 1],
                                                 op0=ALU.mult, op1=ALU.add).then_inc(sem, 1)

                def dense(st, j):
                    dt_, dc = job_of(st, j)
                    q = st.parity

                    def made():
                        dve.wait_ge(s["dense"], st.job(j))

                    def read(j):
                        dve.wait_ge(s[f"free{j % 2}"], st.read(j))

                    fr = s[f"free{j % 2}"]
                    if j == C_OT:
                        made()
                        for tt in range(TT):
                            m = dve.tensor_tensor(
                                tm(c0)[:, tt, :].rearrange("p (c h j) -> p c h j", c=NC, h=HT),
                                dt_[:, tt, :].rearrange("p (c j h) -> p c h j", c=NC, h=HT),
                                uv[1 - q][:, tt, :].rearrange("p (c h j) -> p c h j", c=NC, h=HT), ALU.add)
                        m.then_inc(fr, 1)
                        read(j)
                        o = c0[:, :].rearrange("p (h j) -> p h j", j=S)
                        dve.tensor_reduce(hsum, o, AX, ALU.add).then_inc(s["hsum"], 1)
                        dve.wait_ge(s["hsum"], up_to(st.nc, 1, 1))
                        dve.scalar_tensor_tensor(out=c1[:, :].rearrange("p (h j) -> p h j", j=S),
                                                 in0=hsum.unsqueeze(2).broadcast_to([P, TT * NC * HT, S]),
                                                 scalar=-1.0 / S, in1=o, op0=ALU.mult, op1=ALU.add)\
                           .then_inc(s["centred"], 1)
                    elif j == C_GNT:
                        read(j)
                        dve.scalar_tensor_tensor(out=cm(c0), in0=cm(c0), scalar=0.5, in1=gT[1 - q][:, :, :],
                                                 op0=ALU.mult, op1=ALU.mult).then_inc(s["gated"], 1)
                    elif j == C_WO:
                        made()
                        dve.wait_ge(s["x_residual"], up_to(st.nc, 16, 16))
                        dve.tensor_tensor(tm(xr), tm(xr), dt_[:, :, :], ALU.add).then_inc(fr, 1)
                        read(j)
                        moments(tm(xr), st.nc, "2")
                        normalise(tm(xr), tm(c1), st.nc, "2")
                    elif j == C_XT:
                        read(j)
                        shift(ext2, c0, s["shifted2"])
                        dve.wait_ge(s["shifted2"], up_to(st.nc, 1, 1))
                        mix(c1, c0, ext2, FMR, s["mix2"])
                    elif j == C_FR:
                        made()
                        mix(c1, c0, ext2, FMK, s["mix2"])
                    elif j == C_FV:
                        made()
                        read(C_FR)
                        dve.scalar_tensor_tensor(out=tm(c0), in0=tm(c0), scalar=1.0, in1=dt_[:, :, :],
                                                 op0=ALU.add, op1=ALU.mult).then_inc(fr, 1)
                        read(j)
                        dve.scalar_tensor_tensor(out=xr[:, :], in0=c0[:, :], scalar=0.5, in1=xr[:, :],
                                                 op0=ALU.mult, op1=ALU.add).then_inc(s["x_new"], 1)
                    elif j == F_XT:
                        read(j)
                        shift(ext, sx, s["shifted1"])
                        dve.wait_ge(s["shifted1"], up_to(st.nf, 1, 1))
                        mix(m0, sx, ext, MAAX, s["mix0"])
                    elif j in MIXES:
                        f, turn, last = MIXES[j]
                        made()
                        if turn >= 2:
                            dve.wait_ge(s["dense"], st.job(last))
                        for c in range(NC):
                            m = dve.scalar_tensor_tensor(out=cm((m0, m1)[turn % 2])[:, c, :], in0=dc[:, c, :],
                                                         scalar=par[:, MAAK + f, c:c + 1], in1=cm(sx)[:, c, :],
                                                         op0=ALU.add, op1=ALU.mult).then_inc(s["shift_mixed"], 1)
                        dve.wait_ge(s["shift_mixed"], up_to(st.na, 20, 4 * turn + 4))
                        dve.nop().then_inc(fr, 1)
                    elif j == A_PG:
                        dve.wait_ge(s["g_tanh"], up_to(st.na, 1, 1))
                        dve.scalar_tensor_tensor(out=gT[1 - q][:, :, :], in0=cm(a0), scalar=1.0, in1=dc,
                                                 op0=ALU.add, op1=ALU.mult).then_inc(fr, 1)
                        read(j)
                        read(A_PR)
                        read(A_PK)
                        for c in range(NC):
                            dve.scalar_tensor_tensor(out=cm(a0)[:, c, :], in0=rT[1 - q][:, c, :],
                                                     scalar=par[:, BONUS, c:c + 1], in1=kT[1 - q][:, c, :],
                                                     op0=ALU.mult, op1=ALU.mult).then_inc(s["ruk"], 1)
                    elif j == A_CF:
                        made()
                        dve.tensor_copy(coef, dt_[:, 0, 0:TT * NC * HT]).then_inc(fr, 1)
                    elif j == A_VT:
                        made()
                        read(A_CF)
                        dve.tensor_tensor(uv[1 - q][:, :, :].rearrange("p s (h j) -> p (s h) j", j=S),
                                          dt_[:, :, :].rearrange("p s (h j) -> p (s h) j", j=S),
                                          coef.unsqueeze(2).broadcast_to([P, TT * NC * HT, S]), ALU.mult).then_inc(fr, 1)

                def wkv(st, g):
                    c = g // 4
                    k_ = kT[st.parity][:, c:c + 1, 0:T - 1].broadcast_to([P, 2, T - 1])
                    if g >= 1:
                        dve.wait_ge(s["scanned"], up_to(st.nb, NG, g))
                    for half in range(2):
                        dve.wait_ge(s["spread"], up_to(st.nb, 2 * NG, 2 * g + half + 1))
                        dve.tensor_tensor(drive[:, 2 * half:2 * half + 2, 1:T],
                                          V[half][:, :].rearrange("p (i t) -> p i t", i=2)[:, :, 0:T - 1], k_,
                                          ALU.mult).then_inc(s["kv"], 1)
                    dve.wait_ge(s["kv"], up_to(st.nb, 2 * NG, 2 * g + 2))
                    dve.wait_ge(s["s0_in"], up_to(st.nb, NG, g + 1))
                    dve.wait_ge(s["wrep"], up_to(st.nb, NC, c + 1))
                    if g >= 2:
                        dve.wait_ge(s["reduced"], up_to(st.nb, NG, g - 1))
                    dve.tensor_tensor_scan(state[g % 2][:, :, :].rearrange("p j t -> p (j t)"),
                                           wrep[:, :, :].rearrange("p j t -> p (j t)"),
                                           drive[:, :, :].rearrange("p j t -> p (j t)"),
                                           0.0, ALU.mult, ALU.add).then_inc(s["scanned"], 1)
                    if g not in ON_POOL:
                        dve.wait_ge(s["scanned"], up_to(st.nb, NG, g + 1))
                        dve.tensor_tensor(state[g % 2][:, :, :], state[g % 2][:, :, :],
                                          rT[st.parity][:, c:c + 1, :].broadcast_to([P, 4, T]),
                                          ALU.mult).then_inc(s["rs"], 1)

                def body(st):
                    for g in range(NG):
                        if st.wkv:
                            wkv(st, g)
                        if st.behind and g == 1:
                            dve.wait_ge(s["squared"], up_to(st.nc, 1, 1))
                            dve.tensor_reduce(hvar, oP[:, :, :].rearrange("p c (h j) -> p (c h) j", j=S), AX, ALU.add)\
                               .then_inc(s["hvar"], 1)
                            dve.wait_ge(s["hvar"], up_to(st.nc, 1, 1))
                            dve.tensor_scalar(hve, hvar, 1.0 / S, EPS, ALU.mult, ALU.add).then_inc(s["hve"], 1)
                            dve.wait_ge(s["hve"], up_to(st.nc, 1, 1))
                            inverse_root(s["hrs"], st.nc, hve, hvar, hrs)
                        if st.first and C_FK in SLOTS[g]:
                            dve.wait_ge(s["x_loaded"], up_to(st.nf, 16, 16))
                            moments(tm(a0), st.nf, "1")
                        if st.first and F_XT in SLOTS[g]:
                            if st.ahead:
                                dve.wait_ge(s["dense"], st.job(A_PV))
                            normalise(tm(a0), tm(m0), st.nf, "1")
                        for j in SLOTS[g]:
                            if in_step(st.first_t, j):
                                dense(st, j)
                    if st.wkv:
                        dve.wait_ge(s["rs"], rs_value(st, NG - 1))
                    if st.ahead:
                        dve.wait_ge(s[f"free{A_VT % 2}"], st.read(A_VT))
                    if st.first:
                        dve.wait_ge(s["mix0"], up_to(st.nf, 4, 4))
                    if st.behind:
                        dve.wait_ge(s["x_new"], up_to(st.nc, 1, 1))
                    step_end(dve, st)

                pipeline(dve, layer, body)


def rs_value(st, g):
    if g in ON_POOL:
        return up_to(st.nb, len(ON_POOL), ON_POOL.index(g) + 1)
    mine = [i for i in range(NG) if i not in ON_POOL]
    return up_to(st.nb, len(mine), mine.index(g) + 1)


NH = 16
DH = 32
KEYS = 2 * T
KT = KEYS // P
F = 2048
NF = F // P
RMS_EPS = 1e-6
MASKED = -3e38
QB, KB, VB, PW, B1 = 0, NC, 2 * NC, 3 * NC, 4 * NC
L_Q, L_KX, L_VX, L_P = 0, 1, 2, 3
L_CT, L_RT, L_KC, L_RB, L_KC2, L_OUT, L_VC, L_VC2, L_NT, L_XT = range(L_P + NH, L_P + NH + 10)
L_H = L_XT + 1
L_M2 = L_H + 4
NJ_L = L_M2 + 1
L_NEXT = (L_CT, L_KC, L_KC2, L_VC, L_VC2, L_XT)


def in_latent(n, j):
    if not isinstance(n, int):
        return True
    return n + 1 < B if j in L_NEXT else n >= 0


def latent_jobs(n, j, buffers):
    before = sum(i % 2 in buffers for i in L_NEXT) if not isinstance(n, int) or n >= 0 else 0
    per = NJ_L // 2 * len(buffers)
    own = sum(in_latent(n, i) for i in range(j) if i % 2 in buffers)
    return (n * per if not isinstance(n, int) or n >= 0 else 0) + (before + own)


def latent_layer(nc, k, s, w, ctx_dram, mask, x_src, x_dst):
    ident, nhalf = k["ident"], k["nhalf"]
    with ExitStack() as ctx:
        def sb(name, shape, dt=F32):
            return ctx.enter_context(nc.sbuf_tensor("l_" + name, shape, dt))

        wq, wk, wv, wo = (sb(n, [P, NC, E]) for n in ("wq", "wk", "wv", "wo"))
        w1 = sb("w1", [P, NC, F])
        w2 = sb("w2", [P, NF, E])
        par = sb("par", [P, 4 * NC + NF])
        out_b = sb("out_b", [P, E])
        b2 = sb("b2", [P, E])
        expand = sb("expand", [NH, E])
        ctok = sb("ctok", [P, TT, E])
        xtok = sb("xtok", [P, TT, E])
        xnew = sb("xnew", [P, TT, E])
        maskb = sb("maskb", [P, KEYS])
        maski = maskb[:, 0:T].bitcast(I32)
        hT = sb("hT", [P, NC, KEYS])
        qz = sb("qz", [P, NC, 4, T])
        kT = sb("kT", [P, NC, KEYS])
        v = sb("v", [P, KT, E])
        probs = [[sb(f"probs{i}{j}", [P, KEYS]) for j in range(TT)] for i in range(2)]
        ring = sb("ring", [P, 8, KT, T])
        small = sb("small", [P, 80])
        top = small[:, 0:2 * TT]
        neg = small[:, 4:4 + 2 * TT]
        squares, meane, rstd = (small[:, o:o + TT] for o in (8, 10, 12))
        total = small[:, 16:16 + TT * NH]
        inv = small[:, 48:48 + TT * NH]
        invT = probs[0][0][0:NH, 0:T]
        D, V, O = k["D"], k["V"], k["O"]
        dcm = [d[:, :, :].rearrange("p b (c t) -> p (b c) t", t=T) for d in D]
        hidden = ring[:, 0:4, :, :].rearrange("p a c t -> p (a c) t")
        cT, xT = hT[:, :, 0:T], hT[:, :, T:KEYS]
        aT = xT
        attended = ring[:, 4, :, :].rearrange("p c t -> p (c t)").rearrange("p (s e) -> p s e", s=TT)
        xb = scratch = ring[:, 5, :, :].rearrange("p c t -> p (c t)").rearrange("p (s e) -> p s e", s=TT)
        xn = ring[:, 6, :, :].rearrange("p c t -> p (c t)").rearrange("p (s e) -> p s e", s=TT)
        xnT = ring[:, 7, :, :]
        cs = ctx_dram.rearrange("b (s p) e -> b p s e", p=P)
        xs = x_src.rearrange("b (s p) e -> b p s e", p=P)
        xd = x_dst.rearrange("b (s p) e -> b p s e", p=P)

        def made_value(n, j):
            return latent_jobs(n, j, (0, 1)) + 1

        def fills_before(n, j):
            return latent_jobs(n, j, (j % 2,))

        def batches(eng, body):
            body(-1)
            with eng.Fori(0, B - 1) as n:
                body(n)
            body(B - 1)

        def batch_end(eng, n):
            eng.nop().then_inc(s["l_batch_done"], 1)
            wait_apart(eng, s, s["l_batch_done"], up_to(n, 5, 5))

        with nc.Block() as block:

            @block.sync
            def _(sp):
                for dst, name in ((wk, "wk"), (wv, "wv"), (wq, "wq")):
                    sp.dma_start(dst[:, :, :], w[name].rearrange("(c p) n -> p c n", p=P)).then_inc(s["l_weights"], 16)
                sp.dma_start(par[:, :], w["par"]).then_inc(s["l_weights"], 16)
                sp.dma_start(out_b[:, :], w["out_b"].partition_broadcast(P)).then_inc(s["l_weights"], 16)
                sp.dma_start(b2[:, :], w["b2"].partition_broadcast(P)).then_inc(s["l_weights"], 16)
                sp.dma_start(ctok[:, :, :], cs[0]).then_inc(s["l_ctx"], 16)
                sp.dma_start(xtok[:, :, :], xs[0]).then_inc(s["l_x"], 16)
                sp.dma_start(maski, mask[0].partition_broadcast(P)).then_inc(s["l_mask"], 16)
                sp.dma_start(wo[:, :, :], w["wo"].rearrange("(c p) n -> p c n", p=P)).then_inc(s["l_late_weights"], 16)
                sp.dma_start(expand[:, :], w["expand"]).then_inc(s["l_late_weights"], 16)
                for dst, name in ((w1, "w1"), (w2, "w2")):
                    sp.dma_start(dst[:, :, :], w[name].rearrange("(c p) n -> p c n", p=P)).then_inc(s["l_late_weights"], 16)

                def batch(n):
                    if in_latent(n, L_CT):
                        wait_apart(sp, s, s["l_dense"], latent_jobs(n, L_Q, (0, 1)))
                        wait_apart(sp, s, s["l_ctx"], up_to(n, 16, 16))
                        sp.dma_start(ctok[:, :, :], cs[n + 1]).then_inc(s["l_ctx"], 16)
                        wait_apart(sp, s, s["l_masked"], up_to(n, TT * NH, TT * NH))
                        wait_apart(sp, s, s["l_mask"], up_to(n, 16, 16))
                        sp.dma_start(maski, mask[n + 1].partition_broadcast(P)).then_inc(s["l_mask"], 16)
                        wait_apart(sp, s, s["l_biased"], up_to(n, 1, 1))
                        wait_apart(sp, s, s["l_x"], up_to(n, 16, 16))
                        sp.dma_start(xtok[:, :, :], xs[n + 1]).then_inc(s["l_x"], 16)
                    batch_end(sp, n)
                    wait_apart(sp, s, s["l_new"], up_to(n, 1, 1))
                    sp.dma_start(xd[n], xnew[:, :, :]).then_inc(s["l_stored"], 16)

                with sp.Fori(0, B - 1) as n:
                    batch(n)
                batch(B - 1)
                sp.wait_ge(s["l_stored"], up_to(B - 1, 16, 16))

            @block.tensor
            def _(pe):
                pe.wait_ge(s["l_weights"], 16 * 6)
                pe.wait_ge(s["l_zeros"], 2)

                def batch(n):
                    def free(j):
                        wait(pe, s[f"l_free{j % 2}"], fills_before(n, j))
                        return D[j % 2], dcm[j % 2]

                    def evacuated(j):
                        pe.wait_ge(s[f"l_free{j % 2}"], fills_before(n, j) + 1)

                    def done(m):
                        m.then_inc(s["l_dense"], 1)

                    def transposes_cm(dst, src):
                        for c in range(NC):
                            for tt in range(TT):
                                m = pe.transpose(dst[:, c, tt * P:(tt + 1) * P], src[:, tt, c * P:(c + 1) * P],
                                                 ident[:, :])
                        return m

                    def product_cm(dst, wt, x, tiles):
                        for i, o in enumerate(tiles):
                            for c in range(NC):
                                m = pe.matmul(dst[:, i, :], wt[:, c, o * P:(o + 1) * P], x[:, c, :],
                                              start=(c == 0), stop=(c == NC - 1))
                        return m

                    def product_tm(dst, wt, x, n_in, tiles=range(TT)):
                        for tt in tiles:
                            for c in range(n_in):
                                m = pe.matmul(dst[:, tt, :], x[:, c, tt * P:(tt + 1) * P], wt[:, c, :],
                                              start=(c == 0), stop=(c == n_in - 1))
                        return m

                    def scores(h):
                        c, hh = h // 4, h % 4
                        if h == 0:
                            evacuated(L_Q)
                            evacuated(L_KX)
                        for tt in range(TT):
                            if h >= 1:
                                pe.wait_ge(s["l_masked"], up_to(n, TT * NH, TT * (h - 1) + tt + 1))
                            pe.matmul(V[tt][:, :], qz[:, c, hh, tt * P:(tt + 1) * P], kT[:, c, :],
                                      start=True, stop=True).then_inc(s["l_scores"], 1)

                    def turn(h):
                        pe.wait_ge(s["l_exp"], up_to(n, TT * NH, TT * (h + 1)))
                        _, dc = free(L_P + h)
                        for kt in range(KT):
                            for tt in range(TT):
                                m = pe.transpose(dc[:, kt, tt * P:(tt + 1) * P],
                                                 probs[h % 2][tt][:, kt * P:(kt + 1) * P], ident[:, :])
                        done(m)

                    def values(c):
                        if c == 0:
                            evacuated(L_VX)
                        evacuated(L_P + 4 * c + 2)
                        evacuated(L_P + 4 * c + 3)
                        if c >= 2:
                            pe.wait_ge(s["l_o_read"], up_to(n, NC, c - 1))
                        for kt in range(KT):
                            for hh in range(4):
                                h = 4 * c + hh
                                m = pe.matmul(O[c % 2][DH * hh:DH * hh + DH, 0:T], v[:, kt, h * DH:(h + 1) * DH],
                                              ring[:, h % 8, kt, :], start=(kt == 0), stop=(kt == KT - 1))
                        m.then_inc(s["l_values"], 1)

                    this, more = in_latent(n, L_Q), in_latent(n, L_CT)
                    if this:
                        _, dc = free(L_Q)
                        done(product_cm(dc, wq, xT, range(NC)))
                        _, dc = free(L_KX)
                        done(product_cm(dc, wk, xT, range(NC)))
                        dt_, _ = free(L_VX)
                        done(product_tm(dt_, wv, xT, NC))
                        for h in range(NH + 2):
                            if h < NH:
                                scores(h)
                            if 1 <= h <= NH:
                                turn(h - 1)
                            if h >= 5 and (h - 5) % 4 == 0:
                                values((h - 5) // 4)
                    if more:
                        pe.wait_ge(s["l_ctx"], up_to(n + 1, 16, 16))
                        _, dc = free(L_CT)
                        done(transposes_cm(dc, ctok))
                    if this:
                        dt_, _ = free(L_RT)
                        pe.wait_ge(s["l_inv"], up_to(n, 1, 1))
                        for tt in range(TT):
                            m = pe.transpose(dt_[0:NH, 0, tt * P:(tt + 1) * P], inv[:, tt * NH:(tt + 1) * NH], ident[:, :])
                        done(m)
                    if more:
                        evacuated(L_CT)
                        _, dc = free(L_KC)
                        done(product_cm(dc, wk, cT, (0, 1)))
                    if this:
                        pe.wait_ge(s["l_late_weights"], 16 * 4)
                        evacuated(L_RT)
                        _, dc = free(L_RB)
                        for c in range(NC):
                            m = pe.matmul(dc[:, c, :], expand[:, c * P:(c + 1) * P], invT, start=True, stop=True)
                        done(m)
                    if more:
                        _, dc = free(L_KC2)
                        done(product_cm(dc, wk, cT, (2, 3)))
                    if this:
                        dt_, _ = free(L_OUT)
                        pe.wait_ge(s["l_attended"], up_to(n, NC, NC))
                        done(product_tm(dt_, wo, aT, NC))
                    if more:
                        for tt, j in enumerate((L_VC, L_VC2)):
                            dt_, _ = free(j)
                            done(product_tm(dt_, wv, cT, NC, (tt,)))
                    if this:
                        _, dc = free(L_NT)
                        pe.wait_ge(s["l_normed"], up_to(n, 2, 2))
                        done(transposes_cm(dc, xn))
                    if more:
                        pe.wait_ge(s["l_x"], up_to(n + 1, 16, 16))
                        _, dc = free(L_XT)
                        done(transposes_cm(dc, xtok))
                    if this:
                        evacuated(L_NT)
                        for part in range(4):
                            _, dc = free(L_H + part)
                            done(product_cm(dc, w1, xnT, range(4 * part, 4 * part + 4)))
                        dt_, _ = free(L_M2)
                        evacuated(L_H + 2)
                        evacuated(L_H + 3)
                        done(product_tm(dt_, w2, hidden, NF))
                        pe.wait_ge(s["l_dense"], made_value(n, L_M2))
                        batch_end(pe, n)
                    else:
                        evacuated(L_XT)

                batches(pe, batch)

            @block.scalar
            def _(act):
                act.wait_ge(s["l_weights"], 16 * 6)

                def batch(n):
                    def made(j):
                        act.wait_ge(s["l_dense"], made_value(n, j))
                        return D[j % 2], dcm[j % 2]

                    def done(m, j):
                        m.then_inc(s[f"l_free{j % 2}"], 1)

                    def keys(j, src, dst, tiles):
                        for i, o in enumerate(tiles):
                            m = act.activation(dst[:, o, :], src[:, i, :], ACT.Identity, bias=par[:, KB + o:KB + o + 1])
                        done(m, j)

                    def exps(h):
                        act.wait_ge(s["l_neg"], up_to(n, NH, h + 1))
                        for tt in range(TT):
                            p_ = probs[h % 2][tt]
                            act.activation(p_[:, :], p_[:, :], ACT.Exp, bias=neg[:, TT * (h % 2) + tt:TT * (h % 2) + tt + 1],
                                           scale=1.0 / DH, accum_out=total[:, tt * NH + h:tt * NH + h + 1])\
                               .then_inc(s["l_exp"], 1)

                    def evacuate(h):
                        _, dc = made(L_P + h)
                        if h >= 8:
                            act.wait_ge(s["l_values"], up_to(n, NC, h // 4 - 1))
                        done(act.activation(ring[:, h % 8, :, :], dc, ACT.Copy), L_P + h)

                    def read_o(c):
                        act.wait_ge(s["l_values"], up_to(n, NC, c + 1))
                        act.activation(aT[:, c, :], O[c % 2][:, 0:T], ACT.Copy).then_inc(s["l_o_read"], 1)

                    this, more = in_latent(n, L_Q), in_latent(n, L_CT)
                    if this:
                        _, dc = made(L_KX)
                        keys(L_KX, dc, kT[:, :, T:KEYS], range(NC))
                        dt_, _ = made(L_VX)
                        done(act.activation(v[:, TT:KT, :], dt_[:, :, :], ACT.Copy), L_VX)
                        for h in range(NH + 2):
                            if h < NH:
                                exps(h)
                            if 1 <= h <= NH and (h - 1) % 2 == 0:
                                evacuate(h - 1)
                            if h >= 6 and (h - 6) % 4 == 0:
                                read_o((h - 6) // 4)
                        read_o(NC - 1)
                    if more:
                        _, dc = made(L_CT)
                        done(act.activation(cT, dc, ACT.Copy), L_CT)
                    if this:
                        dt_, _ = made(L_RT)
                        done(act.activation(invT, dt_[0:NH, 0, 0:T], ACT.Copy), L_RT)
                    if more:
                        _, dc = made(L_KC)
                        keys(L_KC, dc, kT[:, :, 0:T], (0, 1))
                    if this:
                        act.wait_ge(s["l_scaled"], up_to(n, 1, 1))
                        for c in range(NC):
                            act.activation(aT[:, c, :], aT[:, c, :], ACT.Identity, bias=par[:, VB + c:VB + c + 1])\
                               .then_inc(s["l_attended"], 1)
                    if more:
                        _, dc = made(L_KC2)
                        keys(L_KC2, dc, kT[:, :, 0:T], (2, 3))
                    if this:
                        act.wait_ge(s["l_residual"], up_to(n, 1, 1))
                        for tt in range(TT):
                            act.activation(scratch[:, tt, :], attended[:, tt, :], ACT.Square,
                                           accum_out=squares[:, tt:tt + 1]).then_inc(s["l_squares"], 1)
                    if more:
                        for tt, j in enumerate((L_VC, L_VC2)):
                            dt_, _ = made(j)
                            done(act.activation(v[:, tt, :], dt_[:, tt, :], ACT.Copy), j)
                    if this:
                        _, dc = made(L_NT)
                        for c in range(NC):
                            m = act.activation(xnT[:, c, :], dc[:, c, :], ACT.Copy, scale=par[:, PW + c:PW + c + 1])
                        done(m, L_NT)
                        for part in range(4):
                            _, dc = made(L_H + part)
                            for i in range(4):
                                o = 4 * part + i
                                m = act.activation(hidden[:, o, :], dc[:, i, :], ACT.Gelu_apprx_tanh,
                                                   bias=par[:, B1 + o:B1 + o + 1])
                            done(m, L_H + part)
                        act.wait_ge(s[f"l_free{(L_H + 3) % 2}"], fills_before(n, L_H + 3) + 1)
                        batch_end(act, n)

                batches(act, batch)

            @block.gpsimd
            def _(pool):
                pool.memset(qz[:, :, :, :], 0.0).then_inc(s["l_zeros"], 1)
                pool.memset(maskb[:, T:KEYS], 0.0).then_inc(s["l_zeros"], 1)
                pool.wait_ge(s["l_weights"], 16 * 6)

                def batch(n, first):
                    if not first:
                        wait_apart(pool, s, s["l_stored"], up_to(n - 1, 16, 16))
                    pool.wait_ge(s["l_x"], up_to(n, 16, 16))
                    for tt in range(TT):
                        pool.tensor_tensor(xnew[:, tt, :], xtok[:, tt, :], b2[:, :], ALU.add).then_inc(s["l_xnew"], 1)
                    pool.wait_ge(s["l_values"], up_to(n, NC, NC))
                    for tt in range(TT):
                        pool.tensor_tensor(xb[:, tt, :], xtok[:, tt, :], out_b[:, :], ALU.add).then_inc(s["l_xb"], 1)
                    pool.wait_ge(s["l_xnew"], up_to(n, TT, TT))
                    pool.wait_ge(s["l_xb"], up_to(n, TT, TT))
                    pool.nop().then_inc(s["l_biased"], 1)
                    wait_apart(pool, s, s["l_squares"], up_to(n, 2, 2))
                    pool.tensor_scalar(meane, squares, 1.0 / E, RMS_EPS, ALU.mult, ALU.add).then_inc(s["l_rstd"], 1)
                    pool.wait_ge(s["l_rstd"], up_to(n, 2, 1))
                    pool.tensor_tensor(rstd, meane, nhalf[:, :], ALU.pow).then_inc(s["l_rstd"], 1)
                    pool.wait_ge(s["l_rstd"], up_to(n, 2, 2))
                    batch_end(pool, n)

                batch(0, True)
                with pool.Fori(1, B) as n:
                    batch(n, False)

            @block.vector
            def _(dve):
                dve.wait_ge(s["l_weights"], 16 * 6)
                dve.wait_ge(s["l_zeros"], 2)

                def batch(n):
                    def made(j):
                        dve.wait_ge(s["l_dense"], made_value(n, j))
                        return D[j % 2], dcm[j % 2]

                    def done(m, j):
                        m.then_inc(s[f"l_free{j % 2}"], 1)

                    def mask_and_max(h):
                        if h >= 2:
                            dve.wait_ge(s["l_dense"], made_value(n, L_P + h - 2))
                        for tt in range(TT):
                            wait_apart(dve, s, s["l_scores"], up_to(n, TT * NH, TT * h + tt + 1))
                            dve.tensor_tensor_reduce(probs[h % 2][tt][:, :], V[tt][:, :], maskb[:, :], 1.0, MASKED,
                                                     ALU.add, ALU.max, top[:, TT * (h % 2) + tt:TT * (h % 2) + tt + 1])\
                               .then_inc(s["l_masked"], 1)
                        dve.wait_ge(s["l_masked"], up_to(n, TT * NH, TT * h + TT))
                        at = slice(TT * (h % 2), TT * (h % 2) + TT)
                        dve.tensor_scalar(neg[:, at], top[:, at], -1.0 / DH, None, ALU.mult).then_inc(s["l_neg"], 1)

                    def evacuate(h):
                        _, dc = made(L_P + h)
                        if h >= 8:
                            dve.wait_ge(s["l_values"], up_to(n, NC, h // 4 - 1))
                        done(dve.tensor_copy(ring[:, h % 8, :, :], dc), L_P + h)

                    this, more = in_latent(n, L_Q), in_latent(n, L_CT)
                    if this:
                        dve.wait_ge(s["l_mask"], up_to(n, 16, 16))
                        dve.tensor_scalar(maskb[:, 0:T], maski, 0.0, MASKED, ALU.is_equal, ALU.mult)\
                           .then_inc(s["l_bias"], 1)
                        _, dc = made(L_Q)
                        for hh in range(4):
                            r = slice(DH * hh, DH * hh + DH)
                            m = dve.tensor_tensor(qz[r, :, hh, :], dc[r, :, :],
                                                  par[r, QB:QB + NC].unsqueeze(2).broadcast_to([DH, NC, T]), ALU.add)
                        done(m, L_Q)
                        dve.wait_ge(s["l_bias"], up_to(n, 1, 1))
                        for h in range(NH + 2):
                            if h < NH:
                                mask_and_max(h)
                            if 1 <= h <= NH and (h - 1) % 2 == 1:
                                evacuate(h - 1)
                        dve.wait_ge(s["l_exp"], up_to(n, TT * NH, TT * NH))
                        dve.reciprocal(inv, total).then_inc(s["l_inv"], 1)
                        _, dc = made(L_RB)
                        dve.wait_ge(s["l_o_read"], up_to(n, NC, NC))
                        m = dve.tensor_tensor(aT[:, :, :], aT[:, :, :], dc, ALU.mult)
                        done(m, L_RB)
                        dve.wait_ge(s[f"l_free{L_RB % 2}"], fills_before(n, L_RB) + 1)
                        dve.nop().then_inc(s["l_scaled"], 1)
                        dt_, _ = made(L_OUT)
                        dve.wait_ge(s["l_biased"], up_to(n, 1, 1))
                        done(dve.tensor_tensor(attended, xb[:, :, :], dt_[:, :, :], ALU.add), L_OUT)
                        dve.wait_ge(s[f"l_free{L_OUT % 2}"], fills_before(n, L_OUT) + 1)
                        dve.nop().then_inc(s["l_residual"], 1)
                        dve.wait_ge(s["l_rstd"], up_to(n, 2, 2))
                        for tt in range(TT):
                            dve.tensor_scalar(xn[:, tt, :], attended[:, tt, :], rstd[:, tt:tt + 1], None, ALU.mult)\
                               .then_inc(s["l_normed"], 1)
                    if more:
                        _, dc = made(L_XT)
                        done(dve.tensor_copy(xT, dc), L_XT)
                    if this:
                        dt_, _ = made(L_M2)
                        done(dve.tensor_tensor(xnew[:, :, :], xnew[:, :, :], dt_[:, :, :], ALU.add), L_M2)
                        dve.wait_ge(s[f"l_free{L_M2 % 2}"], fills_before(n, L_M2) + 1)
                        dve.nop().then_inc(s["l_new"], 1)
                        batch_end(dve, n)

                batches(dve, batch)


X_CT, X_XT, X_K, X_V, X_S, X_PT, X_O = range(7)


def cross_layer(nc, k, s, w, ctx_dram, x_src, out):
    ident = k["ident"]
    scale = float(E) ** -0.5
    with ExitStack() as ctx:
        def sb(name, shape, dt=F32):
            return ctx.enter_context(nc.sbuf_tensor("x_" + name, shape, dt))

        wq, wk, wv, wo = (sb(n, [P, NC, E]) for n in ("wq", "wk", "wv", "wo"))
        wkq = sb("wkq", [P, NC, E])
        wvo = sb("wvo", [P, NC, E])
        alpha = sb("alpha", [P, 1])
        ctok = sb("ctok", [P, TT, E])
        xtok = sb("xtok", [P, TT, E])
        cT = sb("cT", [P, NC, T])
        xT = sb("xT", [P, NC, T])
        kT = sb("kT", [P, NC, T])
        v = sb("v", [P, TT, E])
        probs = sb("probs", [P, TT, T])
        pT = sb("pT", [P, TT, T])
        y = sb("y", [P, TT, E])
        small = sb("small", [P, 32])
        top, neg, total, inv, gain = (small[:, 4 * i:4 * i + TT] for i in range(5))
        D = k["D"]
        dcm = [d[:, :, :].rearrange("p b (c t) -> p (b c) t", t=T) for d in D]
        cs = ctx_dram.rearrange("b (s p) e -> b p s e", p=P)
        xs = x_src.rearrange("b (s p) e -> b p s e", p=P)
        yd = out.rearrange("b (s p) e -> b p s e", p=P)

        def made_value(n, j):
            return up_to(n, 7, j + 1 + 4)

        def fills_before(n, j):
            return up_to(n, 4 - j % 2, j // 2 + 2)

        def batch_end(eng, n):
            eng.nop().then_inc(s["x_batch_done"], 1)
            wait_apart(eng, s, s["x_batch_done"], up_to(n, 4, 4))

        with nc.Block() as block:

            @block.sync
            def _(sp):
                for dst, name in ((wq, "wq"), (wk, "wk"), (wv, "wv"), (wo, "wo")):
                    sp.dma_start(dst[:, :, :], w[name].rearrange("(c p) n -> p c n", p=P)).then_inc(s["x_weights"], 16)
                sp.dma_start(alpha[:, :], w["alpha"].partition_broadcast(P)).then_inc(s["x_weights"], 16)
                with sp.Fori(0, B) as n:
                    sp.dma_start(ctok[:, :, :], cs[n]).then_inc(s["x_ctx"], 16)
                    sp.dma_start(xtok[:, :, :], xs[n]).then_inc(s["x_x"], 16)
                    wait_apart(sp, s, s["x_y"], up_to(n, 2, 2))
                    sp.dma_start(yd[n], y[:, :, :]).then_inc(s["x_out"], 16)
                    sp.wait_ge(s["x_out"], up_to(n, 16, 16))
                    batch_end(sp, n)

            @block.tensor
            def _(pe):
                pe.wait_ge(s["x_weights"], 16 * 5)
                for i, (a, b_) in enumerate(((wk, wq), (wv, wo))):
                    for half in range(2):
                        if i:
                            pe.wait_ge(s[f"x_free{half}"], i)
                        for r in range(2):
                            o = 2 * half + r
                            for c in range(NC):
                                m = pe.matmul(D[half][:, r, :], a[:, c, o * P:(o + 1) * P], b_[:, c, :],
                                              start=(c == 0), stop=(c == NC - 1))
                        m.then_inc(s["x_dense"], 1)
                pe.wait_ge(s["x_free0"], 2)
                pe.wait_ge(s["x_free1"], 2)

                def batch(n):
                    def free(j):
                        pe.wait_ge(s[f"x_free{j % 2}"], fills_before(n, j))
                        return D[j % 2], dcm[j % 2]

                    def evacuated(j):
                        pe.wait_ge(s[f"x_free{j % 2}"], fills_before(n, j) + 1)

                    def done(m):
                        m.then_inc(s["x_dense"], 1)

                    for j, src, loaded in ((X_CT, ctok, "x_ctx"), (X_XT, xtok, "x_x")):
                        pe.wait_ge(s[loaded], up_to(n, 16, 16))
                        _, dc = free(j)
                        for c in range(NC):
                            for tt in range(TT):
                                m = pe.transpose(dc[:, c, tt * P:(tt + 1) * P], src[:, tt, c * P:(c + 1) * P],
                                                 ident[:, :])
                        done(m)
                    _, dc = free(X_K)
                    for o in range(NC):
                        for c in range(NC):
                            m = pe.matmul(dc[:, o, :], wkq[:, c, o * P:(o + 1) * P], cT[:, c, :],
                                          start=(c == 0), stop=(c == NC - 1))
                    done(m)
                    dt_, _ = free(X_V)
                    for tt in range(TT):
                        for c in range(NC):
                            m = pe.matmul(dt_[:, tt, :], cT[:, c, tt * P:(tt + 1) * P], wvo[:, c, :],
                                          start=(c == 0), stop=(c == NC - 1))
                    done(m)
                    evacuated(X_K)
                    dt_, _ = free(X_S)
                    for tt in range(TT):
                        for c in range(NC):
                            m = pe.matmul(dt_[:, tt, 0:T], xT[:, c, tt * P:(tt + 1) * P], kT[:, c, :],
                                          start=(c == 0), stop=(c == NC - 1))
                    done(m)
                    evacuated(X_S)
                    _, dc = free(X_PT)
                    for kt in range(TT):
                        for tt in range(TT):
                            m = pe.transpose(dc[:, kt, tt * P:(tt + 1) * P], probs[:, tt, kt * P:(kt + 1) * P],
                                             ident[:, :])
                    done(m)
                    evacuated(X_PT)
                    dt_, _ = free(X_O)
                    for tt in range(TT):
                        for kt in range(TT):
                            m = pe.matmul(dt_[:, tt, :], pT[:, kt, tt * P:(tt + 1) * P], v[:, kt, :],
                                          start=(kt == 0), stop=(kt == TT - 1))
                    done(m)

                with pe.Fori(0, B) as n:
                    batch(n)
                    pe.wait_ge(s["x_dense"], made_value(n, X_O))
                    batch_end(pe, n)

            @block.scalar
            def _(act):
                for i, dst in enumerate((wkq, wvo)):
                    for half in range(2):
                        act.wait_ge(s["x_dense"], 2 * i + half + 1)
                        act.activation(dst[:, 2 * half:2 * half + 2, :], D[half][:, :, :], ACT.Copy)\
                           .then_inc(s[f"x_free{half}"], 1)

                def batch(n):
                    def made(j):
                        act.wait_ge(s["x_dense"], made_value(n, j))
                        return D[j % 2], dcm[j % 2]

                    def done(m, j):
                        m.then_inc(s[f"x_free{j % 2}"], 1)

                    _, dc = made(X_CT)
                    done(act.activation(cT[:, :, :], dc, ACT.Copy), X_CT)
                    _, dc = made(X_XT)
                    done(act.activation(xT[:, :, :], dc, ACT.Copy), X_XT)
                    _, dc = made(X_K)
                    done(act.activation(kT[:, :, :], dc, ACT.Copy), X_K)
                    act.wait_ge(s["x_neg"], up_to(n, 1, 1))
                    dt_, _ = D[X_S % 2], None
                    for tt in range(TT):
                        m = act.activation(probs[:, tt, :], dt_[:, tt, 0:T], ACT.Exp, bias=neg[:, tt:tt + 1],
                                           scale=scale, accum_out=total[:, tt:tt + 1])
                    done(m, X_S)
                    _, dc = made(X_PT)
                    done(act.activation(pT[:, :, :], dc[:, 0:TT, :], ACT.Copy), X_PT)

                with act.Fori(0, B) as n:
                    batch(n)
                    act.wait_ge(s["x_free1"], fills_before(n, X_PT) + 1)
                    batch_end(act, n)

            @block.vector
            def _(dve):
                dve.wait_ge(s["x_weights"], 16 * 5)

                def batch(n):
                    def made(j):
                        dve.wait_ge(s["x_dense"], made_value(n, j))
                        return D[j % 2], dcm[j % 2]

                    dt_, _ = made(X_V)
                    dve.tensor_copy(v[:, :, :], dt_[:, :, :]).then_inc(s["x_free1"], 1)
                    dt_, _ = made(X_S)
                    dve.tensor_reduce(top, dt_[:, :, 0:T], AX, ALU.max).then_inc(s["x_top"], 1)
                    dve.wait_ge(s["x_top"], up_to(n, 1, 1))
                    dve.tensor_scalar(neg, top, -scale, None, ALU.mult).then_inc(s["x_neg"], 1)
                    dve.wait_ge(s["x_free0"], fills_before(n, X_S) + 1)
                    dve.reciprocal(inv, total).then_inc(s["x_inv"], 1)
                    dve.wait_ge(s["x_inv"], up_to(n, 1, 1))
                    dve.tensor_scalar(gain, inv, alpha[:, 0:1], None, ALU.mult).then_inc(s["x_gain"], 1)
                    dve.wait_ge(s["x_gain"], up_to(n, 1, 1))
                    dve.wait_ge(s["x_x"], up_to(n, 16, 16))
                    dt_, _ = made(X_O)
                    for tt in range(TT):
                        m = dve.scalar_tensor_tensor(out=y[:, tt, :], in0=dt_[:, tt, :], scalar=gain[:, tt:tt + 1],
                                                     in1=xtok[:, tt, :], op0=ALU.mult, op1=ALU.add)
                        m.then_inc(s["x_y"], 1)
                    dve.wait_ge(s["x_y"], up_to(n, 2, 2))
                    dve.nop().then_inc(s["x_free0"], 1)

                with dve.Fori(0, B) as n:
                    batch(n)
                    batch_end(dve, n)


RWKV_SEMS = """weights zeros step_done dense free0 free1 spread kv s0_in wrep scanned rs rs_pool reduced o_read
x_residual x_new x_stored x_loaded centred squared hsum hvar hve hrs gn_scaled gated stats1 moments1 rstd1 normed1
stats2 moments2 rstd2 normed2 shifted1 shifted2 mix0 mix2 kk tanh1 shift_mixed mixed tanh_d decay v v_high
v_low g_tanh ruk""".split()
LATENT_SEMS = """l_batch_done l_weights l_late_weights l_xb l_xnew l_zeros l_ctx l_x l_mask l_bias l_dense l_free0 l_free1 l_scores l_masked
l_neg l_exp l_values l_o_read l_inv l_scaled l_attended l_residual l_squares l_biased l_rstd l_normed l_new
l_stored""".split()
CROSS_SEMS = """x_batch_done x_weights x_ctx x_x x_dense x_free0 x_free1 x_top x_neg x_inv x_gain x_y x_out""".split()


def four_layers(nc, t, out):
    scratch = [nc.dram_tensor(f"x_after_{i}", [B, T, E], F32, kind="Internal").ap() for i in range(3)]
    with ExitStack() as ctx:
        def sb(name, shape, dt=F32):
            return ctx.enter_context(nc.sbuf_tensor(name, shape, dt))

        s = {n: ctx.enter_context(nc.semaphore("s_" + n)) for n in ["constants", "rounded", "parted"] + RWKV_SEMS + LATENT_SEMS + CROSS_SEMS}
        k = dict(
            ident=sb("ident", [P, P]), stT=sb("stT", [P, B, 2, NC]), s0=sb("s0", [P, B, NC, S]),
            selr=sb("selr", [P, S, P], F32R), red=sb("red", [P, 4, 32]), head8=sb("head8", [P, HT]),
            nhalf=sb("nhalf", [P, TT]),
            D=[ctx.enter_context(nc.psum_tensor(f"D{i}", [P, 2, 512], F32)) for i in range(2)],
            V=[ctx.enter_context(nc.psum_tensor(f"V{i}", [P, 512], F32)) for i in range(2)],
            O=[ctx.enter_context(nc.psum_tensor(f"O{i}", [P, 512], F32)) for i in range(2)],
        )
        with nc.sbuf_tensor("sel", [P, S, P], F32) as sel, nc.Block() as block:
            @block.sync
            def _(sp):
                for dst, name in ((k["ident"], "c_ident"), (sel, "c_sel"), (k["red"], "c_red"), (k["head8"], "c_head8"),
                                  (k["stT"], "state_rows"), (k["s0"], "state_heads")):
                    sp.dma_start(dst[tuple([slice(None)] * len(dst.shape))], t[name]).then_inc(s["constants"], 16)
                sp.wait_ge(s["constants"], 16 * 6)

            @block.vector
            def _(dve):
                dve.memset(k["nhalf"][:, :], -0.5).then_inc(s["rounded"], 1)
                dve.wait_ge(s["constants"], 16 * 6)
                dve.tensor_copy(k["selr"][:, :, :], sel[:, :, :]).then_inc(s["rounded"], 1)
                dve.wait_ge(s["rounded"], 2)

        def rw(i):
            return {n: t[f"r{i}_{n}"] for n in ("w1", "w2", "td1", "td2", "Wk", "Wv", "Wr", "Wg", "Wo", "Wfr", "Wfk", "Wfv", "par")}

        rwkv_layer(nc, 0, k, s, rw(0), t["x"], scratch[0])
        latent_layer(nc, k, s, {n: t["l_" + n] for n in ("wq", "wk", "wv", "wo", "w1", "w2", "par", "expand", "out_b", "b2")},
                     t["ctx"], t["mask"], scratch[0], scratch[1])
        rwkv_layer(nc, 1, k, s, rw(1), scratch[1], scratch[2])
        cross_layer(nc, k, s, {n: t["x_" + n] for n in ("wq", "wk", "wv", "wo", "alpha")}, t["ctx"], scratch[2], out)


def laid_out(inputs):
    a = {n: np.asarray(x) for n, x in inputs.items()}
    cols = lambda v: v.reshape(-1, P).T
    head = np.arange(P) // S
    row = np.arange(P) % S
    sel = np.zeros((P, S, P), np.float32)
    for j in range(S):
        sel[:, j, :] = (head[:, None] == head[None, :]) & (row[:, None] == j)
    red = np.zeros((P, 4, 32), np.float32)
    for jg in range(4):
        red[np.arange(P), jg, HT * jg + head] = 1.0
    ctx = a["ctx_2048"]
    t = {
        "x": a["x"], "ctx": ctx, "mask": a["mask_BxS2_ik0"].reshape(B, 1, T),
        "c_ident": np.eye(P, dtype=np.float32), "c_sel": sel, "c_red": red,
        "c_head8": (head[:, None] == np.arange(HT)[None, :]).astype(np.float32),
        "state_rows": ctx[:, 0:2].reshape(B, 2, NC, P).transpose(3, 0, 1, 2),
        "state_heads": ctx[:, 2:2 + S].reshape(B, NC, P, S).transpose(2, 0, 1, 3),
    }
    for i, pre, names in ((0, "L0_xattn_", ("td_w1", "td_w2", "u", "Wfk", "Wfr", "Wfv")),
                          (1, "L2_xattn_", ("decay_w1", "decay_w2", "faaaa", "ffn_Wk", "ffn_Wr", "ffn_Wv"))):
        td1, td2, u, fk, fr, fv = (a[pre + n] for n in names)
        g = lambda n: a[pre + n]
        stack = g("maa_stack").reshape(5, E)
        vectors = [g("ln1_w"), g("ln1_b"), g("maa_x"), *stack, g("time_decay"), u.reshape(E), g("gn_w"), g("gn_b"),
                   g("ln2_w"), g("ln2_b"), g("ffn_maa_k"), g("ffn_maa_r")]
        t |= {f"r{i}_w1": g("maa_w1"), f"r{i}_w2": g("maa_w2").reshape(5 * DM, E), f"r{i}_td1": td1, f"r{i}_td2": td2,
              f"r{i}_Wk": g("Wk").T, f"r{i}_Wv": g("Wv").T, f"r{i}_Wr": g("Wr").T, f"r{i}_Wg": g("Wg").T,
              f"r{i}_Wo": g("Wo").T, f"r{i}_Wfr": fr.T, f"r{i}_Wfk": fk.T, f"r{i}_Wfv": fv.T,
              f"r{i}_par": np.stack([cols(v) for v in vectors], axis=1)}
    g = lambda n: a["L1_xattn_" + n]
    kvw, kvb = g("kv_w").reshape(E, E, 2), g("kv_b").reshape(E, 2)
    t |= {"l_wq": g("q_w"), "l_wk": kvw[:, :, 0], "l_wv": kvw[:, :, 1], "l_wo": g("out_w"), "l_w1": g("mlp_w1"),
          "l_w2": g("mlp_w2"),
          "l_par": np.concatenate([cols(v) for v in (g("q_b"), kvb[:, 0], kvb[:, 1], g("postnorm_w"), g("mlp_b1"))], axis=1),
          "l_expand": (np.arange(NH)[:, None] == np.arange(E)[None, :] // DH).astype(np.float32),
          "l_out_b": g("out_b").reshape(1, E), "l_b2": g("mlp_b2").reshape(1, E)}
    g = lambda n: a["L3_xattn_" + n]
    t |= {"x_wq": g("w_q"), "x_wk": g("w_k"), "x_wv": g("w_v"), "x_wo": g("w_o").T, "x_alpha": g("alpha").reshape(1, 1)}
    return {n: np.ascontiguousarray(x) for n, x in t.items()}


def kernel(**inputs):
    import concourse.bacc as bacc
    from concourse.bass_utils import run_bass_kernel_spmd

    nc = bacc.Bacc("TRN2", target_bir_lowering=False, num_devices=1)
    arrays = {f"in_{n}": x for n, x in laid_out(inputs).items()}
    t = {n[3:]: nc.dram_tensor(n, x.shape, mybir.dt.from_np(x.dtype), kind="ExternalInput").ap()
         for n, x in arrays.items()}
    out = nc.dram_tensor("out", [B, T, E], F32, kind="ExternalOutput").ap()
    four_layers(nc, t, out)
    r = run_bass_kernel_spmd(nc, [arrays], core_ids=[0])
    return r.results[0]["out"]
```

```python
import numpy as np
from contextlib import ExitStack

import concourse.bass as bass
from concourse import mybir

F32 = mybir.dt.float32
F32R = mybir.dt.float32r
I32 = mybir.dt.int32
ALU = mybir.AluOpType
ACT = mybir.ActivationFunctionType
AX = mybir.AxisListType.X

P = 128
E = 512
NC = E // P
B = 8
T = 256
TT = T // P
S = 16
HT = P // S
DM = 32
DD = 64
NG = 16
EPS = 1e-5

(LN1W, LN1B, MAAX, MAAK, MAAW, MAAV, MAAR, MAAG, DECAY, BONUS,
 GNW, GNB, LN2W, LN2B, FMK, FMR) = range(16)
NPAR = 16

(A_XK, C_OT, A_XW, A_PK, A_XR, A_PD1, C_GNT, A_XG, A_PD2, A_PR, C_WO, A_XV, A_PG, C_XT, A_PV,
 C_FR, A_CF, C_FK, F_XT, A_VT, C_FV, F_W1) = range(22)
NJ = 22
IN_C = (C_OT, C_GNT, C_WO, C_XT, C_FR, C_FK, C_FV)
IN_F = (F_XT, F_W1)
MIXES = {A_XK: (0, 0, F_XT), A_XW: (1, 1, F_W1), A_XR: (3, 2, A_PK), A_XG: (4, 3, A_PD1), A_XV: (2, 4, A_PR)}
SLOTS = [[A_XK, C_OT], [A_XW, A_PK], [A_XR, A_PD1], [C_GNT, A_XG], [A_PD2, A_PR], [C_WO], [A_XV, A_PG],
         [C_XT], [A_PV], [C_FR], [A_CF], [C_FK], [F_XT, A_VT], [C_FV], [F_W1], []]
ON_POOL = (0, 1, 3, 5, 6, 7, 9, 11, 12, 13, 14)
NEWTON = 3
ROOT_STEPS = 2 + 3 * NEWTON


def up_to(n, per, k):
    return n * per + k


def wait(eng, sem, value):
    if not (isinstance(value, int) and value <= 0):
        eng.wait_ge(sem, value)


def wait_apart(eng, s, sem, value):
    eng.wait_ge(sem, value)
    eng.nop().then_inc(s["parted"], 1)


def in_step(t, j):
    return 0 <= (t - 1 if j in IN_C else t + 2 if j in IN_F else t + 1) < B


class Step:

    def __init__(self, layer, t, u=None):
        tt = t if u is None else u * 2 + t
        self.first_t, self.t, self.parity = t, tt, t % 2
        self.wkv, self.behind = 0 <= t < B, in_step(t, C_OT)
        self.ahead, self.first = in_step(t, A_XK), in_step(t, F_XT)
        self.nb, self.nc = tt + B * layer, tt + (B * layer - 1)
        self.na, self.nf = tt + (B * layer + 1), tt + (B * layer + 2)
        self.steps = tt + (2 + (B + 3) * layer)
        made = [sum(in_step(i, j) for i in range(-2, t) for j in range(p, NJ, 2)) + B * layer * NJ // 2
                for p in range(2)]
        self.fills = [m if u is None else u * NJ + m for m in made]
        self.jobs = sum(made) if u is None else u * (2 * NJ) + sum(made)

    def job(self, j):
        return self.jobs + sum(in_step(self.first_t, i) for i in range(j + 1))

    def fills_before(self, j):
        return self.fills[j % 2] + sum(in_step(self.first_t, i) for i in range(j % 2, j, 2))

    def read(self, j):
        return self.fills_before(j) + 1


def pipeline(eng, layer, body):
    for t in (-2, -1, 0):
        body(Step(layer, t))
    with eng.Fori(0, 2) as u:
        body(Step(layer, 1, u))
        body(Step(layer, 2, u))
    for t in (5, 6, 7, 8):
        body(Step(layer, t))


def rwkv_layer(nc, layer, k, sems, w, x_src, x_dst):
    ident, stT, s0, selr, red, head8 = k["ident"], k["stT"], k["s0"], k["selr"], k["red"], k["head8"]
    tag = f"r{layer}_"
    with ExitStack() as ctx:
        def sb(name, shape, dt=F32):
            return ctx.enter_context(nc.sbuf_tensor(tag + name, shape, dt))

        wr, wk, wv, wg, wo = (sb(n, [P, NC, E]) for n in ("wr", "wk", "wv", "wg", "wo"))
        wfk, wfr, wfv = (sb(n, [P, NC, E]) for n in ("wfk", "wfr", "wfv"))
        w1 = sb("w1", [P, NC, 5 * DM])
        w2 = sb("w2", [P, E])
        w2g = sb("w2g", [P, E])
        td1 = sb("td1", [P, NC, DD])
        td2 = sb("td2", [P, E])
        par = sb("par", [P, NPAR, NC])

        decay = [sb(f"decay{i}", [P, NC, T + 1]) for i in range(2)]
        kT = [sb(f"kT{i}", [P, NC, T]) for i in range(2)]
        rT = [sb(f"rT{i}", [P, NC, T]) for i in range(2)]
        vhi = [sb(f"vhi{i}", [P, NC, T], F32R) for i in range(2)]
        vlo = [sb(f"vlo{i}", [P, NC, T], F32R) for i in range(2)]
        gT = [sb(f"gT{i}", [P, NC, T]) for i in range(2)]
        uv = [sb(f"uv{i}", [P, TT, E]) for i in range(2)]
        oP = sb("oP", [P, NC, T])
        wrep = sb("wrep", [P, 4, T])
        drive = sb("drive", [P, 4, T])
        state = [sb(f"state{i}", [P, 4, T]) for i in range(2)]
        a0, sx, m0, m1 = (sb(n, [P, 1024]) for n in ("a0", "sx", "m0", "m1"))
        ext = sb("ext", [P, NC, T + 1])
        c0, c1, xr = (sb(n, [P, 1024]) for n in ("c0", "c1", "xr"))
        ext2 = sb("ext2", [P, NC, T + 1])
        th = sb("th", [P, 4, T])
        thg = sb("thg", [P, T])
        td = sb("td", [P, T])
        small = sb("small", [P, 384])
        norms = {w: (small[:, o:o + 12].rearrange("p (a b) -> p a b", a=2),
                     small[:, o + 16:o + 20].rearrange("p (a b) -> p a b", a=2),
                     small[:, o + 24:o + 26], small[:, o + 28:o + 30]) for w, o in (("1", 0), ("2", 32))}
        hsum = small[:, 64:128]
        hvar = small[:, 128:192]
        hve = small[:, 192:256]
        hrs = small[:, 256:320]
        coef = small[:, 320:384]
        nhalf = k["nhalf"]

        def cm(x):
            return x[:, :].rearrange("p (c t) -> p c t", c=NC)

        def tm(x):
            return x[:, :].rearrange("p (s e) -> p s e", s=TT)

        D, V, O = k["D"], k["V"], k["O"]
        dcm = [d[:, :, :].rearrange("p b (c t) -> p (b c) t", t=T) for d in D]

        s = sems
        xs = x_src.rearrange("b (s p) e -> b p s e", p=P)
        xd = x_dst.rearrange("b (s p) e -> b p s e", p=P)

        def step_end(eng, st):
            eng.nop().then_inc(s["step_done"], 1)
            wait_apart(eng, s, s["step_done"], up_to(st.steps, 5, 5))

        def job_of(st, j):
            return D[j % 2], dcm[j % 2]

        with nc.Block() as block:

            @block.sync
            def _(sp):
                def load(sem, *pairs):
                    for dst, name in pairs:
                        sp.dma_start(dst[:, :, :], w[name].rearrange("(c p) n -> p c n", p=P)).then_inc(s[sem], 16)

                sp.dma_start(par[:, :, :], w["par"]).then_inc(s["weights"], 16)
                load("weights", (w1, "w1"))

                def load_ahead():
                    sp.dma_start(w2[:, :], w["w2"][0:P, :]).then_inc(s["weights_a"], 16)
                    sp.wait_ge(s["zeros"], up_to(layer, 7, 2))
                    sp.dma_start(w2g[0:DM, :], w["w2"][P:P + DM, :]).then_inc(s["weights_a"], 16)
                    sp.dma_start(td2[0:DD, :], w["td2"]).then_inc(s["weights_a"], 16)
                    load("weights_a", (td1, "td1"), (wk, "Wk"), (wr, "Wr"), (wg, "Wg"), (wv, "Wv"))

                def load_behind():
                    load("weights_c", (wo, "Wo"), (wfr, "Wfr"), (wfk, "Wfk"), (wfv, "Wfv"))

                def body(st):
                    if st.first_t == -1:
                        load_behind()
                    if st.behind:
                        sp.dma_start(tm(xr), xs[st.t - 1]).then_inc(s["x_residual"], 16)
                    if st.first:
                        if st.ahead:
                            wait_apart(sp, s, s["dense"], st.job(A_CF))
                        sp.dma_start(tm(a0), xs[st.t + 2]).then_inc(s["x_loaded"], 16)
                        if st.first_t == -2:
                            load_ahead()
                        wait_apart(sp, s, s["x_loaded"], up_to(st.nf, 16, 16))
                    if st.behind:
                        wait_apart(sp, s, s["x_new"], up_to(st.nc, 1, 1))
                        sp.dma_start(xd[st.t - 1], tm(xr)).then_inc(s["x_stored"], 16)
                        sp.wait_ge(s["x_stored"], up_to(st.nc, 16, 16))
                    step_end(sp, st)

                pipeline(sp, layer, body)

            @block.tensor
            def _(pe):
                pe.wait_ge(s["weights"], up_to(layer, 16 * 2, 16 * 2))
                pe.wait_ge(s["zeros"], up_to(layer, 7, 7))

                def free(st, j):
                    wait(pe, s[f"free{j % 2}"], st.fills_before(j))
                    return job_of(st, j)

                def transposes_cm(dst, src):
                    for c in range(NC):
                        for tt in range(TT):
                            m = pe.transpose(dst[:, c, tt * P:(tt + 1) * P], src[:, tt, c * P:(c + 1) * P], ident[:, :])
                    return m

                def transposes_tm(dst, src):
                    for tt in range(TT):
                        for c in range(NC):
                            m = pe.transpose(dst[:, tt, c * P:(c + 1) * P], src[:, c, tt * P:(tt + 1) * P], ident[:, :])
                    return m

                def product_cm(dst, wt, x):
                    for o in range(NC):
                        for c in range(NC):
                            m = pe.matmul(dst[:, o, :], wt[:, c, o * P:(o + 1) * P], x[:, c, :],
                                          start=(c == 0), stop=(c == NC - 1))
                    return m

                def product_tm(dst, wt, x):
                    for tt in range(TT):
                        for c in range(NC):
                            m = pe.matmul(dst[:, tt, :], x[:, c, tt * P:(tt + 1) * P], wt[:, c, :],
                                          start=(c == 0), stop=(c == NC - 1))
                    return m

                def dense(st, j):
                    dt_, dc = free(st, j)
                    q = st.parity
                    if j == C_OT:
                        m = transposes_tm(dt_, oP)
                    elif j == C_GNT:
                        pe.wait_ge(s["gn_scaled"], up_to(st.nc, 1, 1))
                        m = transposes_cm(dc, tm(c1))
                    elif j == C_WO:
                        pe.wait_ge(s["gated"], up_to(st.nc, 1, 1))
                        m = product_tm(dt_, wo, cm(c0))
                    elif j == C_XT:
                        pe.wait_ge(s["normed2"], up_to(st.nc, 2, 2))
                        m = transposes_cm(dc, tm(c1))
                    elif j == C_FR:
                        pe.wait_ge(s["mix2"], up_to(st.nc, 8, 4))
                        m = product_tm(dt_, wfr, cm(c1))
                    elif j == C_FK:
                        pe.wait_ge(s["mix2"], up_to(st.nc, 8, 8))
                        m = product_cm(dc, wfk, cm(c1))
                    elif j == C_FV:
                        pe.wait_ge(s["kk"], up_to(st.nc, 1, 1))
                        m = product_tm(dt_, wfv, cm(c1))
                    elif j == F_XT:
                        pe.wait_ge(s["normed1"], up_to(st.nf, 2, 2))
                        m = transposes_cm(dc, tm(m0))
                    elif j == F_W1:
                        pe.wait_ge(s["mix0"], up_to(st.nf, 4, 4))
                        for c in range(NC):
                            pe.matmul(dt_[:, 0, 0:T], w1[:, c, 0:P], cm(m0)[:, c, :], start=(c == 0), stop=(c == NC - 1))
                        for c in range(NC):
                            m = pe.matmul(dt_[0:DM, 0, T:2 * T], w1[:, c, P:P + DM], cm(m0)[:, c, :],
                                          start=(c == 0), stop=(c == NC - 1))
                    elif j in MIXES:
                        f = MIXES[j][0]
                        pe.wait_ge(s["tanh1"], up_to(st.na, 5, 5))
                        for o in range(NC):
                            lhs = w2 if f < 4 else w2g
                            m = pe.matmul(dc[:, o, :], lhs[:, o * P:(o + 1) * P], th[:, f, :] if f < 4 else thg[:, :],
                                          start=True, stop=True)
                    elif j in (A_PK, A_PV, A_PR, A_PG):
                        turn, wt = {A_PK: (0, wk), A_PR: (2, wr), A_PG: (3, wg), A_PV: (4, wv)}[j]
                        pe.wait_ge(s["mixed"], up_to(st.na, 5, turn + 1))
                        m = product_cm(dc, wt, cm((m0, m1)[turn % 2]))
                    elif j == A_PD1:
                        pe.wait_ge(s["mixed"], up_to(st.na, 5, 2))
                        for c in range(NC):
                            m = pe.matmul(dt_[0:DD, 0, 0:T], td1[:, c, :], cm(m1)[:, c, :], start=(c == 0), stop=(c == NC - 1))
                    elif j == A_PD2:
                        pe.wait_ge(s["tanh_d"], up_to(st.na, 1, 1))
                        for o in range(NC):
                            m = pe.matmul(dc[:, o, :], td2[:, o * P:(o + 1) * P], td[:, :], start=True, stop=True)
                    elif j == A_CF:
                        pe.wait_ge(s["ruk"], up_to(st.na, 4, 4))
                        for tt in range(TT):
                            for c in range(NC):
                                m = pe.matmul(dt_[:, 0, (tt * NC + c) * HT:(tt * NC + c + 1) * HT],
                                              cm(a0)[:, c, tt * P:(tt + 1) * P], head8[:, :], start=True, stop=True)
                    elif j == A_VT:
                        pe.wait_ge(s["v"], up_to(st.na, 1, 1))
                        m = transposes_tm(dt_, cm(m1))
                    m.then_inc(s["dense"], 1)

                def spread_v(st, g):
                    c, jg = g // 4, g % 4
                    for half in range(2):
                        n = 2 * g + half
                        if n >= 2:
                            pe.wait_ge(s["kv"], up_to(st.nb, 2 * NG, n - 1))
                        for i in range(2):
                            j = 4 * (2 * half + i) + jg
                            for part in (vhi, vlo):
                                m = pe.matmul(V[half][:, i * T:(i + 1) * T], selr[:, j, :], part[st.parity][:, c, :],
                                              start=(part is vhi), stop=(part is vlo))
                        m.then_inc(s["spread"], 1)

                def reduce_heads(st, g):
                    c, jg = g // 4, g % 4
                    if jg == 0 and c >= 2:
                        pe.wait_ge(s["o_read"], up_to(st.nb, NC, c - 1))
                    pe.wait_ge(s["rs"] if g not in ON_POOL else s["rs_pool"],
                               rs_value(st, g))
                    for q in range(4):
                        m = pe.matmul(O[c % 2][32 * q:32 * q + 32, 0:T], red[:, jg, :], state[g % 2][:, q, :],
                                      start=(jg == 0), stop=(jg == 3))
                    m.then_inc(s["reduced"], 1)

                def body(st):
                    if st.first_t == -1:
                        pe.wait_ge(s["weights_a"], up_to(layer, 16 * 8, 16 * 8))
                    if st.first_t == 1:
                        pe.wait_ge(s["weights_c"], up_to(layer, 16 * 4, 16 * 4))
                    if st.wkv:
                        spread_v(st, 0)
                    for g in range(NG):
                        if st.wkv and g >= 1:
                            spread_v(st, g)
                        for j in SLOTS[g]:
                            if in_step(st.first_t, j):
                                dense(st, j)
                        if st.wkv and g >= 1:
                            reduce_heads(st, g - 1)
                    if st.wkv:
                        reduce_heads(st, NG - 1)
                        pe.wait_ge(s["reduced"], up_to(st.nb, NG, NG))
                    pe.wait_ge(s["dense"], st.job(NJ - 1))
                    step_end(pe, st)

                pipeline(pe, layer, body)

            @block.scalar
            def _(act):
                act.wait_ge(s["weights"], up_to(layer, 16 * 2, 16 * 2))
                act.wait_ge(s["zeros"], up_to(layer, 7, 7))

                def dense(st, j):
                    dt_, dc = job_of(st, j)
                    q = st.parity

                    def made():
                        act.wait_ge(s["dense"], st.job(j))

                    fr = s[f"free{j % 2}"]
                    if j == C_OT:
                        act.wait_ge(s["centred"], up_to(st.nc, 1, 1))
                        act.activation(oP[:, :, :].rearrange("p c t -> p (c t)"), c1[:, :], ACT.Square)\
                           .then_inc(s["squared"], 1)
                    elif j == C_GNT:
                        made()
                        for c in range(NC):
                            m = act.activation(cm(c0)[:, c, :], dc[:, c, :], ACT.Identity,
                                               bias=par[:, GNB, c:c + 1], scale=par[:, GNW, c:c + 1])
                        m.then_inc(fr, 1)
                    elif j in (C_XT, F_XT):
                        dst, lw, lb, row, batch = ((ext2, LN2W, LN2B, 0, st.t - 1) if j == C_XT
                                                   else (ext, LN1W, LN1B, 1, st.t + 2))
                        made()
                        act.activation(dst[:, :, 0:1], stT[:, bass.ds(batch, 1), row, :].rearrange("p a c -> p c a"),
                                       ACT.Copy)
                        for c in range(NC):
                            m = act.activation(dst[:, c, 1:T + 1], dc[:, c, :], ACT.Identity,
                                               bias=par[:, lb, c:c + 1], scale=par[:, lw, c:c + 1])
                        m.then_inc(fr, 1)
                    elif j == C_FR:
                        made()
                        act.wait_ge(s["mix2"], up_to(st.nc, 8, 8))
                        act.activation(tm(c0), dt_[:, :, :], ACT.Tanh, scale=0.5).then_inc(fr, 1)
                    elif j == C_FK:
                        made()
                        act.activation(cm(c1), dc, ACT.Relu).then_inc(fr, 1)
                        act.wait_ge(fr, st.read(j))
                        act.activation(c1[:, :], c1[:, :], ACT.Square).then_inc(s["kk"], 1)
                    elif j == F_W1:
                        made()
                        for f in range(4):
                            act.activation(th[f * DM:(f + 1) * DM, f, :], dt_[f * DM:(f + 1) * DM, 0, 0:T],
                                           ACT.Tanh).then_inc(s["tanh1"], 1)
                        act.activation(thg[0:DM, :], dt_[0:DM, 0, T:2 * T], ACT.Tanh).then_inc(s["tanh1"], 1)
                        act.wait_ge(s["tanh1"], up_to(st.nf, 5, 5))
                        act.nop().then_inc(fr, 1)
                    elif j == A_PK:
                        made()
                        act.activation(kT[1 - q][:, :, :], dc, ACT.Copy).then_inc(fr, 1)
                    elif j == A_PR:
                        made()
                        act.activation(rT[1 - q][:, :, :], dc, ACT.Copy).then_inc(fr, 1)
                    elif j == A_PD1:
                        made()
                        act.activation(td[0:DD, :], dt_[0:DD, 0, 0:T], ACT.Tanh).then_inc(s["tanh_d"], 1)
                        act.wait_ge(s["tanh_d"], up_to(st.na, 1, 1))
                        act.nop().then_inc(fr, 1)
                    elif j == A_PD2:
                        made()
                        for c in range(NC):
                            m = act.activation(cm(a0)[:, c, :], dc[:, c, :], ACT.Exp, bias=par[:, DECAY, c:c + 1])
                        m.then_inc(fr, 1)
                        act.wait_ge(fr, st.read(j))
                        act.activation(decay[1 - q][:, :, 1:T + 1], cm(a0), ACT.Exp, scale=-1.0).then_inc(s["decay"], 1)
                    elif j == A_PV:
                        made()
                        act.activation(cm(m1), dc, ACT.Copy).then_inc(s["v"], 1)
                        act.wait_ge(s["v"], up_to(st.na, 1, 1))
                        act.nop().then_inc(fr, 1)
                        act.activation(vhi[1 - q][:, :, :], cm(m1), ACT.Copy).then_inc(s["v_high"], 1)
                    elif j == A_PG:
                        made()
                        act.wait_ge(s["decay"], up_to(st.na, 1, 1))
                        act.activation(cm(a0), dc, ACT.Tanh, scale=0.5).then_inc(s["g_tanh"], 1)

                def wkv(st, g):
                    c, jg = g // 4, g % 4
                    if jg == 0:
                        if c >= 1:
                            act.wait_ge(s["scanned"], up_to(st.nb, NG, 4 * c))
                        act.activation(wrep[:, :, :], decay[st.parity][:, c:c + 1, 0:T].broadcast_to([P, 4, T]),
                                       ACT.Copy).then_inc(s["wrep"], 1)
                    if g >= 1:
                        act.wait_ge(s["scanned"], up_to(st.nb, NG, g))
                    act.activation(drive[:, :, 0:1],
                                   s0[:, bass.ds(st.t, 1), c, jg:S:4].rearrange("p a j -> p j a"),
                                   ACT.Copy).then_inc(s["s0_in"], 1)

                def read_o(st, c):
                    act.wait_ge(s["reduced"], up_to(st.nb, NG, 4 * c + 4))
                    if st.behind and c == 0:
                        act.wait_ge(s["hvar"], up_to(st.nc, 1, 1))
                    act.activation(oP[:, c, :], O[c % 2][:, 0:T], ACT.Copy).then_inc(s["o_read"], 1)

                def body(st):
                    for g in range(NG):
                        if st.wkv:
                            wkv(st, g)
                            if g % 4 == 1 and g >= 4:
                                read_o(st, g // 4 - 1)
                        for j in SLOTS[g]:
                            if in_step(st.first_t, j):
                                dense(st, j)
                    if st.wkv:
                        read_o(st, NC - 1)
                        act.wait_ge(s["o_read"], up_to(st.nb, NC, NC))
                    if st.first:
                        act.wait_ge(s["tanh1"], up_to(st.nf, 5, 5))
                    if st.ahead:
                        act.wait_ge(s["v_high"], up_to(st.na, 1, 1))
                    if st.behind:
                        act.wait_ge(s["kk"], up_to(st.nc, 1, 1))
                    step_end(act, st)

                pipeline(act, layer, body)

            @block.gpsimd
            def _(pool):
                pool.memset(w2g[:, :], 0.0).then_inc(s["zeros"], 1)
                pool.memset(td2[:, :], 0.0).then_inc(s["zeros"], 1)
                pool.memset(th[:, :, :], 0.0).then_inc(s["zeros"], 1)
                pool.memset(thg[:, :], 0.0).then_inc(s["zeros"], 1)
                pool.memset(td[:, :], 0.0).then_inc(s["zeros"], 1)
                pool.memset(decay[0][:, :, 0:1], 0.0).then_inc(s["zeros"], 1)
                pool.memset(decay[1][:, :, 0:1], 0.0).then_inc(s["zeros"], 1)

                def inverse_root(ssem, var, tmp, out, n, scale):
                    pool.tensor_scalar(tmp, var, scale, EPS, ALU.mult, ALU.add).then_inc(ssem, 1)
                    pool.wait_ge(ssem, up_to(n, 2, 1))
                    pool.tensor_tensor(out, tmp, nhalf[:, :], ALU.pow).then_inc(ssem, 1)

                def dense(st, j):
                    q = st.parity
                    if j == C_WO:
                        _, mv, vare, rstd = norms["2"]
                        wait_apart(pool, s, s["moments2"], up_to(st.nc, 2, 2))
                        inverse_root(s["rstd2"], mv[:, :, 1], vare, rstd, st.nc, 1.0)
                    elif j in MIXES:
                        turn = MIXES[j][1]
                        pool.wait_ge(s["shift_mixed"], up_to(st.na, 20, 4 * turn + 4))
                        m = cm((m0, m1)[turn % 2])
                        pool.tensor_tensor(m, m, ext[:, :, 1:T + 1], ALU.add).then_inc(s["mixed"], 1)
                    elif j == A_PV:
                        pool.wait_ge(s["v_high"], up_to(st.na, 1, 1))
                        pool.tensor_tensor(vlo[1 - q][:, :, :], cm(m1), vhi[1 - q][:, :, :].bitcast(F32),
                                           ALU.subtract).then_inc(s["v_low"], 1)

                def scale_heads(st):
                    pool.wait_ge(s["hrs"], up_to(st.nc, ROOT_STEPS, ROOT_STEPS))
                    v = c1[:, :].rearrange("p (h j) -> p h j", j=S)
                    pool.tensor_tensor(v, v, hrs.unsqueeze(2).broadcast_to([P, TT * NC * HT, S]),
                                       ALU.mult).then_inc(s["gn_scaled"], 1)

                def wkv(st, g):
                    if g in ON_POOL:
                        c = g // 4
                        pool.wait_ge(s["scanned"], up_to(st.nb, NG, g + 1))
                        pool.tensor_tensor(state[g % 2][:, :, :], state[g % 2][:, :, :],
                                           rT[st.parity][:, c:c + 1, :].broadcast_to([P, 4, T]),
                                           ALU.mult).then_inc(s["rs_pool"], 1)

                def body(st):
                    for g in range(NG):
                        if st.wkv:
                            wkv(st, g)
                        if st.first and C_FK in SLOTS[g]:
                            _, mv, vare, rstd = norms["1"]
                            wait_apart(pool, s, s["moments1"], up_to(st.nf, 2, 2))
                            inverse_root(s["rstd1"], mv[:, :, 1], vare, rstd, st.nf, 1.0)
                        for j in SLOTS[g]:
                            if in_step(st.first_t, j):
                                dense(st, j)
                        if st.behind and g == 1:
                            scale_heads(st)
                    if st.wkv:
                        pool.wait_ge(s["rs_pool"], up_to(st.nb, len(ON_POOL), len(ON_POOL)))
                    if st.ahead:
                        pool.wait_ge(s["v_low"], up_to(st.na, 1, 1))
                        pool.wait_ge(s["mixed"], up_to(st.na, 5, 5))
                    if st.behind:
                        pool.wait_ge(s["rstd2"], up_to(st.nc, 2, 2))
                    if st.first:
                        pool.wait_ge(s["rstd1"], up_to(st.nf, 2, 2))
                    step_end(pool, st)

                pipeline(pool, layer, body)

            @block.vector
            def _(dve):
                dve.wait_ge(s["weights"], up_to(layer, 16 * 2, 16 * 2))

                def moments(x, n, which):
                    stats, mv, _, rstd = norms[which]
                    for tt in range(TT):
                        dve.bn_stats(stats[:, tt, :], x[:, tt, :]).then_inc(s["stats" + which], 1)
                    for tt in range(TT):
                        wait_apart(dve, s, s["stats" + which], up_to(n, 2, tt + 1))
                        dve.bn_aggr(mv[:, tt, :], stats[:, tt, :]).then_inc(s["moments" + which], 1)

                def normalise(x, out, n, which):
                    stats, mv, _, rstd = norms[which]
                    dve.wait_ge(s["moments" + which], up_to(n, 2, 2))
                    dve.wait_ge(s["rstd" + which], up_to(n, 2, 2))
                    for tt in range(TT):
                        dve.tensor_scalar(out[:, tt, :], x[:, tt, :], mv[:, tt, 0:1], rstd[:, tt:tt + 1],
                                          ALU.subtract, ALU.mult).then_inc(s["normed" + which], 1)

                def inverse_root(sem, n, x, half, y):
                    done = [0]

                    def then(m):
                        m.then_inc(sem, 1)
                        done[0] += 1
                        dve.wait_ge(sem, up_to(n, ROOT_STEPS, done[0]))

                    then(dve.tensor_scalar(half.bitcast(I32), x.bitcast(I32), 1, None, ALU.logical_shift_right))
                    then(dve.tensor_scalar(y.bitcast(I32), half.bitcast(I32), -1, 0x5F3759DF, ALU.mult, ALU.add))
                    for _ in range(NEWTON):
                        then(dve.scalar_tensor_tensor(out=half, in0=y, scalar=-0.5, in1=y, op0=ALU.mult, op1=ALU.mult))
                        then(dve.tensor_tensor(half, half, x, ALU.mult))
                        then(dve.scalar_tensor_tensor(out=y, in0=half, scalar=1.5, in1=y, op0=ALU.add, op1=ALU.mult))

                def shift(src, out, sem):
                    dve.tensor_tensor(cm(out), src[:, :, 0:T], src[:, :, 1:T + 1], ALU.subtract).then_inc(sem, 1)

                def mix(out, shifted, src, coef_row, sem):
                    for c in range(NC):
                        dve.scalar_tensor_tensor(out=cm(out)[:, c, :], in0=cm(shifted)[:, c, :],
                                                 scalar=par[:, coef_row, c:c + 1], in1=src[:, c, 1:T + 1],
                                                 op0=ALU.mult, op1=ALU.add).then_inc(sem, 1)

                def dense(st, j):
                    dt_, dc = job_of(st, j)
                    q = st.parity

                    def made():
                        dve.wait_ge(s["dense"], st.job(j))

                    def read(j):
                        dve.wait_ge(s[f"free{j % 2}"], st.read(j))

                    fr = s[f"free{j % 2}"]
                    if j == C_OT:
                        made()
                        for tt in range(TT):
                            m = dve.tensor_tensor(
                                tm(c0)[:, tt, :].rearrange("p (c h j) -> p c h j", c=NC, h=HT),
                                dt_[:, tt, :].rearrange("p (c j h) -> p c h j", c=NC, h=HT),
                                uv[1 - q][:, tt, :].rearrange("p (c h j) -> p c h j", c=NC, h=HT), ALU.add)
                        m.then_inc(fr, 1)
                        read(j)
                        o = c0[:, :].rearrange("p (h j) -> p h j", j=S)
                        dve.tensor_reduce(hsum, o, AX, ALU.add).then_inc(s["hsum"], 1)
                        dve.wait_ge(s["hsum"], up_to(st.nc, 1, 1))
                        dve.scalar_tensor_tensor(out=c1[:, :].rearrange("p (h j) -> p h j", j=S),
                                                 in0=hsum.unsqueeze(2).broadcast_to([P, TT * NC * HT, S]),
                                                 scalar=-1.0 / S, in1=o, op0=ALU.mult, op1=ALU.add)\
                           .then_inc(s["centred"], 1)
                    elif j == C_GNT:
                        read(j)
                        dve.scalar_tensor_tensor(out=cm(c0), in0=cm(c0), scalar=0.5, in1=gT[1 - q][:, :, :],
                                                 op0=ALU.mult, op1=ALU.mult).then_inc(s["gated"], 1)
                    elif j == C_WO:
                        made()
                        dve.wait_ge(s["x_residual"], up_to(st.nc, 16, 16))
                        dve.tensor_tensor(tm(xr), tm(xr), dt_[:, :, :], ALU.add).then_inc(fr, 1)
                        read(j)
                        moments(tm(xr), st.nc, "2")
                        normalise(tm(xr), tm(c1), st.nc, "2")
                    elif j == C_XT:
                        read(j)
                        shift(ext2, c0, s["shifted2"])
                        dve.wait_ge(s["shifted2"], up_to(st.nc, 1, 1))
                        mix(c1, c0, ext2, FMR, s["mix2"])
                    elif j == C_FR:
                        made()
                        mix(c1, c0, ext2, FMK, s["mix2"])
                    elif j == C_FV:
                        made()
                        read(C_FR)
                        dve.scalar_tensor_tensor(out=tm(c0), in0=tm(c0), scalar=1.0, in1=dt_[:, :, :],
                                                 op0=ALU.add, op1=ALU.mult).then_inc(fr, 1)
                        read(j)
                        dve.scalar_tensor_tensor(out=xr[:, :], in0=c0[:, :], scalar=0.5, in1=xr[:, :],
                                                 op0=ALU.mult, op1=ALU.add).then_inc(s["x_new"], 1)
                    elif j == F_XT:
                        read(j)
                        shift(ext, sx, s["shifted1"])
                        dve.wait_ge(s["shifted1"], up_to(st.nf, 1, 1))
                        mix(m0, sx, ext, MAAX, s["mix0"])
                    elif j in MIXES:
                        f, turn, last = MIXES[j]
                        made()
                        if turn >= 2:
                            dve.wait_ge(s["dense"], st.job(last))
                        for c in range(NC):
                            m = dve.scalar_tensor_tensor(out=cm((m0, m1)[turn % 2])[:, c, :], in0=dc[:, c, :],
                                                         scalar=par[:, MAAK + f, c:c + 1], in1=cm(sx)[:, c, :],
                                                         op0=ALU.add, op1=ALU.mult).then_inc(s["shift_mixed"], 1)
                        dve.wait_ge(s["shift_mixed"], up_to(st.na, 20, 4 * turn + 4))
                        dve.nop().then_inc(fr, 1)
                    elif j == A_PG:
                        dve.wait_ge(s["g_tanh"], up_to(st.na, 1, 1))
                        dve.scalar_tensor_tensor(out=gT[1 - q][:, :, :], in0=cm(a0), scalar=1.0, in1=dc,
                                                 op0=ALU.add, op1=ALU.mult).then_inc(fr, 1)
                        read(j)
                        read(A_PR)
                        read(A_PK)
                        for c in range(NC):
                            dve.scalar_tensor_tensor(out=cm(a0)[:, c, :], in0=rT[1 - q][:, c, :],
                                                     scalar=par[:, BONUS, c:c + 1], in1=kT[1 - q][:, c, :],
                                                     op0=ALU.mult, op1=ALU.mult).then_inc(s["ruk"], 1)
                    elif j == A_CF:
                        made()
                        dve.tensor_copy(coef, dt_[:, 0, 0:TT * NC * HT]).then_inc(fr, 1)
                    elif j == A_VT:
                        made()
                        read(A_CF)
                        dve.tensor_tensor(uv[1 - q][:, :, :].rearrange("p s (h j) -> p (s h) j", j=S),
                                          dt_[:, :, :].rearrange("p s (h j) -> p (s h) j", j=S),
                                          coef.unsqueeze(2).broadcast_to([P, TT * NC * HT, S]), ALU.mult).then_inc(fr, 1)

                def wkv(st, g):
                    c = g // 4
                    k_ = kT[st.parity][:, c:c + 1, 0:T - 1].broadcast_to([P, 2, T - 1])
                    if g >= 1:
                        dve.wait_ge(s["scanned"], up_to(st.nb, NG, g))
                    for half in range(2):
                        dve.wait_ge(s["spread"], up_to(st.nb, 2 * NG, 2 * g + half + 1))
                        dve.tensor_tensor(drive[:, 2 * half:2 * half + 2, 1:T],
                                          V[half][:, :].rearrange("p (i t) -> p i t", i=2)[:, :, 0:T - 1], k_,
                                          ALU.mult).then_inc(s["kv"], 1)
                    dve.wait_ge(s["kv"], up_to(st.nb, 2 * NG, 2 * g + 2))
                    dve.wait_ge(s["s0_in"], up_to(st.nb, NG, g + 1))
                    dve.wait_ge(s["wrep"], up_to(st.nb, NC, c + 1))
                    if g >= 2:
                        dve.wait_ge(s["reduced"], up_to(st.nb, NG, g - 1))
                    dve.tensor_tensor_scan(state[g % 2][:, :, :].rearrange("p j t -> p (j t)"),
                                           wrep[:, :, :].rearrange("p j t -> p (j t)"),
                                           drive[:, :, :].rearrange("p j t -> p (j t)"),
                                           0.0, ALU.mult, ALU.add).then_inc(s["scanned"], 1)
                    if g not in ON_POOL:
                        dve.wait_ge(s["scanned"], up_to(st.nb, NG, g + 1))
                        dve.tensor_tensor(state[g % 2][:, :, :], state[g % 2][:, :, :],
                                          rT[st.parity][:, c:c + 1, :].broadcast_to([P, 4, T]),
                                          ALU.mult).then_inc(s["rs"], 1)

                def body(st):
                    for g in range(NG):
                        if st.wkv:
                            wkv(st, g)
                        if st.behind and g == 1:
                            dve.wait_ge(s["squared"], up_to(st.nc, 1, 1))
                            dve.tensor_reduce(hvar, oP[:, :, :].rearrange("p c (h j) -> p (c h) j", j=S), AX, ALU.add)\
                               .then_inc(s["hvar"], 1)
                            dve.wait_ge(s["hvar"], up_to(st.nc, 1, 1))
                            dve.tensor_scalar(hve, hvar, 1.0 / S, EPS, ALU.mult, ALU.add).then_inc(s["hve"], 1)
                            dve.wait_ge(s["hve"], up_to(st.nc, 1, 1))
                            inverse_root(s["hrs"], st.nc, hve, hvar, hrs)
                        if st.first and C_FK in SLOTS[g]:
                            dve.wait_ge(s["x_loaded"], up_to(st.nf, 16, 16))
                            moments(tm(a0), st.nf, "1")
                        for j in SLOTS[g]:
                            if in_step(st.first_t, j):
                                dense(st, j)
                        if st.first and F_XT in SLOTS[(g + 1) % NG]:
                            if st.ahead:
                                dve.wait_ge(s["dense"], st.job(A_PV))
                            normalise(tm(a0), tm(m0), st.nf, "1")
                    if st.wkv:
                        dve.wait_ge(s["rs"], rs_value(st, NG - 1))
                    if st.ahead:
                        dve.wait_ge(s[f"free{A_VT % 2}"], st.read(A_VT))
                    if st.first:
                        dve.wait_ge(s["mix0"], up_to(st.nf, 4, 4))
                    if st.behind:
                        dve.wait_ge(s["x_new"], up_to(st.nc, 1, 1))
                    step_end(dve, st)

                pipeline(dve, layer, body)


def rs_value(st, g):
    if g in ON_POOL:
        return up_to(st.nb, len(ON_POOL), ON_POOL.index(g) + 1)
    mine = [i for i in range(NG) if i not in ON_POOL]
    return up_to(st.nb, len(mine), mine.index(g) + 1)


NH = 16
DH = 32
KEYS = 2 * T
KT = KEYS // P
F = 2048
NF = F // P
RMS_EPS = 1e-6
MASKED = -3e38
QB, KB, VB, PW, B1 = 0, NC, 2 * NC, 3 * NC, 4 * NC
L_Q, L_KX, L_VX, L_P = 0, 1, 2, 3
L_CT, L_RT, L_KC, L_RB, L_KC2, L_OUT, L_VC, L_VC2, L_NT, L_XT = range(L_P + NH, L_P + NH + 10)
L_H = L_XT + 1
L_M2 = L_H + 4
NJ_L = L_M2 + 1
L_NEXT = (L_CT, L_KC, L_KC2, L_VC, L_VC2, L_XT)


def in_latent(n, j):
    if not isinstance(n, int):
        return True
    return n + 1 < B if j in L_NEXT else n >= 0


def latent_jobs(n, j, buffers):
    before = sum(i % 2 in buffers for i in L_NEXT) if not isinstance(n, int) or n >= 0 else 0
    per = NJ_L // 2 * len(buffers)
    own = sum(in_latent(n, i) for i in range(j) if i % 2 in buffers)
    return (n * per if not isinstance(n, int) or n >= 0 else 0) + (before + own)


def latent_layer(nc, k, s, w, ctx_dram, mask, x_src, x_dst):
    ident, nhalf = k["ident"], k["nhalf"]
    with ExitStack() as ctx:
        def sb(name, shape, dt=F32):
            return ctx.enter_context(nc.sbuf_tensor("l_" + name, shape, dt))

        wq, wk, wv, wo = (sb(n, [P, NC, E]) for n in ("wq", "wk", "wv", "wo"))
        w1 = sb("w1", [P, NC, F])
        w2 = sb("w2", [P, NF, E])
        par = sb("par", [P, 4 * NC + NF])
        out_b = sb("out_b", [P, E])
        b2 = sb("b2", [P, E])
        expand = sb("expand", [NH, E])
        ctok = sb("ctok", [P, TT, E])
        xtok = sb("xtok", [P, TT, E])
        xnew = sb("xnew", [P, TT, E])
        maskb = sb("maskb", [P, KEYS])
        maski = maskb[:, 0:T].bitcast(I32)
        hT = sb("hT", [P, NC, KEYS])
        qz = sb("qz", [P, NC, 4, T])
        kT = sb("kT", [P, NC, KEYS])
        v = sb("v", [P, KT, E])
        probs = [[sb(f"probs{i}{j}", [P, KEYS]) for j in range(TT)] for i in range(2)]
        ring = sb("ring", [P, 8, KT, T])
        small = sb("small", [P, 80])
        top = small[:, 0:2 * TT]
        neg = small[:, 4:4 + 2 * TT]
        squares, meane, rstd = (small[:, o:o + TT] for o in (8, 10, 12))
        total = small[:, 16:16 + TT * NH]
        inv = small[:, 48:48 + TT * NH]
        invT = probs[0][0][0:NH, 0:T]
        D, V, O = k["D"], k["V"], k["O"]
        dcm = [d[:, :, :].rearrange("p b (c t) -> p (b c) t", t=T) for d in D]
        hidden = ring[:, 0:4, :, :].rearrange("p a c t -> p (a c) t")
        cT, xT = hT[:, :, 0:T], hT[:, :, T:KEYS]
        aT = xT
        attended = ring[:, 4, :, :].rearrange("p c t -> p (c t)").rearrange("p (s e) -> p s e", s=TT)
        xb = scratch = ring[:, 5, :, :].rearrange("p c t -> p (c t)").rearrange("p (s e) -> p s e", s=TT)
        xn = ring[:, 6, :, :].rearrange("p c t -> p (c t)").rearrange("p (s e) -> p s e", s=TT)
        xnT = ring[:, 7, :, :]
        cs = ctx_dram.rearrange("b (s p) e -> b p s e", p=P)
        xs = x_src.rearrange("b (s p) e -> b p s e", p=P)
        xd = x_dst.rearrange("b (s p) e -> b p s e", p=P)

        def made_value(n, j):
            return latent_jobs(n, j, (0, 1)) + 1

        def fills_before(n, j):
            return latent_jobs(n, j, (j % 2,))

        def batches(eng, body):
            body(-1)
            with eng.Fori(0, B - 1) as n:
                body(n)
            body(B - 1)

        def batch_end(eng, n):
            eng.nop().then_inc(s["l_batch_done"], 1)
            wait_apart(eng, s, s["l_batch_done"], up_to(n, 5, 5))

        with nc.Block() as block:

            @block.sync
            def _(sp):
                for dst, name in ((wk, "wk"), (wv, "wv"), (wq, "wq")):
                    sp.dma_start(dst[:, :, :], w[name].rearrange("(c p) n -> p c n", p=P)).then_inc(s["l_weights"], 16)
                sp.dma_start(par[:, :], w["par"]).then_inc(s["l_weights"], 16)
                sp.dma_start(out_b[:, :], w["out_b"].partition_broadcast(P)).then_inc(s["l_weights"], 16)
                sp.dma_start(b2[:, :], w["b2"].partition_broadcast(P)).then_inc(s["l_weights"], 16)
                sp.dma_start(ctok[:, :, :], cs[0]).then_inc(s["l_ctx"], 16)
                sp.dma_start(xtok[:, :, :], xs[0]).then_inc(s["l_x"], 16)
                sp.dma_start(maski, mask[0].partition_broadcast(P)).then_inc(s["l_mask"], 16)
                sp.dma_start(wo[:, :, :], w["wo"].rearrange("(c p) n -> p c n", p=P)).then_inc(s["l_late_weights"], 16)
                sp.dma_start(expand[:, :], w["expand"]).then_inc(s["l_late_weights"], 16)
                for dst, name in ((w1, "w1"), (w2, "w2")):
                    sp.dma_start(dst[:, :, :], w[name].rearrange("(c p) n -> p c n", p=P)).then_inc(s["l_late_weights"], 16)

                def batch(n):
                    if in_latent(n, L_CT):
                        wait_apart(sp, s, s["l_dense"], latent_jobs(n, L_Q, (0, 1)))
                        wait_apart(sp, s, s["l_ctx"], up_to(n, 16, 16))
                        sp.dma_start(ctok[:, :, :], cs[n + 1]).then_inc(s["l_ctx"], 16)
                        wait_apart(sp, s, s["l_masked"], up_to(n, TT * NH, TT * NH))
                        wait_apart(sp, s, s["l_mask"], up_to(n, 16, 16))
                        sp.dma_start(maski, mask[n + 1].partition_broadcast(P)).then_inc(s["l_mask"], 16)
                        wait_apart(sp, s, s["l_biased"], up_to(n, 1, 1))
                        wait_apart(sp, s, s["l_x"], up_to(n, 16, 16))
                        sp.dma_start(xtok[:, :, :], xs[n + 1]).then_inc(s["l_x"], 16)
                    batch_end(sp, n)
                    wait_apart(sp, s, s["l_new"], up_to(n, 1, 1))
                    sp.dma_start(xd[n], xnew[:, :, :]).then_inc(s["l_stored"], 16)

                with sp.Fori(0, B - 1) as n:
                    batch(n)
                batch(B - 1)
                sp.wait_ge(s["l_stored"], up_to(B - 1, 16, 16))

            @block.tensor
            def _(pe):
                pe.wait_ge(s["l_weights"], 16 * 6)
                pe.wait_ge(s["l_zeros"], 2)

                def batch(n):
                    def free(j):
                        wait(pe, s[f"l_free{j % 2}"], fills_before(n, j))
                        return D[j % 2], dcm[j % 2]

                    def evacuated(j):
                        pe.wait_ge(s[f"l_free{j % 2}"], fills_before(n, j) + 1)

                    def done(m):
                        m.then_inc(s["l_dense"], 1)

                    def transposes_cm(dst, src):
                        for c in range(NC):
                            for tt in range(TT):
                                m = pe.transpose(dst[:, c, tt * P:(tt + 1) * P], src[:, tt, c * P:(c + 1) * P],
                                                 ident[:, :])
                        return m

                    def product_cm(dst, wt, x, tiles):
                        for i, o in enumerate(tiles):
                            for c in range(NC):
                                m = pe.matmul(dst[:, i, :], wt[:, c, o * P:(o + 1) * P], x[:, c, :],
                                              start=(c == 0), stop=(c == NC - 1))
                        return m

                    def product_tm(dst, wt, x, n_in, tiles=range(TT)):
                        for tt in tiles:
                            for c in range(n_in):
                                m = pe.matmul(dst[:, tt, :], x[:, c, tt * P:(tt + 1) * P], wt[:, c, :],
                                              start=(c == 0), stop=(c == n_in - 1))
                        return m

                    def scores(h):
                        c, hh = h // 4, h % 4
                        if h == 0:
                            evacuated(L_Q)
                            evacuated(L_KX)
                        for tt in range(TT):
                            if h >= 1:
                                pe.wait_ge(s["l_masked"], up_to(n, TT * NH, TT * (h - 1) + tt + 1))
                            pe.matmul(V[tt][:, :], qz[:, c, hh, tt * P:(tt + 1) * P], kT[:, c, :],
                                      start=True, stop=True).then_inc(s["l_scores"], 1)

                    def turn(h):
                        pe.wait_ge(s["l_exp"], up_to(n, TT * NH, TT * (h + 1)))
                        _, dc = free(L_P + h)
                        for kt in range(KT):
                            for tt in range(TT):
                                m = pe.transpose(dc[:, kt, tt * P:(tt + 1) * P],
                                                 probs[h % 2][tt][:, kt * P:(kt + 1) * P], ident[:, :])
                        done(m)

                    def values(c):
                        if c == 0:
                            evacuated(L_VX)
                        evacuated(L_P + 4 * c + 2)
                        evacuated(L_P + 4 * c + 3)
                        if c >= 2:
                            pe.wait_ge(s["l_o_read"], up_to(n, NC, c - 1))
                        for kt in range(KT):
                            for hh in range(4):
                                h = 4 * c + hh
                                m = pe.matmul(O[c % 2][DH * hh:DH * hh + DH, 0:T], v[:, kt, h * DH:(h + 1) * DH],
                                              ring[:, h % 8, kt, :], start=(kt == 0), stop=(kt == KT - 1))
                        m.then_inc(s["l_values"], 1)

                    this, more = in_latent(n, L_Q), in_latent(n, L_CT)
                    if this:
                        _, dc = free(L_Q)
                        done(product_cm(dc, wq, xT, range(NC)))
                        _, dc = free(L_KX)
                        done(product_cm(dc, wk, xT, range(NC)))
                        dt_, _ = free(L_VX)
                        done(product_tm(dt_, wv, xT, NC))
                        for h in range(NH + 2):
                            if h < NH:
                                scores(h)
                            if 1 <= h <= NH:
                                turn(h - 1)
                            if h >= 5 and (h - 5) % 4 == 0:
                                values((h - 5) // 4)
                    if more:
                        pe.wait_ge(s["l_ctx"], up_to(n + 1, 16, 16))
                        _, dc = free(L_CT)
                        done(transposes_cm(dc, ctok))
                    if this:
                        dt_, _ = free(L_RT)
                        pe.wait_ge(s["l_inv"], up_to(n, 1, 1))
                        for tt in range(TT):
                            m = pe.transpose(dt_[0:NH, 0, tt * P:(tt + 1) * P], inv[:, tt * NH:(tt + 1) * NH], ident[:, :])
                        done(m)
                    if more:
                        evacuated(L_CT)
                        _, dc = free(L_KC)
                        done(product_cm(dc, wk, cT, (0, 1)))
                    if this:
                        pe.wait_ge(s["l_late_weights"], 16 * 4)
                        evacuated(L_RT)
                        _, dc = free(L_RB)
                        for c in range(NC):
                            m = pe.matmul(dc[:, c, :], expand[:, c * P:(c + 1) * P], invT, start=True, stop=True)
                        done(m)
                    if more:
                        _, dc = free(L_KC2)
                        done(product_cm(dc, wk, cT, (2, 3)))
                    if this:
                        dt_, _ = free(L_OUT)
                        pe.wait_ge(s["l_attended"], up_to(n, NC, NC))
                        done(product_tm(dt_, wo, aT, NC))
                    if more:
                        for tt, j in enumerate((L_VC, L_VC2)):
                            dt_, _ = free(j)
                            done(product_tm(dt_, wv, cT, NC, (tt,)))
                    if this:
                        _, dc = free(L_NT)
                        pe.wait_ge(s["l_normed"], up_to(n, 2, 2))
                        done(transposes_cm(dc, xn))
                    if more:
                        pe.wait_ge(s["l_x"], up_to(n + 1, 16, 16))
                        _, dc = free(L_XT)
                        done(transposes_cm(dc, xtok))
                    if this:
                        evacuated(L_NT)
                        for part in range(4):
                            _, dc = free(L_H + part)
                            done(product_cm(dc, w1, xnT, range(4 * part, 4 * part + 4)))
                        dt_, _ = free(L_M2)
                        for tt in range(TT):
                            for c in range(NF):
                                if tt == 0 and c % 4 == 0 and c >= NF // 2:
                                    evacuated(L_H + c // 4)
                                m = pe.matmul(dt_[:, tt, :], hidden[:, c, tt * P:(tt + 1) * P], w2[:, c, :],
                                              start=(c == 0), stop=(c == NF - 1))
                        done(m)
                        pe.wait_ge(s["l_dense"], made_value(n, L_M2))
                        batch_end(pe, n)
                    else:
                        evacuated(L_XT)

                batches(pe, batch)

            @block.scalar
            def _(act):
                act.wait_ge(s["l_weights"], 16 * 6)

                def batch(n):
                    def made(j):
                        act.wait_ge(s["l_dense"], made_value(n, j))
                        return D[j % 2], dcm[j % 2]

                    def done(m, j):
                        m.then_inc(s[f"l_free{j % 2}"], 1)

                    def keys(j, src, dst, tiles):
                        for i, o in enumerate(tiles):
                            m = act.activation(dst[:, o, :], src[:, i, :], ACT.Identity, bias=par[:, KB + o:KB + o + 1])
                        done(m, j)

                    def exps(h):
                        act.wait_ge(s["l_neg"], up_to(n, NH, h + 1))
                        for tt in range(TT):
                            p_ = probs[h % 2][tt]
                            act.activation(p_[:, :], p_[:, :], ACT.Exp, bias=neg[:, TT * (h % 2) + tt:TT * (h % 2) + tt + 1],
                                           scale=1.0 / DH, accum_out=total[:, tt * NH + h:tt * NH + h + 1])\
                               .then_inc(s["l_exp"], 1)

                    def evacuate(h):
                        _, dc = made(L_P + h)
                        if h >= 8:
                            act.wait_ge(s["l_values"], up_to(n, NC, h // 4 - 1))
                        done(act.activation(ring[:, h % 8, :, :], dc, ACT.Copy), L_P + h)

                    def read_o(c):
                        act.wait_ge(s["l_values"], up_to(n, NC, c + 1))
                        act.activation(aT[:, c, :], O[c % 2][:, 0:T], ACT.Copy).then_inc(s["l_o_read"], 1)

                    this, more = in_latent(n, L_Q), in_latent(n, L_CT)
                    if this:
                        _, dc = made(L_KX)
                        keys(L_KX, dc, kT[:, :, T:KEYS], range(NC))
                        dt_, _ = made(L_VX)
                        done(act.activation(v[:, TT:KT, :], dt_[:, :, :], ACT.Copy), L_VX)
                        for h in range(NH + 2):
                            if h < NH:
                                exps(h)
                            if 1 <= h <= NH and (h - 1) % 2 == 0:
                                evacuate(h - 1)
                            if h >= 6 and (h - 6) % 4 == 0:
                                read_o((h - 6) // 4)
                        read_o(NC - 1)
                    if more:
                        _, dc = made(L_CT)
                        done(act.activation(cT, dc, ACT.Copy), L_CT)
                    if this:
                        dt_, _ = made(L_RT)
                        done(act.activation(invT, dt_[0:NH, 0, 0:T], ACT.Copy), L_RT)
                    if more:
                        _, dc = made(L_KC)
                        keys(L_KC, dc, kT[:, :, 0:T], (0, 1))
                    if this:
                        act.wait_ge(s["l_scaled"], up_to(n, 1, 1))
                        for c in range(NC):
                            act.activation(aT[:, c, :], aT[:, c, :], ACT.Identity, bias=par[:, VB + c:VB + c + 1])\
                               .then_inc(s["l_attended"], 1)
                    if more:
                        _, dc = made(L_KC2)
                        keys(L_KC2, dc, kT[:, :, 0:T], (2, 3))
                    if this:
                        act.wait_ge(s["l_residual"], up_to(n, 1, 1))
                        for tt in range(TT):
                            act.activation(scratch[:, tt, :], attended[:, tt, :], ACT.Square,
                                           accum_out=squares[:, tt:tt + 1]).then_inc(s["l_squares"], 1)
                    if more:
                        for tt, j in enumerate((L_VC, L_VC2)):
                            dt_, _ = made(j)
                            done(act.activation(v[:, tt, :], dt_[:, tt, :], ACT.Copy), j)
                    if this:
                        _, dc = made(L_NT)
                        for c in range(NC):
                            m = act.activation(xnT[:, c, :], dc[:, c, :], ACT.Copy, scale=par[:, PW + c:PW + c + 1])
                        done(m, L_NT)
                        for part in range(4):
                            _, dc = made(L_H + part)
                            for i in range(4):
                                o = 4 * part + i
                                m = act.activation(hidden[:, o, :], dc[:, i, :], ACT.Gelu_apprx_tanh,
                                                   bias=par[:, B1 + o:B1 + o + 1])
                            done(m, L_H + part)
                        act.wait_ge(s[f"l_free{(L_H + 3) % 2}"], fills_before(n, L_H + 3) + 1)
                        batch_end(act, n)

                batches(act, batch)

            @block.gpsimd
            def _(pool):
                pool.memset(qz[:, :, :, :], 0.0).then_inc(s["l_zeros"], 1)
                pool.memset(maskb[:, T:KEYS], 0.0).then_inc(s["l_zeros"], 1)
                pool.wait_ge(s["l_weights"], 16 * 6)

                def batch(n, first):
                    if not first:
                        wait_apart(pool, s, s["l_stored"], up_to(n - 1, 16, 16))
                    pool.wait_ge(s["l_x"], up_to(n, 16, 16))
                    for tt in range(TT):
                        pool.tensor_tensor(xnew[:, tt, :], xtok[:, tt, :], b2[:, :], ALU.add).then_inc(s["l_xnew"], 1)
                    pool.wait_ge(s["l_values"], up_to(n, NC, NC))
                    for tt in range(TT):
                        pool.tensor_tensor(xb[:, tt, :], xtok[:, tt, :], out_b[:, :], ALU.add).then_inc(s["l_xb"], 1)
                    pool.wait_ge(s["l_xnew"], up_to(n, TT, TT))
                    pool.wait_ge(s["l_xb"], up_to(n, TT, TT))
                    pool.nop().then_inc(s["l_biased"], 1)
                    wait_apart(pool, s, s["l_squares"], up_to(n, 2, 2))
                    pool.tensor_scalar(meane, squares, 1.0 / E, RMS_EPS, ALU.mult, ALU.add).then_inc(s["l_rstd"], 1)
                    pool.wait_ge(s["l_rstd"], up_to(n, 2, 1))
                    pool.tensor_tensor(rstd, meane, nhalf[:, :], ALU.pow).then_inc(s["l_rstd"], 1)
                    pool.wait_ge(s["l_rstd"], up_to(n, 2, 2))
                    batch_end(pool, n)

                batch(0, True)
                with pool.Fori(1, B) as n:
                    batch(n, False)

            @block.vector
            def _(dve):
                dve.wait_ge(s["l_weights"], 16 * 6)
                dve.wait_ge(s["l_zeros"], 2)

                def batch(n):
                    def made(j):
                        dve.wait_ge(s["l_dense"], made_value(n, j))
                        return D[j % 2], dcm[j % 2]

                    def done(m, j):
                        m.then_inc(s[f"l_free{j % 2}"], 1)

                    def mask_and_max(h):
                        if h >= 2:
                            dve.wait_ge(s["l_dense"], made_value(n, L_P + h - 2))
                        for tt in range(TT):
                            wait_apart(dve, s, s["l_scores"], up_to(n, TT * NH, TT * h + tt + 1))
                            dve.tensor_tensor_reduce(probs[h % 2][tt][:, :], V[tt][:, :], maskb[:, :], 1.0, MASKED,
                                                     ALU.add, ALU.max, top[:, TT * (h % 2) + tt:TT * (h % 2) + tt + 1])\
                               .then_inc(s["l_masked"], 1)
                        dve.wait_ge(s["l_masked"], up_to(n, TT * NH, TT * h + TT))
                        at = slice(TT * (h % 2), TT * (h % 2) + TT)
                        dve.tensor_scalar(neg[:, at], top[:, at], -1.0 / DH, None, ALU.mult).then_inc(s["l_neg"], 1)

                    def evacuate(h):
                        _, dc = made(L_P + h)
                        if h >= 8:
                            dve.wait_ge(s["l_values"], up_to(n, NC, h // 4 - 1))
                        done(dve.tensor_copy(ring[:, h % 8, :, :], dc), L_P + h)

                    this, more = in_latent(n, L_Q), in_latent(n, L_CT)
                    if this:
                        dve.wait_ge(s["l_mask"], up_to(n, 16, 16))
                        dve.tensor_scalar(maskb[:, 0:T], maski, 0.0, MASKED, ALU.is_equal, ALU.mult)\
                           .then_inc(s["l_bias"], 1)
                        _, dc = made(L_Q)
                        for hh in range(4):
                            r = slice(DH * hh, DH * hh + DH)
                            m = dve.tensor_tensor(qz[r, :, hh, :], dc[r, :, :],
                                                  par[r, QB:QB + NC].unsqueeze(2).broadcast_to([DH, NC, T]), ALU.add)
                        done(m, L_Q)
                        dve.wait_ge(s["l_bias"], up_to(n, 1, 1))
                        for h in range(NH + 2):
                            if h < NH:
                                mask_and_max(h)
                            if 1 <= h <= NH and (h - 1) % 2 == 1:
                                evacuate(h - 1)
                        dve.wait_ge(s["l_exp"], up_to(n, TT * NH, TT * NH))
                        dve.reciprocal(inv, total).then_inc(s["l_inv"], 1)
                        _, dc = made(L_RB)
                        dve.wait_ge(s["l_o_read"], up_to(n, NC, NC))
                        m = dve.tensor_tensor(aT[:, :, :], aT[:, :, :], dc, ALU.mult)
                        done(m, L_RB)
                        dve.wait_ge(s[f"l_free{L_RB % 2}"], fills_before(n, L_RB) + 1)
                        dve.nop().then_inc(s["l_scaled"], 1)
                        dt_, _ = made(L_OUT)
                        dve.wait_ge(s["l_biased"], up_to(n, 1, 1))
                        done(dve.tensor_tensor(attended, xb[:, :, :], dt_[:, :, :], ALU.add), L_OUT)
                        dve.wait_ge(s[f"l_free{L_OUT % 2}"], fills_before(n, L_OUT) + 1)
                        dve.nop().then_inc(s["l_residual"], 1)
                        dve.wait_ge(s["l_rstd"], up_to(n, 2, 2))
                        for tt in range(TT):
                            dve.tensor_scalar(xn[:, tt, :], attended[:, tt, :], rstd[:, tt:tt + 1], None, ALU.mult)\
                               .then_inc(s["l_normed"], 1)
                    if more:
                        _, dc = made(L_XT)
                        done(dve.tensor_copy(xT, dc), L_XT)
                    if this:
                        dt_, _ = made(L_M2)
                        done(dve.tensor_tensor(xnew[:, :, :], xnew[:, :, :], dt_[:, :, :], ALU.add), L_M2)
                        dve.wait_ge(s[f"l_free{L_M2 % 2}"], fills_before(n, L_M2) + 1)
                        dve.nop().then_inc(s["l_new"], 1)
                        batch_end(dve, n)

                batches(dve, batch)


X_S, X_CT, X_XT, X_PT, X_K, X_O, X_V = range(7)
X_NEXT = (X_CT, X_XT, X_K, X_V)
X_IN_D = ((X_CT, X_K, X_V), (X_XT, X_O))


class CrossBatch:

    def __init__(self, n, u=None):
        self.n, self.parity = (n if u is None else u * 2 + n), n % 2
        self.this, self.more = n >= 0, n + 1 < B or u is not None

    def has(self, j):
        return self.more if j in X_NEXT else self.this

    def before(self, j, kinds, first):
        own = sum(self.has(i) for i in kinds if i < j)
        if not self.this:
            return first + own
        return self.n * len(kinds) + (first + sum(i in X_NEXT for i in kinds) + own)

    def made(self, j):
        return self.before(j, range(7), 4) + 1

    def buffer(self, j):
        return 0 if j in X_IN_D[0] else 1

    def fills_before(self, j):
        return self.before(j, X_IN_D[self.buffer(j)], 2)


def cross_layer(nc, k, s, w, ctx_dram, x_src, out):
    ident = k["ident"]
    scale = float(E) ** -0.5
    with ExitStack() as ctx:
        def sb(name, shape, dt=F32):
            return ctx.enter_context(nc.sbuf_tensor("x_" + name, shape, dt))

        def pair(name, shape):
            return [sb(f"{name}{i}", shape) for i in range(2)]

        wq, wk, wv, wo = (sb(n, [P, NC, E]) for n in ("wq", "wk", "wv", "wo"))
        wkq = sb("wkq", [P, NC, E])
        wvo = sb("wvo", [P, NC, E])
        alpha = sb("alpha", [P, 1])
        ctok, xtok = pair("ctok", [P, TT, E]), pair("xtok", [P, TT, E])
        cT, xT, kT = pair("cT", [P, NC, T]), pair("xT", [P, NC, T]), pair("kT", [P, NC, T])
        v, y = pair("v", [P, TT, E]), pair("y", [P, TT, E])
        probs = sb("probs", [P, TT, T])
        pT = sb("pT", [P, TT, T])
        small = sb("small", [P, 32])
        top, neg, total, inv, gain = (small[:, 4 * i:4 * i + TT] for i in range(5))
        D, S_, PT_ = k["D"], k["V"], k["O"]
        dcm = [d[:, :, :].rearrange("p b (c t) -> p (b c) t", t=T) for d in D]
        cs = ctx_dram.rearrange("b (s p) e -> b p s e", p=P)
        xs = x_src.rearrange("b (s p) e -> b p s e", p=P)
        yd = out.rearrange("b (s p) e -> b p s e", p=P)

        def batch_end(eng, b):
            eng.nop().then_inc(s["x_batch_done"], 1)
            wait_apart(eng, s, s["x_batch_done"], up_to(b.n, 4, 4))

        def batches(eng, body):
            body(CrossBatch(-1))
            body(CrossBatch(0))
            with eng.Fori(0, (B - 2) // 2) as u:
                body(CrossBatch(1, u))
                body(CrossBatch(2, u))
            body(CrossBatch(B - 1))

        with nc.Block() as block:

            @block.sync
            def _(sp):
                for dst, name, sem in ((wk, "wk", "x_weights"), (wq, "wq", "x_weights"),
                                       (wv, "wv", "x_weights_v"), (wo, "wo", "x_weights_v")):
                    sp.dma_start(dst[:, :, :], w[name].rearrange("(c p) n -> p c n", p=P)).then_inc(s[sem], 16)
                sp.dma_start(alpha[:, :], w["alpha"].partition_broadcast(P)).then_inc(s["x_weights_v"], 16)

                def batch(b):
                    if b.this:
                        wait_apart(sp, s, s["x_ctx"], up_to(b.n, 16, 16))
                        wait_apart(sp, s, s["x_x"], up_to(b.n, 16, 16))
                    if b.more:
                        sp.dma_start(ctok[1 - b.parity][:, :, :], cs[b.n + 1]).then_inc(s["x_ctx"], 16)
                        sp.dma_start(xtok[1 - b.parity][:, :, :], xs[b.n + 1]).then_inc(s["x_x"], 16)
                    if b.this:
                        if not isinstance(b.n, int) or b.n >= 1:
                            wait_apart(sp, s, s["x_out"], up_to(b.n, 16, 0))
                        batch_end(sp, b)
                        sp.dma_start(yd[b.n], y[b.parity][:, :, :]).then_inc(s["x_out"], 16)

                batches(sp, batch)
                sp.wait_ge(s["x_out"], up_to(B - 1, 16, 16))

            @block.tensor
            def _(pe):
                for i, (a, b_, sem, n) in enumerate(((wk, wq, "x_weights", 2), (wv, wo, "x_weights_v", 3))):
                    pe.wait_ge(s[sem], 16 * n)
                    for half in range(2):
                        if i:
                            pe.wait_ge(s[f"x_free{half}"], i)
                        for r in range(2):
                            o = 2 * half + r
                            for c in range(NC):
                                m = pe.matmul(D[half][:, r, :], a[:, c, o * P:(o + 1) * P], b_[:, c, :],
                                              start=(c == 0), stop=(c == NC - 1))
                        m.then_inc(s["x_dense"], 1)
                pe.wait_ge(s["x_free0"], 2)
                pe.wait_ge(s["x_free1"], 2)

                def batch(b):
                    def free(j):
                        i = b.buffer(j)
                        pe.wait_ge(s[f"x_free{i}"], b.fills_before(j))
                        return D[i], dcm[i]

                    def evacuated(j):
                        pe.wait_ge(s[f"x_free{b.buffer(j)}"], b.fills_before(j) + 1)

                    def done(m):
                        m.then_inc(s["x_dense"], 1)

                    here, there = b.parity, 1 - b.parity
                    if b.this:
                        for tt in range(TT):
                            for c in range(NC):
                                m = pe.matmul(S_[tt][:, 0:T], xT[here][:, c, tt * P:(tt + 1) * P], kT[here][:, c, :],
                                              start=(c == 0), stop=(c == NC - 1))
                        done(m)
                    if b.more:
                        for j, src, loaded in ((X_CT, ctok[there], "x_ctx"), (X_XT, xtok[there], "x_x")):
                            pe.wait_ge(s[loaded], up_to(b.n, 16, 32))
                            _, dc = free(j)
                            for c in range(NC):
                                for tt in range(TT):
                                    m = pe.transpose(dc[:, c, tt * P:(tt + 1) * P], src[:, tt, c * P:(c + 1) * P],
                                                     ident[:, :])
                            done(m)
                    if b.this:
                        pe.wait_ge(s["x_exp"], up_to(b.n, TT, TT))
                        for kt in range(TT):
                            for tt in range(TT):
                                m = pe.transpose(PT_[kt][:, tt * P:(tt + 1) * P], probs[:, tt, kt * P:(kt + 1) * P],
                                                 ident[:, :])
                        done(m)
                    if b.more:
                        evacuated(X_CT)
                        evacuated(X_XT)
                        _, dc = free(X_K)
                        for o in range(NC):
                            for c in range(NC):
                                m = pe.matmul(dc[:, o, :], wkq[:, c, o * P:(o + 1) * P], cT[there][:, c, :],
                                              start=(c == 0), stop=(c == NC - 1))
                        done(m)
                    if b.this:
                        pe.wait_ge(s["x_pt_read"], up_to(b.n, TT, TT))
                        dt_, _ = free(X_O)
                        for tt in range(TT):
                            for kt in range(TT):
                                m = pe.matmul(dt_[:, tt, :], pT[:, kt, tt * P:(tt + 1) * P], v[here][:, kt, :],
                                              start=(kt == 0), stop=(kt == TT - 1))
                        done(m)
                    if b.more:
                        evacuated(X_K)
                        dt_, _ = free(X_V)
                        for tt in range(TT):
                            for c in range(NC):
                                m = pe.matmul(dt_[:, tt, :], cT[there][:, c, tt * P:(tt + 1) * P], wvo[:, c, :],
                                              start=(c == 0), stop=(c == NC - 1))
                        done(m)
                        evacuated(X_V)
                    if b.this:
                        batch_end(pe, b)

                batches(pe, batch)

            @block.scalar
            def _(act):
                for i, dst in enumerate((wkq, wvo)):
                    for half in range(2):
                        act.wait_ge(s["x_dense"], 2 * i + half + 1)
                        act.activation(dst[:, 2 * half:2 * half + 2, :], D[half][:, :, :], ACT.Copy)\
                           .then_inc(s[f"x_free{half}"], 1)

                def batch(b):
                    def copy(j, dst):
                        i = b.buffer(j)
                        act.wait_ge(s["x_dense"], b.made(j))
                        act.activation(dst[:, :, :], dcm[i], ACT.Copy).then_inc(s[f"x_free{i}"], 1)

                    if b.this:
                        act.wait_ge(s["x_neg"], up_to(b.n, 1, 1))
                        for tt in range(TT):
                            act.activation(probs[:, tt, :], S_[tt][:, 0:T], ACT.Exp, bias=neg[:, tt:tt + 1],
                                           scale=scale, accum_out=total[:, tt:tt + 1]).then_inc(s["x_exp"], 1)
                    if b.more:
                        copy(X_XT, xT[1 - b.parity])
                    if b.this:
                        act.wait_ge(s["x_dense"], b.made(X_PT))
                        for kt in range(TT):
                            act.activation(pT[:, kt, :], PT_[kt][:, 0:T], ACT.Copy).then_inc(s["x_pt_read"], 1)
                    if b.more:
                        copy(X_K, kT[1 - b.parity])
                    if b.this:
                        batch_end(act, b)

                batches(act, batch)

            @block.vector
            def _(dve):
                dve.wait_ge(s["x_weights_v"], 16 * 3)

                def batch(b):
                    def made(j):
                        dve.wait_ge(s["x_dense"], b.made(j))

                    if b.this:
                        made(X_S)
                        for tt in range(TT):
                            dve.tensor_reduce(top[:, tt:tt + 1], S_[tt][:, 0:T], AX, ALU.max).then_inc(s["x_top"], 1)
                        dve.wait_ge(s["x_top"], up_to(b.n, TT, TT))
                        dve.tensor_scalar(neg, top, -scale, None, ALU.mult).then_inc(s["x_neg"], 1)
                    if b.more:
                        made(X_CT)
                        dve.tensor_copy(cT[1 - b.parity][:, :, :], dcm[0]).then_inc(s["x_free0"], 1)
                    if b.this:
                        dve.wait_ge(s["x_exp"], up_to(b.n, TT, TT))
                        dve.reciprocal(inv, total).then_inc(s["x_inv"], 1)
                        dve.wait_ge(s["x_inv"], up_to(b.n, 1, 1))
                        dve.tensor_scalar(gain, inv, alpha[:, 0:1], None, ALU.mult).then_inc(s["x_gain"], 1)
                        dve.wait_ge(s["x_gain"], up_to(b.n, 1, 1))
                        dve.wait_ge(s["x_x"], up_to(b.n, 16, 16))
                        made(X_O)
                        for tt in range(TT):
                            dve.scalar_tensor_tensor(out=y[b.parity][:, tt, :], in0=D[1][:, tt, :],
                                                     scalar=gain[:, tt:tt + 1], in1=xtok[b.parity][:, tt, :],
                                                     op0=ALU.mult, op1=ALU.add).then_inc(s["x_y"], 1)
                        dve.wait_ge(s["x_y"], up_to(b.n, TT, TT))
                        dve.nop().then_inc(s["x_free1"], 1)
                    if b.more:
                        made(X_V)
                        dve.tensor_copy(v[1 - b.parity][:, :, :], D[0][:, :, :]).then_inc(s["x_free0"], 1)
                    if b.this:
                        batch_end(dve, b)

                batches(dve, batch)


RWKV_SEMS = """weights weights_a weights_c zeros step_done dense free0 free1 spread kv s0_in wrep scanned rs rs_pool reduced o_read
x_residual x_new x_stored x_loaded centred squared hsum hvar hve hrs gn_scaled gated stats1 moments1 rstd1 normed1
stats2 moments2 rstd2 normed2 shifted1 shifted2 mix0 mix2 kk tanh1 shift_mixed mixed tanh_d decay v v_high
v_low g_tanh ruk""".split()
LATENT_SEMS = """l_batch_done l_weights l_late_weights l_xb l_xnew l_zeros l_ctx l_x l_mask l_bias l_dense l_free0 l_free1 l_scores l_masked
l_neg l_exp l_values l_o_read l_inv l_scaled l_attended l_residual l_squares l_biased l_rstd l_normed l_new
l_stored""".split()
CROSS_SEMS = """x_batch_done x_weights x_weights_v x_ctx x_x x_dense x_free0 x_free1 x_exp x_pt_read x_top x_neg
x_inv x_gain x_y x_out""".split()


def four_layers(nc, t, out):
    scratch = [nc.dram_tensor(f"x_after_{i}", [B, T, E], F32, kind="Internal").ap() for i in range(3)]
    with ExitStack() as ctx:
        def sb(name, shape, dt=F32):
            return ctx.enter_context(nc.sbuf_tensor(name, shape, dt))

        s = {n: ctx.enter_context(nc.semaphore("s_" + n)) for n in ["constants", "rounded", "parted"] + RWKV_SEMS + LATENT_SEMS + CROSS_SEMS}
        k = dict(
            ident=sb("ident", [P, P]), stT=sb("stT", [P, B, 2, NC]), s0=sb("s0", [P, B, NC, S]),
            selr=sb("selr", [P, S, P], F32R), red=sb("red", [P, 4, 32]), head8=sb("head8", [P, HT]),
            nhalf=sb("nhalf", [P, TT]),
            D=[ctx.enter_context(nc.psum_tensor(f"D{i}", [P, 2, 512], F32)) for i in range(2)],
            V=[ctx.enter_context(nc.psum_tensor(f"V{i}", [P, 512], F32)) for i in range(2)],
            O=[ctx.enter_context(nc.psum_tensor(f"O{i}", [P, 512], F32)) for i in range(2)],
        )
        with nc.sbuf_tensor("sel", [P, S, P], F32) as sel, nc.Block() as block:
            @block.sync
            def _(sp):
                for dst, name in ((k["ident"], "c_ident"), (sel, "c_sel"), (k["red"], "c_red"), (k["head8"], "c_head8"),
                                  (k["stT"], "state_rows"), (k["s0"], "state_heads")):
                    sp.dma_start(dst[tuple([slice(None)] * len(dst.shape))], t[name]).then_inc(s["constants"], 16)
                sp.wait_ge(s["constants"], 16 * 6)

            @block.vector
            def _(dve):
                dve.memset(k["nhalf"][:, :], -0.5).then_inc(s["rounded"], 1)
                dve.wait_ge(s["constants"], 16 * 6)
                dve.tensor_copy(k["selr"][:, :, :], sel[:, :, :]).then_inc(s["rounded"], 1)
                dve.wait_ge(s["rounded"], 2)

        def rw(i):
            return {n: t[f"r{i}_{n}"] for n in ("w1", "w2", "td1", "td2", "Wk", "Wv", "Wr", "Wg", "Wo", "Wfr", "Wfk", "Wfv", "par")}

        rwkv_layer(nc, 0, k, s, rw(0), t["x"], scratch[0])
        latent_layer(nc, k, s, {n: t["l_" + n] for n in ("wq", "wk", "wv", "wo", "w1", "w2", "par", "expand", "out_b", "b2")},
                     t["ctx"], t["mask"], scratch[0], scratch[1])
        rwkv_layer(nc, 1, k, s, rw(1), scratch[1], scratch[2])
        cross_layer(nc, k, s, {n: t["x_" + n] for n in ("wq", "wk", "wv", "wo", "alpha")}, t["ctx"], scratch[2], out)


def laid_out(inputs):
    a = {n: np.asarray(x) for n, x in inputs.items()}
    cols = lambda v: v.reshape(-1, P).T
    head = np.arange(P) // S
    row = np.arange(P) % S
    sel = np.zeros((P, S, P), np.float32)
    for j in range(S):
        sel[:, j, :] = (head[:, None] == head[None, :]) & (row[:, None] == j)
    red = np.zeros((P, 4, 32), np.float32)
    for jg in range(4):
        red[np.arange(P), jg, HT * jg + head] = 1.0
    ctx = a["ctx_2048"]
    t = {
        "x": a["x"], "ctx": ctx, "mask": a["mask_BxS2_ik0"].reshape(B, 1, T),
        "c_ident": np.eye(P, dtype=np.float32), "c_sel": sel, "c_red": red,
        "c_head8": (head[:, None] == np.arange(HT)[None, :]).astype(np.float32),
        "state_rows": ctx[:, 0:2].reshape(B, 2, NC, P).transpose(3, 0, 1, 2),
        "state_heads": ctx[:, 2:2 + S].reshape(B, NC, P, S).transpose(2, 0, 1, 3),
    }
    for i, pre, names in ((0, "L0_xattn_", ("td_w1", "td_w2", "u", "Wfk", "Wfr", "Wfv")),
                          (1, "L2_xattn_", ("decay_w1", "decay_w2", "faaaa", "ffn_Wk", "ffn_Wr", "ffn_Wv"))):
        td1, td2, u, fk, fr, fv = (a[pre + n] for n in names)
        g = lambda n: a[pre + n]
        stack = g("maa_stack").reshape(5, E)
        vectors = [g("ln1_w"), g("ln1_b"), g("maa_x"), *stack, g("time_decay"), u.reshape(E), g("gn_w"), g("gn_b"),
                   g("ln2_w"), g("ln2_b"), g("ffn_maa_k"), g("ffn_maa_r")]
        t |= {f"r{i}_w1": g("maa_w1"), f"r{i}_w2": g("maa_w2").reshape(5 * DM, E), f"r{i}_td1": td1, f"r{i}_td2": td2,
              f"r{i}_Wk": g("Wk").T, f"r{i}_Wv": g("Wv").T, f"r{i}_Wr": g("Wr").T, f"r{i}_Wg": g("Wg").T,
              f"r{i}_Wo": g("Wo").T, f"r{i}_Wfr": fr.T, f"r{i}_Wfk": fk.T, f"r{i}_Wfv": fv.T,
              f"r{i}_par": np.stack([cols(v) for v in vectors], axis=1)}
    g = lambda n: a["L1_xattn_" + n]
    kvw, kvb = g("kv_w").reshape(E, E, 2), g("kv_b").reshape(E, 2)
    t |= {"l_wq": g("q_w"), "l_wk": kvw[:, :, 0], "l_wv": kvw[:, :, 1], "l_wo": g("out_w"), "l_w1": g("mlp_w1"),
          "l_w2": g("mlp_w2"),
          "l_par": np.concatenate([cols(v) for v in (g("q_b"), kvb[:, 0], kvb[:, 1], g("postnorm_w"), g("mlp_b1"))], axis=1),
          "l_expand": (np.arange(NH)[:, None] == np.arange(E)[None, :] // DH).astype(np.float32),
          "l_out_b": g("out_b").reshape(1, E), "l_b2": g("mlp_b2").reshape(1, E)}
    g = lambda n: a["L3_xattn_" + n]
    t |= {"x_wq": g("w_q"), "x_wk": g("w_k"), "x_wv": g("w_v"), "x_wo": g("w_o").T, "x_alpha": g("alpha").reshape(1, 1)}
    return {n: np.ascontiguousarray(x) for n, x in t.items()}


def kernel(**inputs):
    import concourse.bacc as bacc
    from concourse.bass_utils import run_bass_kernel_spmd

    nc = bacc.Bacc("TRN2", target_bir_lowering=False, num_devices=1)
    arrays = {f"in_{n}": x for n, x in laid_out(inputs).items()}
    t = {n[3:]: nc.dram_tensor(n, x.shape, mybir.dt.from_np(x.dtype), kind="ExternalInput").ap()
         for n, x in arrays.items()}
    out = nc.dram_tensor("out", [B, T, E], F32, kind="ExternalOutput").ap()
    four_layers(nc, t, out)
    r = run_bass_kernel_spmd(nc, [arrays], core_ids=[0])
    return r.results[0]["out"]
```
